# Optimizing a Trainium2 kernel written in Bass

```python
import numpy as np
import jax
import jax.numpy as jnp

def _softmax(x, axis=-1):
    return jax.nn.softmax(x, axis=axis)
def _gelu(x):
    return jax.nn.gelu(x, approximate=True)
def _silu(x):
    return jax.nn.silu(x)
def _sigmoid(x):
    return jax.nn.sigmoid(x)
def _layernorm(x, axis=-1, eps=1e-5):
    m = jnp.mean(x, axis=axis, keepdims=True)
    v = jnp.var(x, axis=axis, keepdims=True)
    return (x - m) / jnp.sqrt(v + eps)
def _scatter_add(tgt, idx, src, axis=0):
    return tgt.at[idx].add(src)
def _segment_sum(src, seg, n):
    return jax.ops.segment_sum(src, seg, n)

kernel_name = 'mk_conv_preact_d4_conv_nchw128_530be3'

def setup_inputs(seed: int = 0):
    np.random.seed(seed)
    _w = jnp.asarray
    def _rec_inputs():
        import jax
        import jax.numpy as jnp
        _gk = jax.random.key(seed)
        x = -0.0002928 + 1 * jax.random.normal(jax.random.fold_in(_gk, 1), (8, 128, 64, 64), jnp.float32)
        return x
    x = _rec_inputs()
    def _L0_conv_setup():
        import jax, jax.numpy as jnp
        from jax import lax
        import numpy as np
        EPS = 1e-05

        def ref_points(Hk, Wk):
            ys = jnp.linspace(0.5, Hk - 0.5, Hk) / Hk * 2.0 - 1.0
            xs = jnp.linspace(0.5, Wk - 0.5, Wk) / Wk * 2.0 - 1.0
            yy, xx = jnp.meshgrid(ys, xs, indexing='ij')
            return jnp.stack([yy, xx], axis=-1)

        def grid_sample(img, grid):
            N, C, Hi, Wi = img.shape
            Hg, Wg = (grid.shape[1], grid.shape[2])
            gx = (grid[..., 0] + 1.0) * 0.5 * (Wi - 1)
            gy = (grid[..., 1] + 1.0) * 0.5 * (Hi - 1)
            x0 = jnp.floor(gx)
            y0 = jnp.floor(gy)
            wx1 = gx - x0
            wy1 = gy - y0
            imgf = img.reshape(N, C, Hi * Wi)

            def corner(ix, iy, w):
                valid = (ix >= 0) & (ix < Wi) & (iy >= 0) & (iy < Hi)
                idx = (jnp.clip(iy, 0, Hi - 1).astype(jnp.int32) * Wi + jnp.clip(ix, 0, Wi - 1).astype(jnp.int32)).reshape(N, -1)
                vals = jax.vmap(lambda im, f: im[:, f])(imgf, idx)
                return vals * (w * valid).reshape(N, 1, -1)
            out = corner(x0, y0, (1 - wx1) * (1 - wy1)) + corner(x0 + 1, y0, wx1 * (1 - wy1)) + corner(x0, y0 + 1, (1 - wx1) * wy1) + corner(x0 + 1, y0 + 1, wx1 * wy1)
            return out.reshape(N, C, Hg, Wg)
        key = jax.random.key(seed)
        ks = jax.random.split(key, 8)
        B, C, H, W = (8, 128, 64, 64)
        gc, nH = (64, 4)
        return {'x': jax.random.normal(ks[0], (B, C, H, W), jnp.float32), 'w_dw': jax.random.normal(ks[1], (gc, 1, 5, 5), jnp.float32) * 0.1, 'ln_w': jnp.ones((gc,), jnp.float32), 'w_off': jax.random.normal(ks[2], (3, gc), jnp.float32) * 0.1, 'wq': jax.random.normal(ks[3], (C, C), jnp.float32) * 0.05, 'wk': jax.random.normal(ks[4], (C, C), jnp.float32) * 0.05, 'wv': jax.random.normal(ks[5], (C, C), jnp.float32) * 0.05, 'wo': jax.random.normal(ks[6], (C, C), jnp.float32) * 0.05, 'rpe': jax.random.normal(ks[7], (nH, 2 * H - 1, 2 * W - 1), jnp.float32) * 0.01}
    _L0_conv_all = _L0_conv_setup()
    _L0_conv_in = {k: v for k, v in _L0_conv_all.items() if k in ('w_dw', 'ln_w', 'w_off', 'wq', 'wk', 'wv', 'wo', 'rpe', )}
    del _L0_conv_all

    def _L1_conv_setup():
        import jax, jax.numpy as jnp
        import numpy as np
        from jax import lax
        EPS_NORM = 1e-12
        KS = 3
        K2 = KS * KS
        MIN_CONN, MAX_CONN = (1, 8)
        NUM_GROUPS = 16
        GN_EPS = 1e-05

        def _unfold3x3_reflect(x):
            B, C, H, W = x.shape
            p = jnp.pad(x, ((0, 0), (0, 0), (1, 1), (1, 1)), mode='reflect')
            pats = [p[:, :, dy:dy + H, dx:dx + W] for dy in range(KS) for dx in range(KS)]
            return jnp.stack(pats, axis=2)

        def _df_counts(x):
            B = x.shape[0]
            avg = jnp.mean(x, axis=1, keepdims=True)
            kern = jnp.array([[0.0, -1.0, 0.0], [-1.0, 4.0, -1.0], [0.0, -1.0, 0.0]], dtype=x.dtype).reshape(1, 1, 3, 3)
            df = jnp.abs(lax.conv_general_dilated(avg, kern, window_strides=(1, 1), padding=((1, 1), (1, 1)), dimension_numbers=('NCHW', 'OIHW', 'NCHW')))
            dmin = df.reshape(B, -1).min(axis=1).reshape(B, 1, 1, 1)
            dmax = df.reshape(B, -1).max(axis=1).reshape(B, 1, 1, 1)
            dn = (df - dmin) / (dmax - dmin + 1e-08)
            return MIN_CONN + jnp.round(dn * (MAX_CONN - MIN_CONN))

        def _group_norm(x, w, b):
            B, C, H, W = x.shape
            g = x.reshape(B, NUM_GROUPS, -1)
            mu = g.mean(-1, keepdims=True)
            var = g.var(-1, keepdims=True)
            g = (g - mu) * lax.rsqrt(var + GN_EPS)
            return g.reshape(B, C, H, W) * w[None, :, None, None] + b[None, :, None, None]
        key = jax.random.key(seed)
        ks = jax.random.split(key, 7)
        B, C, H, W = (8, 128, 96, 96)
        return {'x': jax.random.normal(ks[0], (B, C, H, W), jnp.float32), 'gn_weight': jax.random.uniform(ks[1], (C,), jnp.float32, 0.5, 1.5), 'gn_bias': jax.random.normal(ks[2], (C,), jnp.float32) * 0.1, 'w1': jax.random.normal(ks[3], (2 * C, C), jnp.float32) * 0.02, 'b1': jax.random.normal(ks[4], (2 * C,), jnp.float32) * 0.02, 'w2': jax.random.normal(ks[5], (C, 2 * C), jnp.float32) * 0.02, 'b2': jax.random.normal(ks[6], (C,), jnp.float32) * 0.02}
    _L1_conv_all = _L1_conv_setup()
    _L1_conv_in = {k: v for k, v in _L1_conv_all.items() if k in ('gn_weight', 'gn_bias', 'w1', 'b1', 'w2', 'b2', )}
    del _L1_conv_all

    def _L2_conv_setup():
        import jax, jax.numpy as jnp
        import numpy as np
        DIM = 128

        def _dwconv(x, w, b, pad):
            y = jax.lax.conv_general_dilated(x, w, window_strides=(1, 1), padding=pad, dimension_numbers=('NCHW', 'OIHW', 'NCHW'), feature_group_count=x.shape[1])
            return y + b[None, :, None, None]
        key = jax.random.key(seed)
        ks = jax.random.split(key, 13)
        d = DIM
        s = lambda k, shape, fan: jax.random.normal(k, shape, jnp.float32) * (1.0 / np.sqrt(fan))
        return {'x': jax.random.normal(ks[0], (16, d, 128, 128), jnp.float32), 'w0': s(ks[1], (d, 1, 3, 3), 9), 'b0': jnp.zeros((d,), jnp.float32), 'w0_1': s(ks[2], (d, 1, 1, 5), 5), 'b0_1': jnp.zeros((d,), jnp.float32), 'w0_2': s(ks[3], (d, 1, 5, 1), 5), 'b0_2': jnp.zeros((d,), jnp.float32), 'w1_1': s(ks[4], (d, 1, 1, 11), 11), 'b1_1': jnp.zeros((d,), jnp.float32), 'w1_2': s(ks[5], (d, 1, 11, 1), 11), 'b1_2': jnp.zeros((d,), jnp.float32), 'w3': s(ks[6], (d, d, 1, 1), d), 'b3': jnp.zeros((d,), jnp.float32)}
    _L2_conv_all = _L2_conv_setup()
    _L2_conv_in = {k: v for k, v in _L2_conv_all.items() if k in ('w0', 'b0', 'w0_1', 'b0_1', 'w0_2', 'b0_2', 'w1_1', 'b1_1', 'w1_2', 'b1_2', 'w3', 'b3', )}
    del _L2_conv_all

    def _L3_conv_setup():
        import jax, jax.numpy as jnp
        import numpy as np
        B, C, H, W = (16, 128, 72, 200)
        K, PAD = (9, 4)

        def conv1d(x, w):
            return jax.lax.conv_general_dilated(x, w, window_strides=(1,), padding=[(PAD, PAD)], dimension_numbers=('NCH', 'OIH', 'NCH'))

        def sweep_fwd(seq, w):

            def step(carry, row):
                new = row + jax.nn.relu(conv1d(carry, w))
                return (new, new)
            _, out = jax.lax.scan(step, seq[0], seq[1:])
            return jnp.concatenate([seq[:1], out], axis=0)

        def sweep_bwd(seq, w):
            rev = seq[::-1]

            def step(carry, row):
                new = row + jax.nn.relu(conv1d(carry, w))
                return (new, new)
            _, out = jax.lax.scan(step, rev[0], rev[1:-1])
            return jnp.concatenate([seq[:1], out[::-1], seq[-1:]], axis=0)
        key = jax.random.key(seed)
        kx, kd, ku, kr, kl = jax.random.split(key, 5)
        s = 0.03
        return {'x': jax.random.normal(kx, (B, C, H, W), jnp.float32), 'w_d': jax.random.normal(kd, (C, C, 1, K), jnp.float32) * s, 'w_u': jax.random.normal(ku, (C, C, 1, K), jnp.float32) * s, 'w_r': jax.random.normal(kr, (C, C, K, 1), jnp.float32) * s, 'w_l': jax.random.normal(kl, (C, C, K, 1), jnp.float32) * s}
    _L3_conv_all = _L3_conv_setup()
    _L3_conv_in = {k: v for k, v in _L3_conv_all.items() if k in ('w_d', 'w_u', 'w_r', 'w_l', )}
    del _L3_conv_all

    return {
        "x": x,
        "L0_conv_w_dw": _L0_conv_in["w_dw"],
        "L0_conv_ln_w": _L0_conv_in["ln_w"],
        "L0_conv_w_off": _L0_conv_in["w_off"],
        "L0_conv_wq": _L0_conv_in["wq"],
        "L0_conv_wk": _L0_conv_in["wk"],
        "L0_conv_wv": _L0_conv_in["wv"],
        "L0_conv_wo": _L0_conv_in["wo"],
        "L0_conv_rpe": _L0_conv_in["rpe"],
        "L1_conv_gn_weight": _L1_conv_in["gn_weight"],
        "L1_conv_gn_bias": _L1_conv_in["gn_bias"],
        "L1_conv_w1": _L1_conv_in["w1"],
        "L1_conv_b1": _L1_conv_in["b1"],
        "L1_conv_w2": _L1_conv_in["w2"],
        "L1_conv_b2": _L1_conv_in["b2"],
        "L2_conv_w0": _L2_conv_in["w0"],
        "L2_conv_b0": _L2_conv_in["b0"],
        "L2_conv_w0_1": _L2_conv_in["w0_1"],
        "L2_conv_b0_1": _L2_conv_in["b0_1"],
        "L2_conv_w0_2": _L2_conv_in["w0_2"],
        "L2_conv_b0_2": _L2_conv_in["b0_2"],
        "L2_conv_w1_1": _L2_conv_in["w1_1"],
        "L2_conv_b1_1": _L2_conv_in["b1_1"],
        "L2_conv_w1_2": _L2_conv_in["w1_2"],
        "L2_conv_b1_2": _L2_conv_in["b1_2"],
        "L2_conv_w3": _L2_conv_in["w3"],
        "L2_conv_b3": _L2_conv_in["b3"],
        "L3_conv_w_d": _L3_conv_in["w_d"],
        "L3_conv_w_u": _L3_conv_in["w_u"],
        "L3_conv_w_r": _L3_conv_in["w_r"],
        "L3_conv_w_l": _L3_conv_in["w_l"],
    }

def reference(x, L0_conv_w_dw, L0_conv_ln_w, L0_conv_w_off, L0_conv_wq, L0_conv_wk, L0_conv_wv, L0_conv_wo, L0_conv_rpe, L1_conv_gn_weight, L1_conv_gn_bias, L1_conv_w1, L1_conv_b1, L1_conv_w2, L1_conv_b2, L2_conv_w0, L2_conv_b0, L2_conv_w0_1, L2_conv_b0_1, L2_conv_w0_2, L2_conv_b0_2, L2_conv_w1_1, L2_conv_b1_1, L2_conv_w1_2, L2_conv_b1_2, L2_conv_w3, L2_conv_b3, L3_conv_w_d, L3_conv_w_u, L3_conv_w_r, L3_conv_w_l):
    import jax
    import jax.numpy as jnp
    def _L0_conv_ref(x, w_dw, ln_w, w_off, wq, wk, wv, wo, rpe):
        import jax, jax.numpy as jnp
        from jax import lax
        import numpy as np
        EPS = 1e-05

        def ref_points(Hk, Wk):
            ys = jnp.linspace(0.5, Hk - 0.5, Hk) / Hk * 2.0 - 1.0
            xs = jnp.linspace(0.5, Wk - 0.5, Wk) / Wk * 2.0 - 1.0
            yy, xx = jnp.meshgrid(ys, xs, indexing='ij')
            return jnp.stack([yy, xx], axis=-1)

        def grid_sample(img, grid):
            N, C, Hi, Wi = img.shape
            Hg, Wg = (grid.shape[1], grid.shape[2])
            gx = (grid[..., 0] + 1.0) * 0.5 * (Wi - 1)
            gy = (grid[..., 1] + 1.0) * 0.5 * (Hi - 1)
            x0 = jnp.floor(gx)
            y0 = jnp.floor(gy)
            wx1 = gx - x0
            wy1 = gy - y0
            imgf = img.reshape(N, C, Hi * Wi)

            def corner(ix, iy, w):
                valid = (ix >= 0) & (ix < Wi) & (iy >= 0) & (iy < Hi)
                idx = (jnp.clip(iy, 0, Hi - 1).astype(jnp.int32) * Wi + jnp.clip(ix, 0, Wi - 1).astype(jnp.int32)).reshape(N, -1)
                vals = jax.vmap(lambda im, f: im[:, f])(imgf, idx)
                return vals * (w * valid).reshape(N, 1, -1)
            out = corner(x0, y0, (1 - wx1) * (1 - wy1)) + corner(x0 + 1, y0, wx1 * (1 - wy1)) + corner(x0, y0 + 1, (1 - wx1) * wy1) + corner(x0 + 1, y0 + 1, wx1 * wy1)
            return out.reshape(N, C, Hg, Wg)
        B, C, H, W = x.shape
        G, nH = (2, 4)
        gc = C // G
        dh = C // nH
        gh = nH // G
        scale = dh ** (-0.5)
        orf = 1.0
        conv1x1 = lambda t, w: jnp.einsum('oi,bihw->bohw', w, t)
        q = conv1x1(x, wq)
        q_off = q.reshape(B * G, gc, H, W)
        off = lax.conv_general_dilated(q_off, w_dw, (4, 4), ((2, 2), (2, 2)), dimension_numbers=('NCHW', 'OIHW', 'NCHW'), feature_group_count=gc)
        var = jnp.var(off, axis=1, keepdims=True)
        off = off / jnp.sqrt(var + EPS) * ln_w.reshape(1, -1, 1, 1)
        off = jax.nn.gelu(off, approximate=False)
        off = jnp.einsum('oi,bihw->bohw', w_off, off)
        Hk, Wk = (off.shape[2], off.shape[3])
        n = Hk * Wk
        offset = jnp.stack([jnp.tanh(off[:, 0]) * (orf / Hk), jnp.tanh(off[:, 1]) * (orf / Wk)], axis=-1)
        dm = jax.nn.sigmoid(off[:, 2])[:, None]
        pos = offset + ref_points(Hk, Wk)[None]
        xs = grid_sample(x.reshape(B * G, gc, H, W), pos[..., ::-1])
        xs = (xs * dm).reshape(B, C, 1, n)
        k = conv1x1(xs, wk).reshape(B * nH, dh, n)
        v = conv1x1(xs, wv).reshape(B * nH, dh, n)
        qf = q.reshape(B * nH, dh, H * W)
        attn = jnp.einsum('bcm,bcn->bmn', qf, k) * scale
        rpe_b = jnp.broadcast_to(rpe[None], (B, nH, 2 * H - 1, 2 * W - 1)).reshape(B * G, gh, 2 * H - 1, 2 * W - 1)
        qg = ref_points(H, W).reshape(H * W, 2)
        disp = (qg[None, :, None, :] - pos.reshape(B * G, 1, n, 2)) * 0.5
        bias = grid_sample(rpe_b, disp[..., ::-1]).reshape(B * nH, H * W, n)
        attn = jax.nn.softmax(attn + bias, axis=2)
        out = jnp.einsum('bmn,bcn->bcm', attn, v).reshape(B, C, H, W)
        return conv1x1(out, wo)

    def _L1_conv_ref(x, gn_weight, gn_bias, w1, b1, w2, b2):
        import jax, jax.numpy as jnp
        import numpy as np
        from jax import lax
        EPS_NORM = 1e-12
        KS = 3
        K2 = KS * KS
        MIN_CONN, MAX_CONN = (1, 8)
        NUM_GROUPS = 16
        GN_EPS = 1e-05

        def _unfold3x3_reflect(x):
            B, C, H, W = x.shape
            p = jnp.pad(x, ((0, 0), (0, 0), (1, 1), (1, 1)), mode='reflect')
            pats = [p[:, :, dy:dy + H, dx:dx + W] for dy in range(KS) for dx in range(KS)]
            return jnp.stack(pats, axis=2)

        def _df_counts(x):
            B = x.shape[0]
            avg = jnp.mean(x, axis=1, keepdims=True)
            kern = jnp.array([[0.0, -1.0, 0.0], [-1.0, 4.0, -1.0], [0.0, -1.0, 0.0]], dtype=x.dtype).reshape(1, 1, 3, 3)
            df = jnp.abs(lax.conv_general_dilated(avg, kern, window_strides=(1, 1), padding=((1, 1), (1, 1)), dimension_numbers=('NCHW', 'OIHW', 'NCHW')))
            dmin = df.reshape(B, -1).min(axis=1).reshape(B, 1, 1, 1)
            dmax = df.reshape(B, -1).max(axis=1).reshape(B, 1, 1, 1)
            dn = (df - dmin) / (dmax - dmin + 1e-08)
            return MIN_CONN + jnp.round(dn * (MAX_CONN - MIN_CONN))

        def _group_norm(x, w, b):
            B, C, H, W = x.shape
            g = x.reshape(B, NUM_GROUPS, -1)
            mu = g.mean(-1, keepdims=True)
            var = g.var(-1, keepdims=True)
            g = (g - mu) * lax.rsqrt(var + GN_EPS)
            return g.reshape(B, C, H, W) * w[None, :, None, None] + b[None, :, None, None]
        B, C, H, W = x.shape
        P = H * W
        counts = lax.stop_gradient(_df_counts(x))
        kvals = jnp.minimum(counts, K2).astype(jnp.int32).reshape(B, 1, P)
        patches = _unfold3x3_reflect(x).reshape(B, C, K2, P)
        xc = x.reshape(B, C, P)
        cn = xc / jnp.maximum(jnp.linalg.norm(xc, axis=1, keepdims=True), EPS_NORM)
        pn = patches / jnp.maximum(jnp.linalg.norm(patches, axis=1, keepdims=True), EPS_NORM)
        sim = jnp.einsum('bcp,bckp->bkp', cn, pn)
        order = jnp.argsort(-sim, axis=1)
        top_sim = jnp.take_along_axis(sim, order, axis=1)
        mask = jnp.arange(K2)[None, :, None] < kvals
        wts = jnp.exp(top_sim) * mask
        wts = wts / jnp.sum(wts, axis=1, keepdims=True)
        pat_sorted = jnp.take_along_axis(patches, order[:, None, :, :], axis=2)
        out = jnp.einsum('bckp,bkp->bcp', pat_sorted, wts).reshape(B, C, H, W)
        enhanced = out + _group_norm(x, gn_weight, gn_bias)
        h = jax.nn.relu(jnp.einsum('oi,bihw->bohw', w1, enhanced) + b1[None, :, None, None])
        ffn = jnp.einsum('oi,bihw->bohw', w2, h) + b2[None, :, None, None]
        return enhanced + ffn

    def _L2_conv_ref(x, w0, b0, w0_1, b0_1, w0_2, b0_2, w1_1, b1_1, w1_2, b1_2, w3, b3):
        import jax, jax.numpy as jnp
        import numpy as np
        DIM = 128

        def _dwconv(x, w, b, pad):
            y = jax.lax.conv_general_dilated(x, w, window_strides=(1, 1), padding=pad, dimension_numbers=('NCHW', 'OIHW', 'NCHW'), feature_group_count=x.shape[1])
            return y + b[None, :, None, None]
        x_33 = _dwconv(x, w0, b0, ((1, 1), (1, 1)))
        x_15 = _dwconv(_dwconv(x, w0_1, b0_1, ((0, 0), (2, 2))), w0_2, b0_2, ((2, 2), (0, 0)))
        x_111 = _dwconv(_dwconv(x, w1_1, b1_1, ((0, 0), (5, 5))), w1_2, b1_2, ((5, 5), (0, 0)))
        add = x_33 + x_15 + x_111
        mixer = jnp.einsum('nchw,oc->nohw', add, w3[:, :, 0, 0]) + b3[None, :, None, None]
        return mixer * x

    def _L3_conv_ref(x, w_d, w_u, w_r, w_l):
        import jax, jax.numpy as jnp
        import numpy as np
        B, C, H, W = (16, 128, 72, 200)
        K, PAD = (9, 4)

        def conv1d(x, w):
            return jax.lax.conv_general_dilated(x, w, window_strides=(1,), padding=[(PAD, PAD)], dimension_numbers=('NCH', 'OIH', 'NCH'))

        def sweep_fwd(seq, w):

            def step(carry, row):
                new = row + jax.nn.relu(conv1d(carry, w))
                return (new, new)
            _, out = jax.lax.scan(step, seq[0], seq[1:])
            return jnp.concatenate([seq[:1], out], axis=0)

        def sweep_bwd(seq, w):
            rev = seq[::-1]

            def step(carry, row):
                new = row + jax.nn.relu(conv1d(carry, w))
                return (new, new)
            _, out = jax.lax.scan(step, rev[0], rev[1:-1])
            return jnp.concatenate([seq[:1], out[::-1], seq[-1:]], axis=0)
        wd = w_d[:, :, 0, :]
        wu = w_u[:, :, 0, :]
        wr = w_r[:, :, :, 0]
        wl = w_l[:, :, :, 0]
        rows = jnp.transpose(x, (2, 0, 1, 3))
        rows = sweep_fwd(rows, wd)
        rows = sweep_bwd(rows, wu)
        x = jnp.transpose(rows, (1, 2, 0, 3))
        cols = jnp.transpose(x, (3, 0, 1, 2))
        cols = sweep_fwd(cols, wr)
        cols = sweep_bwd(cols, wl)
        return jnp.transpose(cols, (1, 2, 3, 0))

    def _gn(v, G=32, eps=1e-5):
        B_, C_, H_, W_ = v.shape
        g = v.reshape(B_, G, C_ // G, H_, W_)
        m = jnp.mean(g, axis=(2, 3, 4), keepdims=True)
        s = jnp.var(g, axis=(2, 3, 4), keepdims=True)
        return ((g - m) / jnp.sqrt(s + eps)).reshape(v.shape)

    def _ln_c(v, eps=1e-6):
        m = jnp.mean(v, axis=1, keepdims=True)
        s = jnp.var(v, axis=1, keepdims=True)
        return (v - m) / jnp.sqrt(s + eps)

    def _ln_t(v, eps=1e-5):
        m = jnp.mean(v, axis=-1, keepdims=True)
        s = jnp.var(v, axis=-1, keepdims=True)
        return (v - m) / jnp.sqrt(s + eps)

    def _to_tokens(v):
        B_, C_, H_, W_ = v.shape
        return v.reshape(B_, C_, H_ * W_).transpose(0, 2, 1)
    def _from_tokens(t, like):
        B_, C_, H_, W_ = like.shape
        return t.transpose(0, 2, 1).reshape(B_, C_, H_, W_)

    x = x + _L0_conv_ref(_gn(x), L0_conv_w_dw, L0_conv_ln_w, L0_conv_w_off, L0_conv_wq, L0_conv_wk, L0_conv_wv, L0_conv_wo, L0_conv_rpe)
    x = x + _L1_conv_ref(_gn(x), L1_conv_gn_weight, L1_conv_gn_bias, L1_conv_w1, L1_conv_b1, L1_conv_w2, L1_conv_b2)
    x = x + _L2_conv_ref(_gn(x), L2_conv_w0, L2_conv_b0, L2_conv_w0_1, L2_conv_b0_1, L2_conv_w0_2, L2_conv_b0_2, L2_conv_w1_1, L2_conv_b1_1, L2_conv_w1_2, L2_conv_b1_2, L2_conv_w3, L2_conv_b3)
    x = x + _L3_conv_ref(_gn(x), L3_conv_w_d, L3_conv_w_u, L3_conv_w_r, L3_conv_w_l)
    return x


_drawn_inputs = setup_inputs


def setup_inputs(seed=0):
    import zlib

    import numpy as np

    out = dict(_drawn_inputs(seed))
    spreads = {'L0_conv_ln_w': (1.0, 0.6),
     'L2_conv_b0': (0.0, 0.579),
     'L2_conv_b0_1': (0.0, 0.8),
     'L2_conv_b0_2': (0.0, 0.652),
     'L2_conv_b1_1': (0.0, 0.749),
     'L2_conv_b1_2': (0.0, 0.669),
     'L2_conv_b3': (0.0, 0.64)}
    factors = {'L0_conv_w_dw': 8.0,
     'L0_conv_w_off': 8.0,
     'L0_conv_wq': 8.0,
     'L0_conv_wk': 8.0,
     'L0_conv_wv': 8.0,
     'L0_conv_wo': 8.0,
     'L0_conv_rpe': 42.925,
     'L1_conv_gn_bias': 3.673,
     'L1_conv_w1': 4.718,
     'L1_conv_b1': 53.751,
     'L1_conv_w2': 3.989,
     'L1_conv_b2': 43.203}
    for name, (base, spread) in spreads.items():
        noise = np.random.default_rng([zlib.crc32(name.encode()), seed]).standard_normal(out[name].shape)
        drawn = base * np.exp(spread * noise) if base else spread * noise
        out[name] = jnp.asarray(drawn.astype(out[name].dtype))
    for name, factor in factors.items():
        out[name] = (out[name] * factor).astype(out[name].dtype)
    return out
```

```python
import numpy as np
from contextlib import ExitStack
import concourse.bass as bass
from concourse import mybir

FP32 = mybir.dt.float32
ALU = mybir.AluOpType
ACT = mybir.ActivationFunctionType
AX = mybir.AxisListType
B, C, H, W = 8, 128, 64, 64
HW = H * W
GROUP = 4
GN_EPS = 1e-5
CHUNK = 512
CHUNKS = HW // CHUNK
ROWS = CHUNK // W


SEMAPHORES_OF_PART = []


def next_part(nc):
    nc.all_engine_barrier()
    nc.clear_and_free_semaphores(list(SEMAPHORES_OF_PART))
    SEMAPHORES_OF_PART.clear()
    nc.all_engine_barrier()


class Names:

    def __init__(self, nc, ctx, prefix):
        self.nc, self.ctx, self.prefix = nc, ctx, prefix

    def sbuf(self, name, shape, dtype=FP32):
        return self.ctx.enter_context(self.nc.sbuf_tensor(f"{self.prefix}_{name}", shape, dtype))

    def psum(self, name, shape=(C, CHUNK)):
        return self.ctx.enter_context(self.nc.psum_tensor(f"{self.prefix}_{name}", list(shape), FP32))

    def sem(self, name):
        taken = self.nc.alloc_semaphore(f"{self.prefix}_{name}")
        SEMAPHORES_OF_PART.append(taken)
        return taken


def wait(eng, sem, value):
    if not isinstance(value, int) or value > 0:
        eng.wait_ge(sem, value)


def each(eng, count, body):
    body(0)
    if count > 1:
        with eng.Fori(1, count) as i:
            body(i)


class Chain:

    def __init__(self, eng, sem, per_iteration=0):
        self.eng, self.sem, self.per, self.count, self.base = eng, sem, per_iteration, 0, 0

    def start(self, iteration):
        self.base, self.count = iteration * self.per, 0

    def step(self, ins):
        self.count += 1
        ins.then_inc(self.sem, 1)
        return self.count

    def link(self, ins):
        self.step(ins)
        self.eng.wait_ge(self.sem, self.base + self.count)

    def end(self):
        assert self.count == self.per, (self.count, self.per)


class Shared:

    def __init__(self, nc, ctx):
        mem = Names(nc, ctx, "all")
        self.ident = mem.sbuf("ident", [C, C])
        self.group_mean = mem.sbuf("group_mean", [C, C])
        self.stats = mem.sbuf("stats", [C, B, CHUNKS, 6])
        self.moments = mem.sbuf("moments", [C, B, 2])
        self.rstd = mem.sbuf("rstd", [C, B])
        self.shift = mem.sbuf("shift", [C, B])


def masks(nc, sh):
    with ExitStack() as ctx:
        mem = Names(nc, ctx, "masks")
        filled = mem.sem("filled")
        block = ctx.enter_context(nc.Block())

        @block.gpsimd
        def _(pool):
            pool.memset(sh.ident[:, :], 0.0).then_inc(filled, 1)
            pool.memset(sh.group_mean[:, :], 1.0 / GROUP).then_inc(filled, 1)
            pool.wait_ge(filled, 2)
            pool.affine_select(out=sh.ident[:, :], in_=sh.ident[:, :], compare_op=ALU.not_equal, fill=1.0,
                               base=0, pattern=[[-1, C]], channel_multiplier=1)
            pool.affine_select(out=sh.group_mean[:, :], in_=sh.group_mean[:, :], compare_op=ALU.is_ge, fill=0.0,
                               base=0, pattern=[[-GROUP, C // GROUP], [0, GROUP]], channel_multiplier=1).then_inc(filled, 1)
            pool.wait_ge(filled, 3)
            pool.affine_select(out=sh.group_mean[:, :], in_=sh.group_mean[:, :], compare_op=ALU.is_ge, fill=0.0,
                               base=GROUP - 1, pattern=[[GROUP, C // GROUP], [0, GROUP]], channel_multiplier=-1)


def input_stats(nc, sh, x_in):
    with ExitStack() as ctx:
        mem = Names(nc, ctx, "stat")
        xs = mem.sbuf("xs", [C, B, HW])
        loaded = [mem.sem(f"loaded{b}") for b in range(B)]
        block = ctx.enter_context(nc.Block())

        @block.sync
        def _(sp):
            for b in range(B):
                sp.dma_start(xs[:, b, :], x_in[b]).then_inc(loaded[b], 16)

        @block.vector
        def _(dve):
            for b in range(B):
                dve.wait_ge(loaded[b], 16)
                for j in range(CHUNKS):
                    dve.bn_stats(sh.stats[:, b, j, :], xs[:, b, j * CHUNK:(j + 1) * CHUNK])


def group_scales(nc, sh, layer):
    with ExitStack() as ctx:
        mem = Names(nc, ctx, f"gs{layer}")
        sq = mem.sbuf("sq", [C, B])
        gstat = mem.sbuf("gstat", [C, B, 2])
        stat_ps = mem.psum("stat_ps")
        chain_sem = mem.sem("chain")
        moments_ready = mem.sem("moments_ready")
        gstat_ready = mem.sem("gstat_ready")
        var_ready = mem.sem("var_ready")
        std_ready = mem.sem("std_ready")
        block = ctx.enter_context(nc.Block())

        @block.tensor
        def _(pe):
            pe.wait_ge(moments_ready, 1)
            pe.matmul(stat_ps[:, 0:2 * B], sh.group_mean[:, :], sh.moments[:, :, :].rearrange("c b t -> c (b t)"),
                      start=True, stop=True).then_inc(gstat_ready, 1)

        @block.scalar
        def _(act):
            act.wait_ge(var_ready, 1)
            act.activation(sh.rstd[:, :], sq[:, :], ACT.Sqrt).then_inc(std_ready, 1)

        @block.vector
        def _(dve):
            chain = Chain(dve, chain_sem)
            for b in range(B):
                last = dve.bn_aggr(sh.moments[:, b, :], sh.stats[:, b, :, :].rearrange("c j s -> c (j s)"))
            chain.link(last)
            chain.link(dve.tensor_tensor(sq[:, :], sh.moments[:, :, 0], sh.moments[:, :, 0], ALU.mult))
            dve.tensor_tensor(sh.moments[:, :, 1], sh.moments[:, :, 1], sq[:, :], ALU.add).then_inc(moments_ready, 1)
            dve.wait_ge(gstat_ready, 1)
            chain.link(dve.tensor_copy(gstat[:, :, :].rearrange("c b t -> c (b t)"), stat_ps[:, 0:2 * B]))
            chain.link(dve.tensor_tensor(sq[:, :], gstat[:, :, 0], gstat[:, :, 0], ALU.mult))
            chain.link(dve.tensor_tensor(sq[:, :], gstat[:, :, 1], sq[:, :], ALU.subtract))
            dve.tensor_scalar(sq[:, :], sq[:, :], GN_EPS, None, ALU.add).then_inc(var_ready, 1)
            dve.wait_ge(std_ready, 1)
            chain.link(dve.reciprocal(sh.rstd[:, :], sh.rstd[:, :]))
            dve.scalar_tensor_tensor(sh.shift[:, :], gstat[:, :, 0], -1.0, sh.rstd[:, :], op0=ALU.mult, op1=ALU.mult)

KH = KW = 16
KEYS = KH * KW
GROUPS, HEADS = 2, 4
GC, DH = C // GROUPS, C // HEADS
HPG = HEADS // GROUPS
SCALE = float(DH) ** -0.5
RPE = 2 * H - 1
TILE_ROWS, WINDOW = 2, 4
HALF = (H - 1) / 2.0
T_GRID, T_REF, T_ROW, T_NEGCOL, T_ONE, T_MEAN, T_END = np.cumsum([0, W, KH, WINDOW * KH, 1, 1, C]).tolist()


def first_tile(ky):
    return min(H // TILE_ROWS - WINDOW, int(ky * (H - 1) / KH) // TILE_ROWS)


def constant_table():
    t = np.zeros((C, T_END), np.float64)
    p = np.arange(C)
    query = (np.arange(H) + 0.5) / H * 2 - 1
    key = ((np.arange(KH) + 0.5) / KH * 2 - 1) * HALF
    t[:, T_GRID:T_REF] = query[None, :] * HALF + (RPE - 1) / 2.0 - p[:, None]
    t[:, T_REF:T_ROW] = key[None, :]
    rows = np.array([[TILE_ROWS * (first_tile(k) + s) for k in range(KH)] for s in range(WINDOW)]).reshape(-1)
    t[:, T_ROW:T_NEGCOL] = rows[None, :] + (p // W)[:, None] - HALF
    t[:, T_NEGCOL] = HALF - p % W
    t[:, T_ONE] = 1.0
    t[:, T_MEAN:T_END] = (p[:, None] // GC == p[None, :] // GC) / float(GC)
    return t.astype(np.float32)


def layer0(nc, sh, x_in, table_in, w, out):
    OCT = 8
    OCTS = W // OCT
    HAT_SLOTS = 4
    PAIR = C // W
    with ExitStack() as ctx:
        mem = Names(nc, ctx, "l0")
        table = mem.sbuf("table", [C, T_END])
        wqT = mem.sbuf("wqT", [C, C])
        wkT = mem.sbuf("wkT", [C, C])
        wvo = mem.sbuf("wvo", [C, HEADS, C])
        woff = mem.sbuf("woff", [C, 3, C])
        wdw = mem.sbuf("wdw", [C, 25])
        lnw = mem.sbuf("lnw", [C, 1])
        rpe = mem.sbuf("rpe", [C, HEADS, C])
        xraw = mem.sbuf("xraw", [C, 2, HW])
        q = mem.sbuf("q", [C, HW])
        bias = mem.sbuf("bias", [C, KEYS, W])
        hats = mem.sbuf("hats", [C, 2, 2, KW * W])
        xn = hats[:, :, :, :].rearrange("c u a n -> c (u a n)")
        rows_T = mem.sbuf("rows_T", [C, 2, KW, C])
        xT = rows_T[:, :, :, :].rearrange("c u k n -> c (u k) n")
        probs = mem.sbuf("probs", [C, 2, OCT, KEYS])
        S = probs[:, 0, :, :].rearrange("c j n -> c (j n)").rearrange("c (t m) -> c t m", t=WINDOW)
        probsT = mem.sbuf("probsT", [C, 2, 2, HPG, OCT, H])
        hat_slots = [hats[:, 0, :, :], hats[:, 1, :, :],
                     probs[:, 1, :, :].rearrange("c j n -> c (j n)").rearrange("c (a n) -> c a n", a=2),
                     probsT[:, 0, :, :, :, :].rearrange("c t h j i -> c (t h j i)").rearrange("c (a n) -> c a n", a=2)]
        qd = mem.sbuf("qd", [C, 2, OCT, HPG, H])
        dg = mem.sbuf("dg", [C, 2, OCT // 2, C])
        spare = probsT[:, 1, :, :, :, :].rearrange("c t h j i -> c (t h j i)").rearrange("c (k n) -> c k n", n=KEYS)
        off, cen, gel, xs = (spare[:, k, :] for k in range(4))
        gate = spare[:, 4:6, :].rearrange("c k n -> c (k n)")
        hat_x = spare[:, 6:8, :].rearrange("c a n -> c (a n)").rearrange("c (k g x) -> c k g x", g=GROUPS, x=KW)
        place = mem.sbuf("place", [C, GROUPS, 2, KEYS])
        keys = mem.sbuf("keys", [C, KEYS])
        vals = mem.sbuf("vals", [C, 2, HEADS * C])
        shift = mem.sbuf("shift", [C, 2, OCT])
        sums = mem.sbuf("sums", [C, 2, OCT])
        inv = mem.sbuf("inv", [C, 2, OCT])
        bank = [mem.psum(f"bank{k}") for k in range(8)]
        grid = table[:, T_GRID:T_REF]
        ref = table[:, T_REF:T_ROW]
        one = table[:, T_ONE:T_MEAN]

        with ExitStack() as sctx:
            smem = Names(nc, sctx, "l0s")
            raw = xraw[:, 0, 0:4 * C].rearrange("c (k n) -> c k n", k=4)
            wvz = xraw[:, 1, 0:HEADS * C].rearrange("c (k n) -> c k n", k=HEADS)
            woT = xraw[:, 1, 2048:2048 + C]
            offc = smem.sbuf("offc", [C, 3])
            loaded = smem.sem("loaded")
            zeroed = smem.sem("zeroed")
            turned = smem.sem("turned")
            copied = smem.sem("copied")
            product = smem.sem("product")
            block = sctx.enter_context(nc.Block())
            col = lambda ap: ap.rearrange("(o a) -> o a", a=1)

            @block.sync
            def _(sp):
                n = 0
                for k, name in enumerate(("wq", "wk", "wv", "wo")):
                    sp.dma_start(raw[:, k, :], w[name]).then_inc(loaded, 16)
                sp.dma_start(table[:, :], table_in).then_inc(loaded, 16)
                for g in range(GROUPS):
                    rows = slice(GC * g, GC * (g + 1))
                    sp.dma_start(wdw[rows, :], w["w_dw"]).then_inc(loaded, 16)
                    sp.dma_start(lnw[rows, :], col(w["ln_w"])).then_inc(loaded, 16)
                    for k in range(3):
                        sp.dma_start(offc[rows, k:k + 1], col(w["w_off"][k])).then_inc(loaded, 16)
                sp.wait_ge(zeroed, 1)
                sp.dma_start(rpe[0:RPE, :, 0:RPE], w["rpe"].rearrange("h y x -> y h x")).then_inc(loaded, 16)
                sp.wait_ge(loaded, 16 * 16)

            @block.gpsimd
            def _(pool):
                pool.memset(rpe[:, :, :], 0.0).then_inc(zeroed, 1)
                pool.memset(qd[:, :, :, :, :], 0.0).then_inc(zeroed, 1)
                pool.memset(wvz, 0.0).then_inc(zeroed, 1)

            @block.tensor
            def _(pe):
                pe.wait_ge(loaded, 16 * 16)
                for k, m in enumerate((0, 1, 3)):
                    pe.transpose(bank[k][:, 0:C], raw[:, m, :], sh.ident[:, :]).then_inc(turned, 1)
                pe.wait_ge(copied, 1)
                for h in range(HEADS):
                    pe.matmul(bank[3][:, h * C:(h + 1) * C], wvz[:, h, :], woT, start=True, stop=True).then_inc(product, 1)

            @block.vector
            def _(dve):
                dve.wait_ge(zeroed, 3)
                dve.wait_ge(loaded, 16 * 16)
                for h in range(HEADS):
                    rows = slice(DH * h, DH * (h + 1))
                    dve.tensor_copy(wvz[rows, h, :], raw[rows, 2, :])
                dve.tensor_copy(woff[:, :, :], offc[:, :].rearrange("c (k o) -> c k o", o=1).to_broadcast([C, 3, C]))
                dve.tensor_scalar(rpe[:, :, :], rpe[:, :, :], -1.0, None, ALU.mult)
                dve.wait_ge(turned, 3)
                dve.tensor_copy(wqT[:, :], bank[0][:, 0:C])
                dve.tensor_scalar(wkT[:, :], bank[1][:, 0:C], -SCALE, None, ALU.mult)
                dve.tensor_copy(woT, bank[2][:, 0:C]).then_inc(copied, 1)
                dve.wait_ge(product, HEADS)
                dve.tensor_copy(wvo[:, :, :].rearrange("c h o -> c (h o)"), bank[3][:, :])

        waits_met = mem.sem("waits_met")
        x_loaded = [mem.sem(f"x_loaded{s}") for s in range(2)]
        stored = [mem.sem(f"stored{s}") for s in range(2)]
        normed = mem.sem("normed")
        q_in_psum = mem.sem("q_in_psum")
        q_by_dve = mem.sem("q_by_dve")
        q_by_act = mem.sem("q_by_act")
        xT_in_psum = mem.sem("xT_in_psum")
        xT_by_dve = mem.sem("xT_by_dve")
        xT_by_act = mem.sem("xT_by_act")
        conv_chain = mem.sem("conv_chain")
        mean_ready = mem.sem("mean_ready")
        sq_ready = mem.sem("sq_ready")
        var_ready = mem.sem("var_ready")
        std_ready = mem.sem("std_ready")
        scaled = mem.sem("scaled")
        gelu_ready = mem.sem("gelu_ready")
        offs_in_psum = mem.sem("offs_in_psum")
        tanh_done = mem.sem("tanh_done")
        place_ready = mem.sem("place_ready")
        dist_ready = mem.sem("dist_ready")
        abs_prelude = mem.sem("abs_prelude")
        hats_prelude = mem.sem("hats_prelude")
        S_ready = mem.sem("S_ready")
        var_chain = mem.sem("var_chain")
        xs_in_psum = mem.sem("xs_in_psum")
        xs_ready = mem.sem("xs_ready")
        kv_in_psum = mem.sem("kv_in_psum")
        k_ready = mem.sem("k_ready")
        v_ready = mem.sem("v_ready")
        conv_done = mem.sem("conv_done")
        sq_made = mem.sem("sq_made")
        subtracted = mem.sem("subtracted")
        abs_done = mem.sem("abs_done")
        hats_ready = mem.sem("hats_ready")
        s1_done = mem.sem("s1_done")
        t_copied = mem.sem("t_copied")
        s2_half = mem.sem("s2_half")
        s2_done = mem.sem("s2_done")
        b_copied = mem.sem("b_copied")
        qd_ready = mem.sem("qd_ready")
        qd_chain = mem.sem("qd_chain")
        l_in_psum = mem.sem("l_in_psum")
        added = mem.sem("added")
        min_ready = mem.sem("min_ready")
        exp_done = mem.sem("exp_done")
        inv_ready = mem.sem("inv_ready")
        diag_ready = mem.sem("diag_ready")
        pt_in_psum = mem.sem("pt_in_psum")
        pt_by_dve = mem.sem("pt_by_dve")
        pt_by_act = mem.sem("pt_by_act")
        probs_turned = mem.sem("probs_turned")
        av_done = mem.sem("av_done")
        acc_done = mem.sem("acc_done")
        stats_done = mem.sem("stats_done")
        CONV_CHAIN = 25
        block = ctx.enter_context(nc.Block())

        def gated(eng, s, value):
            eng.wait_ge(s, value)
            eng.sem_inc(waits_met, 1)

        def batches(eng, body):
            with eng.Fori(0, B // 2) as i:
                for s in range(2):
                    body(i * 2 + s, s)

        def pipelined(eng, count, slots, ahead, behind):
            ahead(0, 0)
            with eng.Fori(0, count // slots - 1) as kk:
                for u in range(slots):
                    ahead(kk * slots + (u + 1), (u + 1) % slots)
                    behind(kk * slots + u, u)
            for k in range(count - slots, count):
                if k + 1 < count:
                    ahead(k + 1, (k + 1) % slots)
                behind(k, k % slots)

        def octets(eng, step):
            step(0, 0, former=False)
            with eng.Fori(0, OCTS // 2 - 1) as oo:
                for u in range(2):
                    step(oo * 2 + (u + 1), 1 - u)
            step(OCTS - 1, 1, more=False)

        def step_a(b, g, ky):
            return b * (2 * KH) + (ky + g * KH)

        def step_e(b, g, o):
            return b * (2 * OCTS) + (o + g * OCTS)

        @block.sync
        def _(sp):
            def load(b, s):
                sp.dma_start(xraw[:, s, :], x_in[bass.ds(b, 1)].rearrange("b c n -> (b c) n")).then_inc(x_loaded[s], 16)

            def store(b, s):
                gated(sp, stats_done, (b + 1) * CHUNKS)
                sp.dma_start(out[bass.ds(b, 1)].rearrange("b c n -> (b c) n"), xraw[:, s, :]).then_inc(stored[s], 16)
            load(0, 0)
            load(1, 1)
            with sp.Fori(0, B // 2 - 1) as i:
                for s in range(2):
                    store(i * 2 + s, s)
                    gated(sp, stored[s], (i + 1) * 16)
                    load(i * 2 + (s + 2), s)
            for s in range(2):
                store(B - 2 + s, s)
            for s in range(2):
                sp.wait_ge(stored[s], 16 * (B // 2))

        @block.gpsimd
        def _(pool):
            def body(b, s):
                def subtract(g, ky, u):
                    a = step_a(b, g, ky)
                    if u == 2:
                        pool.wait_ge(probs_turned, step_e(b, g, 0) + 2)
                        pool.wait_ge(av_done, step_e(b, g, 0) + 1)
                    gated(pool, s2_done, a + 1)
                    pool.tensor_tensor(hat_slots[u].rearrange("c a (n i) -> c a n i", i=W),
                                       grid.rearrange("c (a n i) -> c a n i", a=1, n=1).to_broadcast([C, 2, KW, W]),
                                       place[:, g, :, bass.ds(ky * KW, KW)].rearrange("c a (n o) -> c a n o", o=1).to_broadcast([C, 2, KW, W]),
                                       ALU.subtract).then_inc(subtracted, 1)

                def spread(g, o, u):
                    e = step_e(b, g, o)
                    pool.wait_ge(l_in_psum, e * 4 + 4)
                    pool.wait_ge(subtracted, step_a(b, g, KH))
                    pool.wait_ge(diag_ready, e * 2 + 2)
                    for h in range(HPG):
                        rows = slice(GC * g + DH * h, GC * g + DH * (h + 1))
                        gated(pool, qd_chain, e * 2 + (h + 1))
                        pool.tensor_copy(qd[rows, u, :, h, :],
                                         q[rows, :].rearrange("c (i j) -> c j i", j=W)[:, bass.ds(o * OCT, OCT), :]).then_inc(qd_chain, 1)
                    pool.wait_ge(qd_chain, e * 2 + 3)
                    pool.sem_inc(qd_ready, 1)

                def diagonal(g, o, u):
                    e = step_e(b, g, o)
                    pool.wait_ge(inv_ready, e + 1)
                    for half in range(2):
                        pool.wait_ge(pt_in_psum, e * 4 + (2 * half + 2))
                        pool.tensor_tensor(dg[:, half, :, :], sh.ident[:, :].rearrange("c (o n) -> c o n", o=1).to_broadcast([C, OCT // 2, C]),
                                           inv[:, u, 4 * half:4 * half + 4].rearrange("c (j o) -> c j o", o=1).to_broadcast([C, OCT // 2, C]),
                                           ALU.mult).then_inc(diag_ready, 1)
                gated(pool, place_ready, (b + 1) * 5)
                for g in range(GROUPS):
                    with pool.Fori(0, KH // HAT_SLOTS) as kk:
                        for u in range(HAT_SLOTS):
                            subtract(g, kk * HAT_SLOTS + u, u)
                    pipelined(pool, OCTS, 2, lambda o, u: spread(g, o, u), lambda o, u: diagonal(g, o, u))
            pool.sem_inc(qd_chain, 1)
            pool.sem_inc(diag_ready, 4)
            batches(pool, body)

        @block.tensor
        def _(pe):
            def body(b, s):
                pe.wait_ge(acc_done, b * (2 * OCTS) + 2)
                for k in range(CHUNKS):
                    pe.wait_ge(normed, b * CHUNKS + (k + 1))
                    pe.matmul(bank[k][:, :], wqT[:, :], xn[:, k * CHUNK:(k + 1) * CHUNK], start=True, stop=True).then_inc(q_in_psum, 1)
                for k in range(CHUNKS):
                    pe.wait_ge(q_by_act if k % 2 else q_by_dve, b * 4 + (k // 2 + 1))
                    for t in range(4):
                        last = pe.transpose(bank[k][:, t * C:(t + 1) * C], xn[:, (4 * k + t) * C:(4 * k + t + 1) * C], sh.ident[:, :])
                    last.then_inc(xT_in_psum, 1)
                mask = table[:, T_MEAN:T_END]
                pe.wait_ge(xT_by_dve, (b + 1) * 4)
                pe.wait_ge(xT_by_act, (b + 1) * 4)
                pe.wait_ge(conv_done, b + 1)
                pe.matmul(bank[0][:, 0:KEYS], mask, off, start=True, stop=True).then_inc(mean_ready, 1)
                pe.wait_ge(sq_made, b + 1)
                pe.matmul(bank[1][:, 0:KEYS], mask, gel, start=True, stop=True).then_inc(sq_ready, 1)
                pe.wait_ge(gelu_ready, b + 1)
                for g in range(GROUPS):
                    for k in range(3):
                        target = bank[2 + g][:, k * KEYS:(k + 1) * KEYS] if k < 2 else bank[4 + 2 * g][:, 0:KEYS]
                        last = pe.matmul(target, woff[GC * g:GC * (g + 1), k, :], gel[GC * g:GC * (g + 1), :], start=True, stop=True)
                last.then_inc(offs_in_psum, 1)
                pe.wait_ge(S_ready, b + 1)
                for ky in range(KH):
                    for t in range(WINDOW):
                        last = pe.matmul(bank[5][:, ky * 32:(ky + 1) * 32], xT[:, first_tile(ky) + t, :], S[:, t, ky * 32:(ky + 1) * 32],
                                         start=(t == 0), stop=(t == WINDOW - 1))
                last.then_inc(xs_in_psum, 1)
                pe.wait_ge(xs_ready, 2 * (b + 1))
                pe.matmul(bank[6][:, 0:KEYS], wkT[:, :], xs, start=True, stop=True).then_inc(kv_in_psum, 1)
                for t in range(2):
                    pe.matmul(bank[7 * t][:, :], xs[:, t * C:(t + 1) * C], wvo[:, :, :].rearrange("c h o -> c (h o)"),
                              start=True, stop=True).then_inc(kv_in_psum, 1)
                pe.wait_ge(v_ready, 2 * (b + 1))

                def rows1(g, ky, u):
                    a = step_a(b, g, ky)
                    pe.wait_ge(hats_ready, a + 1)
                    for r in range(4):
                        h, half = r // 2, r % 2
                        pe.wait_ge(t_copied, a * 4 + (r + 1))
                        pe.matmul(bank[r][:, :], rpe[:, HPG * g + h, :], hat_slots[u][:, 0, half * CHUNK:(half + 1) * CHUNK],
                                  start=True, stop=True).then_inc(s1_done, 1)

                def cols2(g, ky, u):
                    a = step_a(b, g, ky)
                    pe.wait_ge(t_copied, a * 4 + 8)
                    for half in range(2):
                        pe.wait_ge(b_copied, a * 2 + (half + 1))
                        for n in range(8):
                            k = half * 8 + n
                            last = pe.matmul(bank[4 + half][:, n * W:(n + 1) * W], rows_T[:, u % 2, k, :], hat_slots[u][:, 1, k * W:(k + 1) * W],
                                             start=True, stop=True)
                        last.then_inc(s2_half, 1)
                    pe.wait_ge(s2_half, a * 2 + 2)
                    pe.sem_inc(s2_done, 1)

                def logits(g, o, u, half):
                    e = step_e(b, g, o)
                    rows = slice(GC * g, GC * (g + 1))
                    if half == 0:
                        pe.wait_ge(qd_ready, e + 1)
                    for p in (2 * half, 2 * half + 1):
                        pe.wait_ge(added, e * 4 + (p + 1))
                        for j in (2 * p, 2 * p + 1):
                            last = pe.matmul(bank[p % 2][:, (j % 2) * KEYS:(j % 2 + 1) * KEYS], qd[rows, u, j, :, :].rearrange("c h i -> c (h i)"),
                                             keys[rows, :], start=True, stop=True)
                        last.then_inc(l_in_psum, 1)

                def turn(g, o, u, half):
                    e = step_e(b, g, o)
                    pe.wait_ge(diag_ready, e * 2 + (half + 5))
                    for t in range(2):
                        pe.wait_ge(pt_by_act if t else pt_by_dve, e * 2 + (half + 1))
                        for jj in range(4):
                            j = half * 4 + jj
                            last = pe.matmul(bank[2 + t][:, jj * C:(jj + 1) * C], probs[:, u, j, t * C:(t + 1) * C], dg[:, half, jj, :], start=True, stop=True)
                        last.then_inc(pt_in_psum, 1)
                    if half:
                        pe.wait_ge(pt_in_psum, e * 4 + 8)
                        pe.sem_inc(probs_turned, 1)

                def attend(g, o, u):
                    e = step_e(b, g, o)
                    pe.wait_ge(pt_by_dve, e * 2 + 3)
                    pe.wait_ge(pt_by_act, e * 2 + 3)
                    pe.wait_ge(acc_done, e + 1)
                    for h in range(HPG):
                        for t in range(2):
                            last = pe.matmul(bank[4 + u][:, :], vals[:, t, (HPG * g + h) * C:(HPG * g + h + 1) * C],
                                             probsT[:, u, t, h, :, :].rearrange("c j i -> c (j i)"),
                                             start=(h == 0 and t == 0), stop=(h == HPG - 1 and t == 1))
                    last.then_inc(av_done, 1)

                for g in range(GROUPS):
                    pe.wait_ge(acc_done, b * (2 * OCTS) + (g * OCTS + 2))
                    pipelined(pe, KH, HAT_SLOTS, lambda ky, u: rows1(g, ky, u), lambda ky, u: cols2(g, ky, u))
                    pe.wait_ge(b_copied, step_a(b, g, KH - 1) * 2 + 4)
                    for half in range(2):
                        logits(g, 0, 0, half)

                    def step(o, u, more=True, former=True):
                        for half in range(2):
                            if more:
                                logits(g, o + 1, 1 - u, half)
                            if half == 0 and former:
                                attend(g, o - 1, 1 - u)
                            turn(g, o, u, half)
                    octets(pe, step)
                    attend(g, OCTS - 1, 1)
            pe.sem_inc(s2_done, HAT_SLOTS)
            pe.sem_inc(av_done, 1)
            pe.sem_inc(l_in_psum, 8)
            pe.sem_inc(probs_turned, 2)
            pe.sem_inc(pt_in_psum, 4)
            batches(pe, body)

        @block.scalar
        def _(act):
            def body(b, s):
                act.wait_ge(x_loaded[s], (b + (2 - s)) * 8)
                gated(act, s2_done, b * (2 * KH) + HAT_SLOTS)
                for k in range(CHUNKS):
                    part = slice(k * CHUNK, (k + 1) * CHUNK)
                    act.activation(xn[:, part], xraw[:, s, part], ACT.Identity, scale=sh.rstd[:, bass.ds(b, 1)],
                                   bias=sh.shift[:, bass.ds(b, 1)]).then_inc(normed, 1)
                for k in range(1, CHUNKS, 2):
                    act.wait_ge(q_in_psum, b * CHUNKS + (k + 1))
                    act.activation(q[:, k * CHUNK:(k + 1) * CHUNK], bank[k][:, :], ACT.Copy).then_inc(q_by_act, 1)
                for k in range(1, CHUNKS, 2):
                    act.wait_ge(xT_in_psum, b * CHUNKS + (k + 1))
                    act.activation(xT[:, 4 * k:4 * k + 4, :].rearrange("c t n -> c (t n)"), bank[k][:, :], ACT.Copy).then_inc(xT_by_act, 1)
                act.wait_ge(var_ready, b + 1)
                act.activation(cen, gel, ACT.Sqrt).then_inc(std_ready, 1)
                act.wait_ge(scaled, b + 1)
                act.activation(gel, off, ACT.Gelu, scale=lnw[:, 0:1]).then_inc(gelu_ready, 1)
                act.wait_ge(offs_in_psum, b + 1)
                for g in range(GROUPS):
                    act.activation(place[:, g, :, :].rearrange("c a n -> c (a n)"), bank[2 + g][:, :], ACT.Tanh).then_inc(tanh_done, 1)
                for g in range(GROUPS):
                    act.activation(gate[:, g * KEYS:(g + 1) * KEYS], bank[4 + 2 * g][:, 0:KEYS], ACT.Tanh, scale=0.5).then_inc(tanh_done, 1)
                by_key = lambda ap: ap.rearrange("c k g x -> c g k x")
                act.wait_ge(place_ready, b * 5 + 5)
                act.activation(by_key(hat_x), place[:, :, 1, :].rearrange("c g (k x) -> c g k x", x=KW), ACT.Abs,
                               bias=table[:, T_NEGCOL:T_ONE]).then_inc(abs_prelude, 1)
                act.wait_ge(dist_ready, b * WINDOW + WINDOW)
                act.activation(S, S, ACT.Abs).then_inc(abs_prelude, 1)
                act.wait_ge(abs_prelude, b * 2 + 2)
                act.activation(hat_x, hat_x, ACT.Relu, scale=-1.0, bias=one).then_inc(hats_prelude, 1)
                act.activation(S, S, ACT.Relu, scale=-1.0, bias=one).then_inc(hats_prelude, 1)
                for t in range(2):
                    act.wait_ge(kv_in_psum, b * 3 + (t + 2))
                    act.activation(vals[:, t, :], bank[7 * t][:, :], ACT.Copy).then_inc(v_ready, 1)

                def distance(g, ky, u):
                    act.wait_ge(subtracted, step_a(b, g, ky) + 1)
                    act.activation(hat_slots[u], hat_slots[u], ACT.Abs).then_inc(abs_done, 1)

                def hat(g, ky, u):
                    act.wait_ge(abs_done, step_a(b, g, ky) + 1)
                    act.activation(hat_slots[u], hat_slots[u], ACT.Relu, scale=-1.0, bias=one).then_inc(hats_ready, 1)

                def exps(g, o, u, half):
                    e = step_e(b, g, o)
                    act.wait_ge(min_ready, e * 2 + (half + 1))
                    for j in range(4 * half, 4 * half + 4):
                        act.activation(probs[:, u, j, :], probs[:, u, j, :], ACT.Exp, scale=-1.0, bias=shift[:, u, j:j + 1],
                                       accum_out=sums[:, u, j:j + 1]).then_inc(exp_done, 1)

                def copy(g, o, u, half):
                    e = step_e(b, g, o)
                    act.wait_ge(pt_in_psum, e * 4 + (2 * half + 6))
                    act.activation(probsT[:, u, 1, :, half * 4:half * 4 + 4, :], bank[3][:, :].rearrange("c (j h i) -> c h j i", j=4, h=HPG),
                                   ACT.Copy).then_inc(pt_by_act, 1)

                for g in range(GROUPS):
                    pipelined(act, KH, HAT_SLOTS, lambda ky, u: distance(g, ky, u), lambda ky, u: hat(g, ky, u))
                    for half in range(2):
                        exps(g, 0, 0, half)

                    def step(o, u, more=True, former=True):
                        for half in range(2):
                            if more:
                                exps(g, o + 1, 1 - u, half)
                            copy(g, o, u, half)
                    octets(act, step)
            act.sem_inc(pt_by_act, 1)
            batches(act, body)

        @block.vector
        def _(dve):
            chain = Chain(dve, conv_chain, CONV_CHAIN)
            link = chain.link

            def body(b, s):
                chain.start(b)
                for k in range(0, CHUNKS, 2):
                    dve.wait_ge(q_in_psum, b * CHUNKS + (k + 1))
                    dve.tensor_copy(q[:, k * CHUNK:(k + 1) * CHUNK], bank[k][:, :]).then_inc(q_by_dve, 1)
                for k in range(0, CHUNKS, 2):
                    dve.wait_ge(xT_in_psum, b * CHUNKS + (k + 1))
                    dve.tensor_copy(xT[:, 4 * k:4 * k + 4, :].rearrange("c t n -> c (t n)"), bank[k][:, :]).then_inc(xT_by_dve, 1)
                dve.wait_ge(q_by_act, b * 4 + 4)
                dve.wait_ge(q_by_dve, b * 4 + 4)
                image = q[:, :].rearrange("c (y x) -> c y x", x=W)
                to = off.rearrange("c (y x) -> c y x", x=KW)
                taps = [(2, 2)] + [(y, x) for y in range(5) for x in range(5) if (y, x) != (2, 2)]
                for y, x in taps:
                    y0, x0 = int(y < 2), int(x < 2)
                    src = image[:, 4 * y0 + y - 2:H - 5 + y:4, 4 * x0 + x - 2:W - 5 + x:4]
                    tap = wdw[:, 5 * y + x:5 * y + x + 1]
                    if (y, x) == (2, 2):
                        link(dve.tensor_scalar(to, src, tap, None, ALU.mult))
                    else:
                        dst = to[:, y0:, x0:]
                        link(dve.scalar_tensor_tensor(dst, src, tap, dst, op0=ALU.mult, op1=ALU.add))
                chain.end()
                dve.sem_inc(conv_done, 1)
                dve.wait_ge(mean_ready, b + 1)
                dve.tensor_tensor(cen, off, bank[0][:, 0:KEYS], ALU.subtract).then_inc(var_chain, 1)
                dve.wait_ge(var_chain, b * 2 + 1)
                dve.tensor_tensor(gel, cen, cen, ALU.mult).then_inc(sq_made, 1)
                dve.wait_ge(sq_ready, b + 1)
                dve.tensor_scalar(gel, bank[1][:, 0:KEYS], GN_EPS, None, ALU.add).then_inc(var_ready, 1)
                dve.wait_ge(std_ready, b + 1)
                dve.reciprocal(cen, cen).then_inc(var_chain, 1)
                dve.wait_ge(var_chain, b * 2 + 2)
                dve.tensor_tensor(off, off, cen, ALU.mult).then_inc(scaled, 1)
                for g in range(GROUPS):
                    dve.wait_ge(tanh_done, b * 4 + (g + 1))
                    for axis in range(2):
                        p = place[:, g, axis, :].rearrange("c (k x) -> c k x", x=KW)
                        at = ref.rearrange("c (k o) -> c k o", o=1) if axis == 0 else ref.rearrange("c (o k) -> c o k", o=1)
                        dve.scalar_tensor_tensor(p, p, HALF / KH, at.to_broadcast([C, KH, KW]), op0=ALU.mult, op1=ALU.add).then_inc(place_ready, 1)
                dve.wait_ge(tanh_done, b * 4 + 4)
                dve.tensor_scalar(gate, gate, 0.5, 0.5, ALU.mult, ALU.add).then_inc(place_ready, 1)
                dve.wait_ge(place_ready, b * 5 + 5)
                for t in range(WINDOW):
                    dve.tensor_tensor(S[:, t, :].rearrange("c (k g x) -> c g k x", g=GROUPS, x=KW),
                                      place[:, :, 0, :].rearrange("c g (k x) -> c g k x", x=KW),
                                      table[:, T_ROW + t * KH:T_ROW + (t + 1) * KH].rearrange("c (g k x) -> c g k x", g=1, x=1).to_broadcast([C, GROUPS, KH, KW]),
                                      ALU.subtract).then_inc(dist_ready, 1)
                dve.wait_ge(hats_prelude, b * 2 + 2)
                dve.tensor_tensor(S, S, hat_x.rearrange("c k g x -> c (k g x)").rearrange("c (t m) -> c t m", t=1).to_broadcast([C, WINDOW, 2 * KEYS]),
                                  ALU.mult).then_inc(S_ready, 1)
                dve.wait_ge(xs_in_psum, b + 1)
                for g in range(GROUPS):
                    rows = slice(GC * g, GC * (g + 1))
                    dve.tensor_tensor(xs[rows, :].rearrange("c (k x) -> c k x", x=KW),
                                      bank[5][rows, :].rearrange("c (k g x) -> c k g x", g=GROUPS, x=KW)[:, :, g, :],
                                      gate[rows, g * KEYS:(g + 1) * KEYS].rearrange("c (k x) -> c k x", x=KW), ALU.mult).then_inc(xs_ready, 1)
                dve.wait_ge(kv_in_psum, b * 3 + 1)
                dve.tensor_copy(keys[:, :], bank[6][:, 0:KEYS]).then_inc(k_ready, 1)

                def copy_rows(g, ky, u):
                    a = step_a(b, g, ky)
                    for r in range(4):
                        h, half = r // 2, r % 2
                        dve.wait_ge(s1_done, a * 4 + (r + 1))
                        dve.tensor_copy(rows_T[:, u, half * 8:half * 8 + 8, h * H:(h + 1) * H],
                                        bank[r][:, :].rearrange("c (n i) -> c n i", i=H)).then_inc(t_copied, 1)

                def copy_bias(g, ky, u):
                    a = step_a(b, g, ky)
                    for half in range(2):
                        dve.wait_ge(s2_half, a * 2 + (half + 1))
                        dve.tensor_copy(bias[:, bass.ds(ky * KW + half * 8, 8), :], bank[4 + half][:, :].rearrange("c (n j) -> c n j", j=W)).then_inc(b_copied, 1)

                def add_bias(g, o, u, half):
                    e = step_e(b, g, o)
                    if half == 0:
                        dve.wait_ge(probs_turned, e + 1)
                    for p in (2 * half, 2 * half + 1):
                        dve.wait_ge(l_in_psum, e * 4 + (p + 1 + 8))
                        dve.tensor_tensor(probs[:, u, 2 * p:2 * p + 2, :], bank[p % 2][:, :].rearrange("c (j n) -> c j n", j=2),
                                          bias[:, :, :].rearrange("c n j -> c j n")[:, bass.ds(o * OCT + 2 * p, 2), :], ALU.add).then_inc(added, 1)
                    dve.wait_ge(added, e * 4 + (2 * half + 4))
                    dve.tensor_reduce(shift[:, u, 4 * half:4 * half + 4], probs[:, u, 4 * half:4 * half + 4, :], axis=AX.X, op=ALU.min).then_inc(min_ready, 1)

                def copy(g, o, u, half):
                    e = step_e(b, g, o)
                    dve.wait_ge(pt_in_psum, e * 4 + (2 * half + 5))
                    dve.tensor_copy(probsT[:, u, 0, :, half * 4:half * 4 + 4, :],
                                    bank[2][:, :].rearrange("c (j h i) -> c h j i", j=4, h=HPG)).then_inc(pt_by_dve, 1)

                def invert(g, o, u):
                    e = step_e(b, g, o)
                    dve.wait_ge(exp_done, e * 8 + 8)
                    dve.wait_ge(diag_ready, e * 2 + 2)
                    dve.reciprocal(inv[:, u, :], sums[:, u, :]).then_inc(inv_ready, 1)

                def accumulate(g, o, u):
                    e = step_e(b, g, o)
                    dve.wait_ge(av_done, e + 2)
                    at = xraw[:, s, :].rearrange("c (i j) -> c j i", j=W)[:, bass.ds(o * OCT, OCT), :]
                    dve.tensor_tensor(at, at, bank[4 + u][:, :].rearrange("c (j i) -> c j i", i=H), ALU.add).then_inc(acc_done, 1)

                for g in range(GROUPS):
                    dve.wait_ge(added, b * (2 * OCTS * 4) + (g * OCTS * 4 + 2))
                    dve.wait_ge(acc_done, b * (2 * OCTS) + (g * OCTS + 2))
                    pipelined(dve, KH, 2, lambda ky, u: copy_rows(g, ky, u), lambda ky, u: copy_bias(g, ky, u))
                    dve.wait_ge(b_copied, step_a(b, g, KH - 1) * 2 + 4)
                    for half in range(2):
                        add_bias(g, 0, 0, half)

                    def step(o, u, more=True, former=True):
                        invert(g, o, u)
                        for half in range(2):
                            if more:
                                add_bias(g, o + 1, 1 - u, half)
                            copy(g, o, u, half)
                            if half == 0 and former:
                                accumulate(g, o - 1, 1 - u)
                    octets(dve, step)
                    accumulate(g, OCTS - 1, 1)
                dve.wait_ge(acc_done, (b + 1) * (2 * OCTS) + 2)
                for k in range(CHUNKS):
                    dve.bn_stats(sh.stats[:, bass.ds(b, 1), k, :].rearrange("c b s -> c (b s)"),
                                 xraw[:, s, k * CHUNK:(k + 1) * CHUNK]).then_inc(stats_done, 1)
            dve.sem_inc(t_copied, 4)
            dve.sem_inc(b_copied, 2)
            dve.sem_inc(added, 2)
            dve.sem_inc(pt_by_dve, 1)
            dve.sem_inc(acc_done, 2)
            batches(dve, body)

def layer1(nc, sh, x_in, w, out):
    PAIRS, K2, MIN_CONN, MAX_CONN, NORM_EPS, GN8 = B // 2, 9, 1, 8, 1e-12, 8
    STEPS = H // ROWS
    LX = mybir.AxisListType.X
    SLOTS = 4
    BY_DVE, BY_POOL = (0, 2, 3, 5, 6), (1, 4, 7)
    ROUND = float(3 << 22)
    with ExitStack() as ctx:
        mem = Names(nc, ctx, "l1")
        xblk = mem.sbuf("xblk", [C, 2, 2, CHUNK])
        xnorm = mem.sbuf("xnorm", [C, ROWS, 2, W])
        xt = mem.sbuf("xt", [C, 2, H + 2, C])
        xleft = mem.sbuf("xleft", [C, 2, ROWS + 1, C])
        xright = mem.sbuf("xright", [C, 2, ROWS + 1, C])
        prod = [mem.sbuf(f"prod{q}", [C, ROWS, C]) for q in range(5)]
        dots = mem.sbuf("dots", [C, K2, H])
        inv_avg = mem.sbuf("inv_avg", [C, 2, 3, H + 2])
        sim = mem.sbuf("sim", [C, K2, H])
        rank = mem.sbuf("rank", [C, K2, H])
        wins = mem.sbuf("wins", [C, K2, H])
        beats = mem.sbuf("beats", [C, K2 - 1, H])
        total = mem.sbuf("total", [C, H])
        lap = mem.sbuf("lap", [C, H])
        kval = mem.sbuf("kval", [C, H])
        extreme = mem.sbuf("extreme", [C, 2])
        ext_row = mem.sbuf("ext_row", [2, 2])
        ext_wide = mem.sbuf("ext_wide", [2, 2, W])
        ext = mem.sbuf("ext", [C, 3])
        wsrc = mem.sbuf("wsrc", [C, K2, H])
        edge = mem.sbuf("edge", [C, 4])
        diag = mem.sbuf("diag", [C, K2, C])
        wdiag = mem.sbuf("wdiag", [C, SLOTS, K2, C])
        stage = mem.sbuf("stage", [C, 2, ROWS + 2, C])
        xres = mem.sbuf("xres", [C, 2, 2, CHUNK])
        affine = mem.sbuf("affine", [C, 2, CHUNK])
        enh = mem.sbuf("enh", [C, 2, 2, CHUNK])
        hid = mem.sbuf("hid", [C, 2, 2, CHUNK])
        res = mem.sbuf("res", [C, 2, 2, CHUNK])
        w1T = mem.sbuf("w1T", [C, 2, C])
        w2T = mem.sbuf("w2T", [C, 2, C])
        b1 = mem.sbuf("b1", [C, 2])
        b2 = mem.sbuf("b2", [C, 1])
        gscale = mem.sbuf("gscale", [C, B])
        gshift = mem.sbuf("gshift", [C, B])

        chain_sem = mem.sem("setup_chain")
        waits_met = mem.sem("waits_met")
        weight_chain = mem.sem("weight_chain")

        with ExitStack() as sctx:
            smem = Names(nc, sctx, "l1s")
            w1, w2 = xblk[:, 0, :, 0:C], xblk[:, 1, :, 0:C]
            gnw = smem.sbuf("gnw", [C, 2])
            mean8 = res[:, 0, 0, 0:C]
            mn = smem.sbuf("mn", [C, 2, B])
            g8 = smem.sbuf("g8", [C, 2, B])
            tmp = smem.sbuf("tmp", [C, B])
            ps = smem.psum("ps")
            ps2 = smem.psum("ps2")
            loaded = smem.sem("loaded")
            masks_ready = smem.sem("masks_ready")
            pool_chain = smem.sem("pool_chain")
            wt_in_psum = smem.sem("wt_in_psum")
            moments_ready = smem.sem("moments_ready")
            g8_ready = smem.sem("g8_ready")
            var_ready = smem.sem("var_ready")
            std_ready = smem.sem("std_ready")
            block = sctx.enter_context(nc.Block())

            @block.sync
            def _(sp):
                sp.dma_start(w1, w["w1"].rearrange("(h o) c -> o h c", h=2)).then_inc(loaded, 16)
                sp.dma_start(w2, w["w2"].rearrange("o (h c) -> o h c", h=2)).then_inc(loaded, 16)
                for h in range(2):
                    sp.dma_start(b1[:, h:h + 1], w["b1"][h * C:(h + 1) * C].rearrange("(o a) -> o a", a=1)).then_inc(loaded, 16)
                sp.dma_start(b2[:, :], w["b2"].rearrange("(o a) -> o a", a=1)).then_inc(loaded, 16)
                sp.dma_start(gnw[:, 0:1], w["gn_weight"].rearrange("(o a) -> o a", a=1)).then_inc(loaded, 16)
                sp.dma_start(gnw[:, 1:2], w["gn_bias"].rearrange("(o a) -> o a", a=1)).then_inc(loaded, 16)
                sp.wait_ge(loaded, 112)

            @block.gpsimd
            def _(pool):
                chain = Chain(pool, pool_chain)
                pool.memset(mean8, 1.0 / GN8)
                pool.memset(edge[:, :], 0.0)
                pool.memset(inv_avg[:, :, :, :], 0.0)
                pool.memset(wsrc[:, :, :], 0.0)
                chain.link(pool.memset(diag[:, :, :], 0.0))
                chain.link(pool.affine_select(out=mean8, in_=mean8, compare_op=ALU.is_ge, fill=0.0, base=0,
                                              pattern=[[-GN8, C // GN8], [0, GN8]], channel_multiplier=1))
                chain.link(pool.affine_select(out=mean8, in_=mean8, compare_op=ALU.is_ge, fill=0.0, base=GN8 - 1,
                                              pattern=[[GN8, C // GN8], [0, GN8]], channel_multiplier=-1))
                for b in range(2):
                    for k in range(K2):
                        part = diag[64 * b:64 * b + 64, k, 64 * b:64 * b + 64]
                        chain.link(pool.affine_select(out=part, in_=part, compare_op=ALU.not_equal, fill=1.0, base=-(k % 3 - 1),
                                                      pattern=[[-1, W]], channel_multiplier=1))
                    for col, at in ((0, 0), (2, W - 1)):
                        part = edge[64 * b:64 * b + 64, col:col + 1]
                        chain.link(pool.affine_select(out=part, in_=part, compare_op=ALU.not_equal, fill=1.0, base=-at,
                                                      pattern=[[0, 1]], channel_multiplier=1))
                pool.sem_inc(masks_ready, 1)

            @block.tensor
            def _(pe):
                pe.wait_ge(loaded, 112)
                for h in range(2):
                    pe.transpose(ps[:, h * C:(h + 1) * C], w1[:, h, :], sh.ident[:, :])
                for h in range(2):
                    last = pe.transpose(ps[:, (2 + h) * C:(3 + h) * C], w2[:, h, :], sh.ident[:, :])
                last.then_inc(wt_in_psum, 1)
                pe.wait_ge(moments_ready, 1)
                pe.wait_ge(masks_ready, 1)
                pe.matmul(ps2[:, 0:2 * B], mean8, mn[:, :, :].rearrange("c t b -> c (t b)"),
                          start=True, stop=True).then_inc(g8_ready, 1)

            @block.scalar
            def _(act):
                act.wait_ge(var_ready, 1)
                act.activation(tmp[:, :], tmp[:, :], ACT.Sqrt).then_inc(std_ready, 1)

            @block.vector
            def _(dve):
                chain = Chain(dve, chain_sem)
                link = chain.link
                mean, second = sh.moments[:, :, 0], sh.moments[:, :, 1]
                link(dve.tensor_tensor(mn[:, 0, :], mean, sh.rstd[:, :], ALU.mult))
                link(dve.tensor_tensor(tmp[:, :], mn[:, 0, :], sh.shift[:, :], ALU.mult))
                link(dve.tensor_tensor(mn[:, 0, :], mn[:, 0, :], sh.shift[:, :], ALU.add))
                link(dve.tensor_tensor(mn[:, 1, :], second, sh.rstd[:, :], ALU.mult))
                link(dve.tensor_tensor(mn[:, 1, :], mn[:, 1, :], sh.rstd[:, :], ALU.mult))
                link(dve.scalar_tensor_tensor(mn[:, 1, :], tmp[:, :], 2.0, mn[:, 1, :], op0=ALU.mult, op1=ALU.add))
                link(dve.tensor_tensor(tmp[:, :], sh.shift[:, :], sh.shift[:, :], ALU.mult))
                dve.tensor_tensor(mn[:, 1, :], mn[:, 1, :], tmp[:, :], ALU.add).then_inc(moments_ready, 1)
                dve.wait_ge(wt_in_psum, 1)
                dve.tensor_copy(w1T[:, :, :].rearrange("c h o -> c (h o)"), ps[:, 0:2 * C])
                dve.tensor_copy(w2T[:, :, :].rearrange("c h o -> c (h o)"), ps[:, 2 * C:4 * C])
                dve.wait_ge(g8_ready, 1)
                link(dve.tensor_copy(g8[:, :, :].rearrange("c t b -> c (t b)"), ps2[:, 0:2 * B]))
                link(dve.tensor_tensor(tmp[:, :], g8[:, 0, :], g8[:, 0, :], ALU.mult))
                link(dve.tensor_tensor(tmp[:, :], g8[:, 1, :], tmp[:, :], ALU.subtract))
                dve.tensor_scalar(tmp[:, :], tmp[:, :], GN_EPS, None, ALU.add).then_inc(var_ready, 1)
                dve.wait_ge(std_ready, 1)
                link(dve.reciprocal(tmp[:, :], tmp[:, :]))
                dve.wait_ge(loaded, 112)
                link(dve.tensor_scalar(tmp[:, :], tmp[:, :], gnw[:, 0:1], None, ALU.mult))
                link(dve.tensor_tensor(gscale[:, :], tmp[:, :], sh.rstd[:, :], ALU.mult))
                link(dve.tensor_tensor(g8[:, 1, :], sh.shift[:, :], g8[:, 0, :], ALU.subtract))
                link(dve.tensor_tensor(g8[:, 1, :], g8[:, 1, :], tmp[:, :], ALU.mult))
                dve.tensor_scalar(gshift[:, :], g8[:, 1, :], gnw[:, 1:2], None, ALU.add)
                dve.wait_ge(masks_ready, 1)
                dve.tensor_scalar(edge[:, 1:2], edge[:, 0:1], -1.0, 1.0, ALU.mult, ALU.add)
                dve.tensor_scalar(edge[:, 3:4], edge[:, 2:3], -1.0, 1.0, ALU.mult, ALU.add)

        turn_ps = [mem.psum("turn_ps")]
        gather_ps = [[mem.psum(f"gather_ps{u}{half}") for half in range(2)] for u in range(2)]
        hid_ps = [mem.psum(f"hid_ps{h}") for h in range(2)]
        ffn_ps = mem.psum("ffn_ps")

        blk_loaded = [mem.sem(f"blk_loaded{u}") for u in range(2)]
        normed = mem.sem("normed")
        turned = mem.sem("turned")
        turn_copied = mem.sem("turn_copied")
        shifted = [mem.sem(f"shifted{u}") for u in range(2)]
        squared = mem.sem("squared")
        pool_prods = mem.sem("pool_prods")
        dve_prods = mem.sem("dve_prods")
        summed = mem.sem("summed")
        norm_sums = mem.sem("norm_sums")
        roots = mem.sem("roots")
        cols_ready = mem.sem("cols_ready")
        cols_shifted = mem.sem("cols_shifted")
        ext_ready = mem.sem("ext_ready")
        ext_turned = mem.sem("ext_turned")
        sims_ready = mem.sem("sims_ready")
        exps_ready = mem.sem("exps_ready")
        weights_ready = mem.sem("weights_ready")
        weights_shifted = mem.sem("weights_shifted")
        res_loaded = [mem.sem(f"res_loaded{u}") for u in range(2)]
        staged = mem.sem("staged")
        diag_dve = mem.sem("diag_dve")
        diag_pool = mem.sem("diag_pool")
        row_done = mem.sem("row_done")
        affine_ready = mem.sem("affine_ready")
        enh_ready = mem.sem("enh_ready")
        hid_in_psum = mem.sem("hid_in_psum")
        hid_ready = mem.sem("hid_ready")
        ffn_in_psum = mem.sem("ffn_in_psum")
        ffn_copied = mem.sem("ffn_copied")
        res_half = mem.sem("res_half")
        res_ready = mem.sem("res_ready")
        stats_done = mem.sem("stats_done")
        stored = [mem.sem(f"stored{u}") for u in range(2)]
        SHIFTS = 8 * 16
        NCOLS = 24 * 16
        WS = 4 * 16

        block = ctx.enter_context(nc.Block())

        def rows_of(t, r, n):
            return xt[:, t % 2, bass.ds(r, n), :]

        def apart(eng, at):
            if not isinstance(at, int):
                eng.sem_inc(waits_met, 1)

        def second_before(t, c):
            return t > 1 or (t == 1 and not (isinstance(c, int) and c < 2))

        def block_before(t, c, lag):
            return (t - 1, c - lag + STEPS) if isinstance(c, int) and c < lag else (t, c - lag)

        def steps(eng, t, step):
            def body(j):
                for u in range(2):
                    step(j * 2 + u, u)
            peeled = 2 if t == 1 else 1
            for j in range(peeled):
                body(j)
            with eng.Fori(peeled, STEPS // 2) as j:
                body(j)

        def image(ap, t, c):
            return ap[2 * t:2 * t + 2].rearrange("b c n -> c b n")[:, :, bass.ds(c * CHUNK, CHUNK)]

        @block.sync
        def _(sp):
            def load_block(t, c, u):
                wait(sp, normed, c + (t * STEPS - 1))
                apart(sp, c)
                sp.dma_start(xblk[:, u, :, :], image(x_in, t, c)).then_inc(blk_loaded[u], 16)

            def shift(t, c, u):
                n = t * STEPS + c
                sp.wait_ge(turn_copied, (n + 1) * 2)
                wait(sp, summed, n - 1)
                apart(sp, c)
                src = rows_of(t, c * ROWS, ROWS + 1)
                for b in range(2):
                    p = 64 * b
                    sp.dma_start(xleft[p + 1:p + 64, u, :, :], src[p:p + 63]).then_inc(shifted[u], 16)
                    sp.dma_start(xleft[p:p + 1, u, :, :], src[p + 1:p + 2]).then_inc(shifted[u], 16)
                    sp.dma_start(xright[p:p + 63, u, :, :], src[p + 1:p + 64]).then_inc(shifted[u], 16)
                    sp.dma_start(xright[p + 63:p + 64, u, :, :], src[p + 62:p + 63]).then_inc(shifted[u], 16)

            def load_res(t, c, u):
                g = (t - 1) * STEPS + c
                wait(sp, res_ready, (g - 1) * 2)
                apart(sp, c)
                sp.dma_start(xres[:, u, :, :], image(x_in, t - 1, c)).then_inc(res_loaded[u], 16)

            def store(t, c, u):
                sp.wait_ge(res_ready, (c + ((t - 1) * STEPS + 1)) * 2)
                apart(sp, c)
                sp.dma_start(image(out, t - 1, c), res[:, u, :, :]).then_inc(stored[u], 16)

            for t in range(PAIRS + 1):
                def step(c, u):
                    if t < PAIRS:
                        load_block(t, c, u)
                    if t >= 1:
                        load_res(t, c, u)
                    if t < PAIRS:
                        shift(t, c, u)
                    if second_before(t, c):
                        store(*block_before(t, c, 2), u)
                steps(sp, t, step)
                if t < PAIRS:
                    sp.wait_ge(cols_ready, t + 1)
                    for b in range(2):
                        p = 64 * b
                        lo, hi = slice(p, p + 63), slice(p + 1, p + 64)
                        first, second, but1, last = (slice(p + q, p + q + 1) for q in (0, 1, 62, 63))
                        moves = [
                            (inv_avg[hi, 0, 0, 1:H + 1], inv_avg[lo, 0, 1, 1:H + 1]),
                            (inv_avg[hi, 1, 0, 1:H + 1], inv_avg[lo, 1, 1, 1:H + 1]),
                            (inv_avg[lo, 0, 2, 1:H + 1], inv_avg[hi, 0, 1, 1:H + 1]),
                            (inv_avg[lo, 1, 2, 1:H + 1], inv_avg[hi, 1, 1, 1:H + 1]),
                            (inv_avg[first, 0, 0, 1:H + 1], inv_avg[second, 0, 1, 1:H + 1]),
                            (inv_avg[last, 0, 2, 1:H + 1], inv_avg[but1, 0, 1, 1:H + 1]),
                            (dots[hi, 3, :], dots[lo, 5, :]),
                            (dots[first, 3, :], dots[first, 5, :]),
                        ]
                        more = [
                            (dots[lo, 8, 0:H - 1], dots[hi, 0, 1:H]),
                            (dots[last, 8, 0:H - 1], dots[but1, 2, 1:H]),
                            (dots[hi, 6, 0:H - 1], dots[lo, 2, 1:H]),
                            (dots[first, 6, 0:H - 1], dots[second, 0, 1:H]),
                        ]
                        for to, of in moves + more:
                            sp.dma_start(to, of).then_inc(cols_shifted, 16)
                    sp.wait_ge(weights_ready, t + 1)
                    by_dx = lambda ap, dx: ap.rearrange("p (e d) y -> p e d y", d=3)[:, :, dx, :]
                    for b in range(2):
                        p = 64 * b
                        lo, hi = slice(p, p + 63), slice(p + 1, p + 64)
                        sp.dma_start(by_dx(wsrc[hi, :, :], 2), by_dx(sim[lo, :, :], 2)).then_inc(weights_shifted, 16)
                        sp.dma_start(by_dx(wsrc[lo, :, :], 0), by_dx(sim[hi, :, :], 0)).then_inc(weights_shifted, 16)
            for c in (STEPS - 2, STEPS - 1):
                store(PAIRS, c, c % 2)
            for u in range(2):
                sp.wait_ge(stored[u], 16 * PAIRS * STEPS // 2)

        @block.gpsimd
        def _(pool):
            def build(t, c, *rows):
                g = (t - 1) * STEPS + c
                pool.wait_ge(weights_shifted, WS * t)
                for y in rows:
                    wait(pool, row_done, g * ROWS + (y + 1 - SLOTS))
                    apart(pool, c)
                    pool.tensor_tensor(wdiag[:, y % SLOTS, :, :], diag[:, :, :],
                                      wsrc[:, :, bass.ds(c * ROWS + y, 1)].to_broadcast([C, K2, C]), ALU.mult).then_inc(diag_pool, 1)

            def prod_up(t, c):
                n = t * STEPS + c
                pool.wait_ge(turn_copied, (n + 1) * 2)
                wait(pool, summed, n)
                apart(pool, c)
                x, up = rows_of(t, c * ROWS + 1, ROWS), rows_of(t, c * ROWS, ROWS)
                pool.tensor_tensor(prod[2][:, :, :], x, up, ALU.mult).then_inc(pool_prods, 1)

            def prod_right(t, c, u):
                x = rows_of(t, c * ROWS + 1, ROWS)
                pool.wait_ge(shifted[u], (c + (t * STEPS + 2 - u)) * (SHIFTS // 2))
                apart(pool, c)
                pool.tensor_tensor(prod[1][:, :, :], x, xright[:, u, 1:ROWS + 1, :], ALU.mult).then_inc(pool_prods, 1)

            def result(g, u, *images):
                for b in images:
                    pool.wait_ge(ffn_copied, g * 2 + (b + 1))
                    pool.tensor_tensor(res[:, u, b, :], res[:, u, b, :], enh[:, u, b, :], ALU.add).then_inc(res_half, 1)
                    pool.wait_ge(res_half, g * 2 + (b + 1))
                    pool.tensor_tensor(res[:, u, b, :], res[:, u, b, :], xres[:, u, b, :], ALU.add).then_inc(res_ready, 1)

            for t in range(PAIRS + 1):
                def step(c, u):
                    if t >= 1:
                        build(t, c, 1)
                    if second_before(t, c):
                        result(c + ((t - 1) * STEPS - 2), u, 0)
                    if t >= 1:
                        build(t, c, 4)
                    if second_before(t, c):
                        result(c + ((t - 1) * STEPS - 2), u, 1)
                    if t < PAIRS and not (isinstance(c, int) and c == 0):
                        prod_up(t, c - 1)
                    if t >= 1:
                        build(t, c, 7)
                    if t < PAIRS and not (isinstance(c, int) and c == 0):
                        prod_right(t, c - 1, 1 - u)
                steps(pool, t, step)
                if t < PAIRS:
                    prod_up(t, STEPS - 1)
                    prod_right(t, STEPS - 1, 1)
            for g in (PAIRS * STEPS - 2, PAIRS * STEPS - 1):
                result(g, g % 2, 0, 1)

        @block.tensor
        def _(pe):
            def turn(t, c, u):
                n = t * STEPS + c
                pe.wait_ge(normed, n + 1)
                if isinstance(c, int) and c == 0:
                    wait(pe, weights_ready, t)
                for half in range(2):
                    wait(pe, turn_copied, n * 2 + half)
                    for r in range(4):
                        y = 4 * half + r
                        last = pe.transpose(turn_ps[0][:, r * C:(r + 1) * C], xnorm[:, y, :, :].rearrange("c b w -> c (b w)"), sh.ident[:, :])
                    last.then_inc(turned, 1)

            def gather(t, c, u, rows):
                g = (t - 1) * STEPS + c
                for y in rows:
                    if y == 0:
                        pe.wait_ge(staged, g + 1)
                        wait(pe, enh_ready, (g - 1) * 2)
                    for ready, own in ((diag_dve, BY_DVE), (diag_pool, BY_POOL)):
                        if y in own:
                            pe.wait_ge(ready, g * len(own) + (own.index(y) + 1))
                    for k in range(K2):
                        last = pe.matmul(gather_ps[u][y // 4][:, y % 4 * C:(y % 4 + 1) * C], stage[:, u, y + k // 3, :],
                                         wdiag[:, y % SLOTS, k, :], start=(k == 0), stop=(k == K2 - 1))
                    last.then_inc(row_done, 1)

            def hidden(g, u, b):
                pe.wait_ge(enh_ready, g * 2 + 2)
                for h in range(2):
                    wait(pe, hid_ready, (g * 2 + b - 1) * 2 + h + 1)
                    pe.matmul(hid_ps[h][:, :], w1T[:, h, :], enh[:, u, b, :], start=True, stop=True).then_inc(hid_in_psum, 1)

            def down(g, b):
                wait(pe, ffn_copied, g * 2 + b)
                for h in range(2):
                    pe.wait_ge(hid_ready, (g * 2 + b) * 2 + (h + 1))
                    last = pe.matmul(ffn_ps[:, :], w2T[:, h, :], hid[:, b, h, :], start=(h == 0), stop=(h == 1))
                last.then_inc(ffn_in_psum, 1)

            for t in range(PAIRS + 1):
                def step(c, u):
                    before = t >= 1 and not (isinstance(c, int) and t == 1 and c == 0)
                    g = (t - 1) * STEPS - 1 + c
                    if t >= 1:
                        gather(t, c, u, (0, 1))
                    if before:
                        hidden(g, 1 - u, 0)
                    if t < PAIRS:
                        turn(t, c, u)
                    if t >= 1:
                        gather(t, c, u, (2, 3))
                    if before:
                        down(g, 0)
                        hidden(g, 1 - u, 1)
                    if t >= 1:
                        gather(t, c, u, (4, 5))
                    if before:
                        down(g, 1)
                    if t >= 1:
                        gather(t, c, u, (6, 7))
                steps(pe, t, step)
                if t < PAIRS:
                    pe.wait_ge(ext_ready, 2 * t + 1)
                    pe.transpose(turn_ps[0][0:2, 0:C], extreme[:, :], sh.ident[:, :]).then_inc(ext_turned, 1)
                    pe.wait_ge(ext_ready, 2 * t + 2)
                    pe.transpose(turn_ps[0][:, C:C + 2], ext_wide[:, :, :].rearrange("q b w -> q (b w)"),
                                 sh.ident[0:2, 0:2]).then_inc(ext_turned, 1)
            g = PAIRS * STEPS - 1
            for b in range(2):
                hidden(g, 1, b)
                down(g, b)

        @block.scalar
        def _(act):
            def norm(t, c, u):
                n = t * STEPS + c
                act.wait_ge(blk_loaded[u], (n + (2 - u)) * 8)
                wait(act, turned, n * 2)
                for b in range(2):
                    last = act.activation(xnorm[:, :, b, :], xblk[:, u, b, :].rearrange("c (r w) -> c r w", w=W), ACT.Identity,
                                          scale=sh.rstd[:, 2 * t + b:2 * t + b + 1], bias=sh.shift[:, 2 * t + b:2 * t + b + 1])
                last.then_inc(normed, 1)

            def copy_turned(t, c, u):
                n = t * STEPS + c
                for half in range(2):
                    act.wait_ge(turned, n * 2 + (half + 1))
                    apart(act, c)
                    if isinstance(c, int) and c == 0 and half == 0:
                        act.activation(xt[:, t % 2, 0, :], turn_ps[0][:, C:2 * C], ACT.Copy)
                    act.activation(rows_of(t, c * ROWS + (1 + 4 * half), 4), turn_ps[0][:, :].rearrange("p (r c) -> p r c", c=C),
                                   ACT.Copy).then_inc(turn_copied, 1)

            def relu(g, b):
                for h in range(2):
                    act.wait_ge(hid_in_psum, (g * 2 + b) * 2 + (h + 1))
                    wait(act, ffn_in_psum, (g - 1) * 2 + b + 1)
                    act.activation(hid[:, b, h, :], hid_ps[h][:, :], ACT.Relu, bias=b1[:, h:h + 1]).then_inc(hid_ready, 1)

            def copy_ffn(g, u, b):
                act.wait_ge(ffn_in_psum, g * 2 + (b + 1))
                if b == 0:
                    wait(act, stored[u], (g - u) * 8)
                    wait(act, stats_done, (g - 1) * 2)
                act.activation(res[:, u, b, :], ffn_ps[:, :], ACT.Identity, bias=b2[:, :]).then_inc(ffn_copied, 1)

            def square(t, c):
                n = t * STEPS + c
                act.wait_ge(turn_copied, (n + 1) * 2)
                wait(act, summed, n)
                apart(act, c)
                act.activation(prod[0][:, :, :], rows_of(t, c * ROWS + 1, ROWS), ACT.Square).then_inc(squared, 1)

            def gn_affine(t, c, u):
                g = (t - 1) * STEPS + c
                act.wait_ge(res_loaded[u], (g + (2 - u)) * 8)
                wait(act, enh_ready, g * 2)
                for b in range(2):
                    n = 2 * (t - 1) + b
                    act.activation(affine[:, b, :], xres[:, u, b, :], ACT.Identity, scale=gscale[:, n:n + 1],
                                   bias=gshift[:, n:n + 1]).then_inc(affine_ready, 1)

            for t in range(PAIRS + 1):
                if 2 <= t < PAIRS:
                    act.wait_ge(staged, (t - 1) * STEPS)

                def step(c, u):
                    before = t >= 1 and not (isinstance(c, int) and t == 1 and c == 0)
                    g = (t - 1) * STEPS - 1 + c
                    if t < PAIRS:
                        norm(t, c, u)
                    if before:
                        relu(g, 0)
                    if t < PAIRS:
                        copy_turned(t, c, u)
                    if before:
                        copy_ffn(g, 1 - u, 0)
                        relu(g, 1)
                    if t < PAIRS and not (isinstance(c, int) and c == 0):
                        square(t, c - 1)
                    if before:
                        copy_ffn(g, 1 - u, 1)
                    if t >= 1:
                        gn_affine(t, c, u)
                steps(act, t, step)
                if t < PAIRS:
                    square(t, STEPS - 1)
                    act.wait_ge(turn_copied, (t + 1) * STEPS * 2)
                    act.activation(xt[:, t % 2, H + 1, :], xt[:, t % 2, H - 1, :], ACT.Copy)
                    act.wait_ge(norm_sums, t + 1)
                    act.activation(total[:, :], dots[:, 4, :], ACT.Sqrt).then_inc(roots, 1)
                    act.wait_ge(sims_ready, t + 1)
                    act.activation(wins[:, :, :], sim[:, :, :], ACT.Exp).then_inc(exps_ready, 1)
            g = PAIRS * STEPS - 1
            for b in range(2):
                relu(g, b)
                copy_ffn(g, 1, b)

        @block.vector
        def _(dve):
            chain = Chain(dve, weight_chain)
            link = chain.link

            def build(t, c, *rows):
                g = (t - 1) * STEPS + c
                for y in rows:
                    wait(dve, row_done, g * ROWS + (y + 1 - SLOTS))
                    dve.tensor_tensor(wdiag[:, y % SLOTS, :, :], diag[:, :, :],
                                      wsrc[:, :, bass.ds(c * ROWS + y, 1)].to_broadcast([C, K2, C]), ALU.mult).then_inc(diag_dve, 1)

            def put_stage(t, c, u):
                g = (t - 1) * STEPS + c
                wait(dve, row_done, (g - 1) * ROWS)
                dve.tensor_copy(stage[:, u, :, :], rows_of(t - 1, c * ROWS, ROWS + 2)).then_inc(staged, 1)

            def enhance(g, u):
                for half in range(2):
                    dve.wait_ge(row_done, g * ROWS + 4 * (half + 1))
                    if half == 0:
                        dve.wait_ge(affine_ready, g * 2 + 2)
                        wait(dve, res_half, (g - 1) * 2)
                    part = lambda ap: ap.rearrange("c b (y x) -> c y b x", x=W)[:, 4 * half:4 * half + 4, :, :]
                    dve.tensor_tensor(part(enh[:, u, :, :]), gather_ps[u][half][:, :].rearrange("c (y b x) -> c y b x", b=2, x=W),
                                      part(affine[:, :, :]), ALU.add).then_inc(enh_ready, 1)

            def stats(t, c, u):
                g = c + (t - 1) * STEPS
                for b in range(2):
                    dve.wait_ge(res_ready, g * 2 + (b + 1))
                    dve.bn_stats(sh.stats[:, 2 * (t - 1) + b, bass.ds(c, 1), :].rearrange("c k s -> c (k s)"),
                                 res[:, u, b, :]).then_inc(stats_done, 1)

            def sums(t, c, u):
                side_prods(t, c, u)
                side_sums(t, c)
                pool_sums(t, c)

            def side_prods(t, c, u):
                n = t * STEPS + c
                x = rows_of(t, c * ROWS + 1, ROWS)
                dve.wait_ge(turn_copied, (n + 1) * 2)
                dve.wait_ge(shifted[u], (c + (t * STEPS + 2 - u)) * (SHIFTS // 2))
                wait(dve, summed, n)
                dve.tensor_tensor(prod[3][:, :, :], x, xleft[:, u, 0:ROWS, :], ALU.mult).then_inc(dve_prods, 1)
                dve.tensor_tensor(prod[4][:, :, :], x, xright[:, u, 0:ROWS, :], ALU.mult).then_inc(dve_prods, 1)

            def sum_up(t, c, *those):
                n, col = t * STEPS + c, bass.ds(c * ROWS, ROWS)
                for q, k, ready, value in those:
                    dve.wait_ge(ready, n * value[0] + value[1])
                    last = dve.reduce_sum(dots[:, k, col], prod[q][:, :, :], axis=LX)
                return last

            def side_sums(t, c):
                dve.reduce_sum(inv_avg[:, 1, 1, bass.ds(c * ROWS + 1, ROWS)], rows_of(t, c * ROWS + 1, ROWS), axis=LX)
                sum_up(t, c, (3, 0, dve_prods, (2, 1)), (4, 2, dve_prods, (2, 2)))

            def pool_sums(t, c):
                sum_up(t, c, (0, 4, squared, (1, 1)), (2, 1, pool_prods, (2, 1)), (1, 5, pool_prods, (2, 2))).then_inc(summed, 1)

            def weights(t):
                dve.wait_ge(summed, (t + 1) * STEPS)
                dve.tensor_copy(dots[:, 7, 0:H - 1], dots[:, 1, 1:H]).then_inc(norm_sums, 1)
                dve.tensor_copy(dots[:, 7, H - 1:H], dots[:, 1, H - 1:H])
                dve.wait_ge(roots, t + 1)
                link(dve.tensor_scalar(total[:, :], total[:, :], NORM_EPS, None, ALU.max))
                dve.tensor_scalar(inv_avg[:, 1, 1, 1:H + 1], inv_avg[:, 1, 1, 1:H + 1], 1.0 / C, None, ALU.mult)
                link(dve.reciprocal(inv_avg[:, 0, 1, 1:H + 1], total[:, :]))
                dve.tensor_copy(inv_avg[:, 0, 1, 0:1], inv_avg[:, 0, 1, 2:3]).then_inc(cols_ready, 1)
                dve.tensor_copy(inv_avg[:, 0, 1, H + 1:H + 2], inv_avg[:, 0, 1, H - 1:H])
                dve.wait_ge(cols_shifted, NCOLS * (t + 1))
                for d in (0, 2):
                    dve.tensor_copy(inv_avg[:, 0, d, 0:1], inv_avg[:, 0, d, 2:3])
                    dve.tensor_copy(inv_avg[:, 0, d, H + 1:H + 2], inv_avg[:, 0, d, H - 1:H])
                dve.tensor_copy(dots[:, 8, H - 1:H], dots[:, 2, H - 1:H])
                link(dve.tensor_copy(dots[:, 6, H - 1:H], dots[:, 0, H - 1:H]))
                a = inv_avg[:, 1, :, :]
                link(dve.tensor_tensor(lap[:, :], a[:, 1, 0:H], a[:, 1, 2:H + 2], ALU.add))
                link(dve.tensor_tensor(lap[:, :], lap[:, :], a[:, 0, 1:H + 1], ALU.add))
                link(dve.tensor_tensor(lap[:, :], lap[:, :], a[:, 2, 1:H + 1], ALU.add))
                link(dve.scalar_tensor_tensor(lap[:, :], a[:, 1, 1:H + 1], 4.0, lap[:, :], op0=ALU.mult, op1=ALU.subtract))
                link(dve.scalar_tensor_tensor(lap[:, :], lap[:, :], -1.0, lap[:, :], op0=ALU.mult, op1=ALU.max))
                dve.tensor_reduce(extreme[:, 0:1], lap[:, :], axis=LX, op=ALU.min)
                dve.tensor_reduce(extreme[:, 1:2], lap[:, :], axis=LX, op=ALU.max, negate=True).then_inc(ext_ready, 1)
                for e in range(3):
                    last = dve.tensor_tensor(sim[:, 3 * e:3 * e + 3, :], dots[:, 3 * e:3 * e + 3, :],
                                             inv_avg[:, 0, :, e:e + H], ALU.mult)
                link(last)
                centre = inv_avg[:, 0, 1:2, 1:H + 1].to_broadcast([C, K2, H])
                dve.tensor_tensor(sim[:, :, :], sim[:, :, :], centre, ALU.mult).then_inc(sims_ready, 1)
                dve.wait_ge(ext_turned, 2 * t + 1)
                link(dve.tensor_reduce(ext_row[:, :], turn_ps[0][0:2, 0:C].rearrange("q (b w) -> q b w", b=2), axis=LX, op=ALU.min))
                dve.tensor_copy(ext_wide[:, :, :], ext_row[:, :].rearrange("q (b o) -> q b o", o=1).to_broadcast([2, 2, W])).then_inc(ext_ready, 1)
                dve.wait_ge(ext_turned, 2 * t + 2)
                link(dve.tensor_copy(ext[:, 0:2], turn_ps[0][:, C:C + 2]))
                link(dve.tensor_tensor(ext[:, 2:3], ext[:, 0:1], ext[:, 1:2], ALU.add))
                link(dve.tensor_scalar(ext[:, 2:3], ext[:, 2:3], -1.0, 1e-8, ALU.mult, ALU.add))
                link(dve.reciprocal(ext[:, 2:3], ext[:, 2:3]))
                link(dve.tensor_scalar(kval[:, :], lap[:, :], ext[:, 0:1], ext[:, 2:3], ALU.subtract, ALU.mult))
                link(dve.tensor_scalar(kval[:, :], kval[:, :], float(MAX_CONN - MIN_CONN), ROUND, ALU.mult, ALU.add))
                link(dve.tensor_scalar(kval[:, :], kval[:, :], ROUND, float(MIN_CONN), ALU.subtract, ALU.add))
                dve.wait_ge(sims_ready, t + 1)
                dve.wait_ge(exps_ready, t + 1)
                for k in range(K2):
                    last = dve.memset(rank[:, k, :], float(K2 - 1 - k))
                link(last)
                for j in range(K2 - 1):
                    m = K2 - 1 - j
                    link(dve.tensor_tensor(beats[:, 0:m, :], sim[:, j:j + 1, :].to_broadcast([C, m, H]), sim[:, j + 1:K2, :], ALU.is_ge))
                    dve.tensor_tensor(rank[:, j + 1:K2, :], rank[:, j + 1:K2, :], beats[:, 0:m, :], ALU.add)
                    link(dve.reduce_sum(total[:, :], beats[:, 0:m, :].rearrange("p k y -> p y k"), axis=LX))
                    link(dve.tensor_tensor(rank[:, j, :], rank[:, j, :], total[:, :], ALU.subtract))
                link(dve.tensor_tensor(rank[:, :, :], rank[:, :, :], kval[:, :].rearrange("p (o y) -> p o y", o=1).to_broadcast([C, K2, H]), ALU.is_lt))
                link(dve.tensor_tensor(wins[:, :, :], wins[:, :, :], rank[:, :, :], ALU.mult))
                link(dve.reduce_sum(total[:, :], wins[:, :, :].rearrange("p k y -> p y k"), axis=LX))
                link(dve.reciprocal(total[:, :], total[:, :]))
                link(dve.tensor_tensor(sim[:, :, :], wins[:, :, :], total[:, :].rearrange("p (o y) -> p o y", o=1).to_broadcast([C, K2, H]), ALU.mult))
                by_dx = lambda ap, d: ap.rearrange("p (e d) y -> p e d y", d=3)[:, :, d, :]
                left, right = by_dx(sim[:, :, :], 0), by_dx(sim[:, :, :], 2)
                link(dve.scalar_tensor_tensor(right, left, edge[:, 0:1], right, op0=ALU.mult, op1=ALU.add))
                link(dve.tensor_scalar(left, left, edge[:, 1:2], None, ALU.mult))
                link(dve.scalar_tensor_tensor(left, right, edge[:, 2:3], left, op0=ALU.mult, op1=ALU.add))
                link(dve.tensor_scalar(right, right, edge[:, 3:4], None, ALU.mult))
                if t:
                    dve.wait_ge(diag_pool, t * STEPS * len(BY_POOL))
                    dve.wait_ge(diag_dve, t * STEPS * len(BY_DVE))
                dve.tensor_copy(by_dx(wsrc[:, :, :], 1), by_dx(sim[:, :, :], 1)).then_inc(weights_ready, 1)

            for t in range(PAIRS + 1):
                if t >= 1:
                    dve.wait_ge(weights_shifted, WS * t)

                def step(c, u):
                    before = t >= 1 and not (isinstance(c, int) and t == 1 and c == 0)
                    g = (t - 1) * STEPS - 1 + c
                    if t >= 1:
                        put_stage(t, c, u)
                        build(t, c, 0, 2)
                    if before:
                        enhance(g, 1 - u)
                    lagging = t < PAIRS and not (isinstance(c, int) and c == 0)
                    if lagging:
                        side_prods(t, c - 1, 1 - u)
                    if t >= 1:
                        build(t, c, 3)
                    if lagging:
                        side_sums(t, c - 1)
                    if t >= 1:
                        build(t, c, 5)
                    if lagging:
                        pool_sums(t, c - 1)
                    if t >= 1:
                        build(t, c, 6)
                    if second_before(t, c):
                        stats(*block_before(t, c, 2), u)
                steps(dve, t, step)
                if t < PAIRS:
                    sums(t, STEPS - 1, 1)
                    weights(t)
            g = PAIRS * STEPS - 1
            enhance(g, 1)
            for c in (STEPS - 2, STEPS - 1):
                stats(PAIRS, c, c % 2)

def layer2(nc, sh, x_in, w, out):
    ROUNDS = B // 2
    P5, P11 = 2, 5
    BLOCKS, BROWS = 4, H // 4
    XW = W + 2 * P11
    with ExitStack() as ctx:
        mem = Names(nc, ctx, "l2")
        xin = mem.sbuf("xin", [C, 2, HW])
        xpad = mem.sbuf("xpad", [C, 2, H + 2, XW])
        sum33 = mem.sbuf("sum33", [C, H, W])
        mid5 = mem.sbuf("mid5", [C, H + 2 * P5, W])
        mid11 = mem.sbuf("mid11", [C, H + 2 * P11, W])
        res = mem.sbuf("res", [C, 2, HW])
        w33 = mem.sbuf("w33", [C, 9])
        w15 = mem.sbuf("w15", [C, 5])
        w51 = mem.sbuf("w51", [C, 5])
        w111 = mem.sbuf("w111", [C, 11])
        w1111 = mem.sbuf("w1111", [C, 11])
        biases = mem.sbuf("biases", [C, 6])
        w3 = mem.sbuf("w3", [C, C])
        w3T = mem.sbuf("w3T", [C, C])
        fold5 = mem.sbuf("fold5", [C, 5, C])
        fold11 = mem.sbuf("fold11", [C, 11, C])
        bsum = mem.sbuf("bsum", [C, 1])
        mix_bias = mem.sbuf("mix_bias", [C, 1])
        NPS = 4
        mix = [mem.psum(f"mix{k}") for k in range(NPS)]
        setup_ps = mem.psum("setup_ps")

        weights_loaded = mem.sem("weights_loaded")
        pads_zero = mem.sem("pads_zero")
        setup_chain = mem.sem("setup_chain")
        w3T_in_psum = mem.sem("w3T_in_psum")
        w3T_ready = mem.sem("w3T_ready")
        bias_in_psum = mem.sem("bias_in_psum")
        mix_bias_ready = mem.sem("mix_bias_ready")
        folds_ready = mem.sem("folds_ready")
        x_loaded = [mem.sem(f"x_loaded{s}") for s in range(2)]
        normed = [mem.sem(f"normed{s}") for s in range(2)]
        tap_chain = mem.sem("tap_chain")
        taps_done = mem.sem("taps_done")
        mixed = mem.sem("mixed")
        evacuated = mem.sem("evacuated")
        gated = mem.sem("gated")
        res_ready = mem.sem("res_ready")
        stats_done = mem.sem("stats_done")
        stored = [mem.sem(f"stored{s}") for s in range(2)]
        smalls = [(w33, w["w0"]), (w15, w["w0_1"]), (w51, w["w0_2"]), (w111, w["w1_1"]), (w1111, w["w1_2"]), (w3, w["w3"])]
        vectors = ["b0", "b0_1", "b0_2", "b1_1", "b1_2", "b3"]
        LOADS = 16 * (len(smalls) + len(vectors))
        block = ctx.enter_context(nc.Block())

        def interior(s, r0=0, nr=H):
            return xpad[:, s, 1 + r0:1 + r0 + nr, P11:P11 + W]

        @block.sync
        def _(sp):
            for t, src in smalls:
                sp.dma_start(t[:, :], src).then_inc(weights_loaded, 16)
            for k, name in enumerate(vectors):
                sp.dma_start(biases[:, k:k + 1], w[name]).then_inc(weights_loaded, 16)

            def load(i, s):
                wait(sp, res_ready, (i * 2 + (s - 1)) * CHUNKS)
                sp.dma_start(xin[:, s, :], x_in[bass.ds(i * 2 + s, 1)].rearrange("b c n -> (b c) n")).then_inc(x_loaded[s], 16)

            def store(i, s):
                n = i * 2 + s
                sp.wait_ge(res_ready, (n + 1) * CHUNKS)
                sp.dma_start(out[bass.ds(n, 1)].rearrange("b c n -> (b c) n"), res[:, s, :]).then_inc(stored[s], 16)

            load(0, 0)
            load(0, 1)
            with sp.Fori(0, ROUNDS - 1) as i:
                for s in range(2):
                    store(i, s)
                    load(i + 1, s)
            for s in range(2):
                store(ROUNDS - 1, s)
            for s in range(2):
                sp.wait_ge(stored[s], 16 * ROUNDS)

        @block.gpsimd
        def _(pool):
            pool.memset(xpad[:, :, :, :], 0.0).then_inc(pads_zero, 1)
            for t, p in ((mid5, P5), (mid11, P11)):
                pool.memset(t[:, 0:p, :], 0.0).then_inc(pads_zero, 1)
                pool.memset(t[:, H + p:H + 2 * p, :], 0.0).then_inc(pads_zero, 1)

            def body(i):
                for s in range(2):
                    n = i * 2 + s
                    for k in range(CHUNKS):
                        part = res[:, s, k * CHUNK:(k + 1) * CHUNK]
                        image = part.rearrange("c (h w) -> c h w", w=W)
                        pool.wait_ge(evacuated, n * CHUNKS + (k + 1))
                        pool.tensor_tensor(image, image, interior(s, k * ROWS, ROWS), ALU.mult).then_inc(gated, 1)
                        pool.wait_ge(gated, n * CHUNKS + (k + 1))
                        pool.tensor_tensor(part, part, xin[:, s, k * CHUNK:(k + 1) * CHUNK], ALU.add).then_inc(res_ready, 1)
            each(pool, ROUNDS, body)

        @block.tensor
        def _(pe):
            pe.wait_ge(weights_loaded, LOADS)
            pe.transpose(setup_ps[:, 0:C], w3[:, :], sh.ident[:, :]).then_inc(w3T_in_psum, 1)
            pe.wait_ge(w3T_ready, 2)
            pe.matmul(setup_ps[:, C:C + 1], w3T[:, :], bsum[:, :], start=True, stop=True).then_inc(bias_in_psum, 1)
            pe.wait_ge(folds_ready, 1)
            pe.wait_ge(pads_zero, 5)

            def body(i):
                for s in range(2):
                    n = i * 2 + s
                    for k in range(CHUNKS):
                        need = min(BLOCKS - 1, (k * ROWS + ROWS - 1 + P11) // BROWS)
                        pe.wait_ge(taps_done, n * BLOCKS + (need + 1))
                        if not isinstance(n, int) or n * CHUNKS + k >= NPS:
                            pe.wait_ge(evacuated, n * CHUNKS + (k + 1 - NPS))
                        bank = mix[k % NPS]
                        r = k * ROWS
                        flat = lambda ap: ap.rearrange("c h w -> c (h w)")
                        for j in range(11):
                            pe.matmul(bank[:, :], fold11[:, j, :], flat(mid11[:, r + j:r + j + ROWS, :]), start=(j == 0), stop=False)
                        for j in range(5):
                            pe.matmul(bank[:, :], fold5[:, j, :], flat(mid5[:, r + j:r + j + ROWS, :]), start=False, stop=False)
                        pe.matmul(bank[:, :], w3T[:, :], flat(sum33[:, r:r + ROWS, :]), start=False, stop=True).then_inc(mixed, 1)
            each(pe, ROUNDS, body)

        @block.scalar
        def _(act):
            act.wait_ge(pads_zero, 5)

            def norm(i, s):
                act.wait_ge(x_loaded[s], (i + 1) * 16)
                n = i * 2 + s
                wait(act, taps_done, (n - 1) * BLOCKS)
                wait(act, gated, (n - 1) * CHUNKS)
                act.activation(interior(s), xin[:, s, :].rearrange("c (h w) -> c h w", w=W), ACT.Identity,
                               scale=sh.rstd[:, bass.ds(n, 1)], bias=sh.shift[:, bass.ds(n, 1)]).then_inc(normed[s], 1)

            def evacuate(i, s):
                n = i * 2 + s
                wait(act, stored[s], i * 16)
                wait(act, stats_done, (n - 1) * CHUNKS)
                for k in range(CHUNKS):
                    act.wait_ge(mixed, n * CHUNKS + (k + 1))
                    bank = mix[k % NPS]
                    act.activation(res[:, s, k * CHUNK:(k + 1) * CHUNK], bank[:, :], ACT.Identity,
                                   bias=mix_bias[:, :]).then_inc(evacuated, 1)

            norm(0, 0)
            norm(0, 1)
            act.wait_ge(mix_bias_ready, 1)
            evacuate(0, 0)
            with act.Fori(1, ROUNDS) as i:
                norm(i, 0)
                evacuate(i - 1, 1)
                norm(i, 1)
                evacuate(i, 0)
            evacuate(ROUNDS - 1, 1)

        @block.vector
        def _(dve):
            dve.wait_ge(weights_loaded, LOADS)
            setup = Chain(dve, setup_chain)
            setup.link(dve.tensor_tensor(bsum[:, :], biases[:, 0:1], biases[:, 2:3], ALU.add))
            dve.tensor_tensor(bsum[:, :], bsum[:, :], biases[:, 4:5], ALU.add).then_inc(w3T_ready, 1)
            dve.wait_ge(w3T_in_psum, 1)
            dve.tensor_copy(w3T[:, :], setup_ps[:, 0:C]).then_inc(w3T_ready, 1)
            dve.wait_ge(w3T_ready, 2)
            for t, taps, n in ((fold5, w51, 5), (fold11, w1111, 11)):
                for k in range(n):
                    last = dve.tensor_scalar(t[:, k, :], w3T[:, :], taps[:, k:k + 1], None, ALU.mult)
            last.then_inc(folds_ready, 1)
            dve.wait_ge(bias_in_psum, 1)
            dve.tensor_tensor(mix_bias[:, :], setup_ps[:, C:C + 1], biases[:, 5:6], ALU.add).then_inc(mix_bias_ready, 1)

            chain = Chain(dve, tap_chain, 2 * BLOCKS * 24)

            def taps(n, s):
                for blk in range(BLOCKS):
                    r = blk * BROWS
                    wait(dve, mixed, (n - 1) * CHUNKS + min(CHUNKS, (r + BROWS - 1 + P11) // ROWS + 1))
                    ended = [0, 0, 0]
                    sums = [(sum33[:, r:r + BROWS, :], None, [(w33[:, 3 * dy + dx:3 * dy + dx + 1],
                             xpad[:, s, r + dy:r + dy + BROWS, P11 - 1 + dx:P11 - 1 + dx + W]) for dy in range(3) for dx in range(3)]),
                            (mid5[:, P5 + r:P5 + r + BROWS, :], biases[:, 1:2], [(w15[:, k:k + 1],
                             xpad[:, s, 1 + r:1 + r + BROWS, P11 - P5 + k:P11 - P5 + k + W]) for k in range(5)]),
                            (mid11[:, P11 + r:P11 + r + BROWS, :], biases[:, 3:4], [(w111[:, k:k + 1],
                             xpad[:, s, 1 + r:1 + r + BROWS, k:k + W]) for k in range(11)])]
                    for j in range(11):
                        for q, (acc, bias, terms) in enumerate(sums):
                            if j >= len(terms):
                                continue
                            tap, src = terms[j]
                            if j == 0:
                                if bias is None:
                                    last = dve.tensor_scalar(acc, src, tap, None, ALU.mult)
                                else:
                                    last = dve.tensor_scalar(acc, src, tap, bias, ALU.mult, ALU.add)
                            else:
                                dve.wait_ge(tap_chain, chain.base + ended[q])
                                last = dve.scalar_tensor_tensor(acc, src, tap, acc, op0=ALU.mult, op1=ALU.add)
                            done = j == 10
                            if done:
                                last.then_inc(taps_done, 1)
                            else:
                                ended[q] = chain.step(last)

            def stats(n, s):
                for k in range(CHUNKS):
                    dve.wait_ge(res_ready, n * CHUNKS + (k + 1))
                    dve.bn_stats(sh.stats[:, bass.ds(n, 1), k, :].rearrange("c b s -> c (b s)"),
                                 res[:, s, k * CHUNK:(k + 1) * CHUNK]).then_inc(stats_done, 1)

            def batch(i, s):
                n = i * 2 + s
                dve.wait_ge(normed[s], i + 1)
                taps(n, s)

            chain.start(0)
            batch(0, 0)
            batch(0, 1)
            stats(0, 0)
            chain.end()
            with dve.Fori(1, ROUNDS) as i:
                chain.start(i)
                batch(i, 0)
                stats(i * 2 - 1, 1)
                batch(i, 1)
                stats(i * 2, 0)
                chain.end()
            stats(B - 1, 1)

def layer3(nc, sh, x_in, w_dirs, out):
    K, PAD = 9, 4
    HALVES, HB = 2, B // 2
    SWEEPS = [("rows", +1), ("rows", -1), ("cols", +1), ("cols", -1)]
    STEPS = [H - 1, H - 2, W - 1, W - 2]
    with ExitStack() as ctx:
        mem = Names(nc, ctx, "l3")
        state = mem.sbuf("state", [C, B, H, W])
        wraw = mem.sbuf("wraw", [C, C, K])
        taps = mem.sbuf("taps", [C, 4, K, C])
        xres = mem.sbuf("xres", [C, 2, HW // 2])
        conv = [mem.psum(f"conv{h}", [C, CHUNK]) for h in range(HALVES)]
        wt_ps = [mem.psum(f"wt{h}", [C, CHUNK]) for h in range(2)]

        x_loaded = [mem.sem(f"x_loaded{b}") for b in range(B)]
        w_loaded = mem.sem("w_loaded")
        wt_ready = mem.sem("wt_ready")
        wt_copied = mem.sem("wt_copied")
        conv_done = [mem.sem(f"conv_done{h}") for h in range(HALVES)]
        carry_ready = [mem.sem(f"carry_ready{h}") for h in range(HALVES)]
        res_loaded = [mem.sem(f"res_loaded{h}") for h in range(2)]
        out_ready = mem.sem("out_ready")
        stored = [mem.sem(f"stored{h}") for h in range(2)]

        def line(b0, nb, sweep, at, lo, n):
            if SWEEPS[sweep][0] == "rows":
                return state[:, b0:b0 + nb, bass.ds(at, 1), lo:lo + n].rearrange("c b o w -> c b (o w)")
            return state[:, b0:b0 + nb, lo:lo + n, bass.ds(at, 1)].rearrange("c b h o -> c b (h o)")

        block = ctx.enter_context(nc.Block())

        @block.sync
        def _(sp):
            for b in range(B):
                sp.dma_start(state[:, b, :, :].rearrange("c h w -> c (h w)"), x_in[b]).then_inc(x_loaded[b], 16)
                if b % 2 == 1:
                    s = b // 2
                    if s:
                        sp.wait_ge(wt_ready, 3 * s)
                    sp.dma_start(wraw[:, :, :], w_dirs[s]).then_inc(w_loaded, 16)
            for t in range(2 * B):
                b, half = t // 2, t % 2
                src = x_in[b][:, half * (HW // 2):(half + 1) * (HW // 2)]
                if t >= 2:
                    sp.wait_ge(stored[t % 2], 16 * (t // 2))
                sp.dma_start(xres[:, t % 2, :], src).then_inc(res_loaded[t % 2], 16)
                if t >= 1:
                    u = t - 1
                    sp.wait_ge(out_ready, u + 1)
                    sp.dma_start(out[u // 2][:, (u % 2) * (HW // 2):(u % 2 + 1) * (HW // 2)],
                                 xres[:, u % 2, :]).then_inc(stored[u % 2], 16)
            u = 2 * B - 1
            sp.wait_ge(out_ready, u + 1)
            sp.dma_start(out[u // 2][:, (u % 2) * (HW // 2):(u % 2 + 1) * (HW // 2)],
                         xres[:, u % 2, :]).then_inc(stored[u % 2], 16)
            sp.wait_ge(stored[0], 16 * B)
            sp.wait_ge(stored[1], 16 * B)

        @block.tensor
        def _(pe):
            n = 0
            for s in range(4):
                pe.wait_ge(w_loaded, 16 * (s + 1))
                for k0 in range(0, K, 4):
                    ks = range(k0, min(k0 + 4, K))
                    if n >= 2:
                        pe.wait_ge(wt_copied, n - 1)
                    for k in ks:
                        last = pe.transpose(wt_ps[n % 2][:, (k - k0) * C:(k - k0 + 1) * C], wraw[:, :, k], sh.ident[:, :])
                    last.then_inc(wt_ready, 1)
                    n += 1
            pe.wait_ge(wt_copied, n)
            order = [PAD] + [k for k in range(K) if k != PAD]
            done = 0
            for s, (axis, way) in enumerate(SWEEPS):
                with pe.Fori(0, STEPS[s]) as i:
                    at = i if way > 0 else i * -1 + (H - 1)
                    for h in range(HALVES):
                        pe.wait_ge(carry_ready[h], i + (done + 1))
                        for j, k in enumerate(order):
                            off = k - PAD
                            lo, ncol = max(0, -off), W - abs(off)
                            last = pe.matmul(conv[h][:, 0:HB * W].rearrange("c (b w) -> c b w", b=HB)[:, :, lo:lo + ncol],
                                             taps[:, s, k, :], line(h * HB, HB, s, at, lo + off, ncol),
                                             start=(j == 0), stop=(j == K - 1))
                        last.then_inc(conv_done[h], 1)
                done += STEPS[s]

        @block.scalar
        def _(act):
            n = 0
            for s in range(4):
                for k0 in range(0, K, 4):
                    nk = min(4, K - k0)
                    act.wait_ge(wt_ready, n + 1)
                    act.activation(taps[:, s, k0:k0 + nk, :].rearrange("c k o -> c (k o)"), wt_ps[n % 2][:, 0:nk * C],
                                   ACT.Copy).then_inc(wt_copied, 1)
                    n += 1

        @block.vector
        def _(dve):
            for b in range(B):
                flat = state[:, b, :, :].rearrange("c h w -> c (h w)")
                dve.wait_ge(x_loaded[b], 16)
                last = dve.tensor_scalar(flat, flat, sh.rstd[:, b:b + 1], sh.shift[:, b:b + 1], ALU.mult, ALU.add)
                if b % HB == HB - 1:
                    last.then_inc(carry_ready[b // HB], 1)
            done = 0
            for s, (axis, way) in enumerate(SWEEPS):
                with dve.Fori(0, STEPS[s]) as i:
                    at = i + 1 if way > 0 else i * -1 + (H - 2)
                    for h in range(HALVES):
                        dve.wait_ge(conv_done[h], i + (done + 1))
                        row = line(h * HB, HB, s, at, 0, W)
                        dve.scalar_tensor_tensor(row, conv[h][:, 0:HB * W].rearrange("c (b w) -> c b w", b=HB), 0.0,
                                                 row, op0=ALU.max, op1=ALU.add).then_inc(carry_ready[h], 1)
                done += STEPS[s]
            dve.wait_ge(carry_ready[0], done + 1)
            dve.wait_ge(carry_ready[1], done + 1)
            for t in range(2 * B):
                b, half = t // 2, t % 2
                flat = state[:, b, :, :].rearrange("c h w -> c (h w)")[:, half * (HW // 2):(half + 1) * (HW // 2)]
                dve.wait_ge(res_loaded[t % 2], 16 * (t // 2 + 1))
                dve.tensor_tensor(xres[:, t % 2, :], xres[:, t % 2, :], flat, ALU.add).then_inc(out_ready, 1)

def program(nc, x, table, w, out):
    SEMAPHORES_OF_PART.clear()
    mids = [nc.dram_tensor(f"after_layer{k}", (B, C, HW), FP32, kind="Internal").ap() for k in range(3)]
    of_layer = lambda k: {name[len("L0_conv_"):]: ap for name, ap in w.items() if name.startswith(f"L{k}_")}
    with ExitStack() as ctx:
        sh = Shared(nc, ctx)
        masks(nc, sh)
        input_stats(nc, sh, x)
        next_part(nc)
        group_scales(nc, sh, 0)
        next_part(nc)
        layer0(nc, sh, x, table, of_layer(0), mids[0])
        next_part(nc)
        group_scales(nc, sh, 1)
        next_part(nc)
        layer1(nc, sh, mids[0], of_layer(1), mids[1])
        next_part(nc)
        group_scales(nc, sh, 2)
        next_part(nc)
        layer2(nc, sh, mids[1], of_layer(2), mids[2])
        next_part(nc)
        group_scales(nc, sh, 3)
        nc.all_engine_barrier()
        w3 = of_layer(3)
        layer3(nc, sh, mids[2], [w3["w_d"], w3["w_u"], w3["w_r"], w3["w_l"]], out)


_SHAPES = {
    "L0_conv_w_dw": (GC, 25), "L0_conv_ln_w": (GC,), "L0_conv_w_off": (3, GC),
    "L0_conv_wq": (C, C), "L0_conv_wk": (C, C), "L0_conv_wv": (C, C), "L0_conv_wo": (C, C), "L0_conv_rpe": (HEADS, RPE, RPE),
    "L1_conv_gn_weight": (C,), "L1_conv_gn_bias": (C,), "L1_conv_w1": (2 * C, C), "L1_conv_b1": (2 * C,),
    "L1_conv_w2": (C, 2 * C), "L1_conv_b2": (C,),
    "L2_conv_w0": (C, 9), "L2_conv_b0": (C, 1), "L2_conv_w0_1": (C, 5), "L2_conv_b0_1": (C, 1), "L2_conv_w0_2": (C, 5),
    "L2_conv_b0_2": (C, 1), "L2_conv_w1_1": (C, 11), "L2_conv_b1_1": (C, 1), "L2_conv_w1_2": (C, 11), "L2_conv_b1_2": (C, 1),
    "L2_conv_w3": (C, C), "L2_conv_b3": (C, 1),
    "L3_conv_w_d": (C, C, 9), "L3_conv_w_u": (C, C, 9), "L3_conv_w_r": (C, C, 9), "L3_conv_w_l": (C, C, 9),
}


def kernel(**inputs):
    import concourse.bacc as _bacc
    from concourse.bass_utils import run_bass_kernel_spmd as _run

    nc = _bacc.Bacc("TRN2", target_bir_lowering=False, num_devices=1)
    arrays = {"x": np.ascontiguousarray(inputs["x"]).reshape(B, C, HW), "coordinates": constant_table()}
    for name, shape in _SHAPES.items():
        arrays[name] = np.ascontiguousarray(inputs[name]).reshape(shape)
    aps = {name: nc.dram_tensor(f"in_{name}", a.shape, mybir.dt.from_np(a.dtype), kind="ExternalInput").ap()
           for name, a in arrays.items()}
    out = nc.dram_tensor("out", (B, C, HW), FP32, kind="ExternalOutput").ap()
    program(nc, aps["x"], aps["coordinates"], {name: aps[name] for name in _SHAPES}, out)
    r = _run(nc, [{f"in_{name}": a for name, a in arrays.items()}], core_ids=[0])
    return r.results[0]["out"].reshape(B, C, H, W)
```

```python
import numpy as np
from contextlib import ExitStack
import concourse.bass as bass
from concourse import mybir

FP32 = mybir.dt.float32
FP32R = mybir.dt.float32r
ALU = mybir.AluOpType
ACT = mybir.ActivationFunctionType
AX = mybir.AxisListType
B, C, H, W = 8, 128, 64, 64
HW = H * W
GROUP = 4
GN_EPS = 1e-5
CHUNK = 512
CHUNKS = HW // CHUNK
ROWS = CHUNK // W


SEMAPHORES_OF_PART = []


def next_part(nc):
    nc.all_engine_barrier()
    nc.clear_and_free_semaphores(list(SEMAPHORES_OF_PART))
    SEMAPHORES_OF_PART.clear()
    nc.all_engine_barrier()


class Names:

    def __init__(self, nc, ctx, prefix):
        self.nc, self.ctx, self.prefix = nc, ctx, prefix

    def sbuf(self, name, shape, dtype=FP32):
        return self.ctx.enter_context(self.nc.sbuf_tensor(f"{self.prefix}_{name}", shape, dtype))

    def psum(self, name, shape=(C, CHUNK)):
        return self.ctx.enter_context(self.nc.psum_tensor(f"{self.prefix}_{name}", list(shape), FP32))

    def sem(self, name):
        taken = self.nc.alloc_semaphore(f"{self.prefix}_{name}")
        SEMAPHORES_OF_PART.append(taken)
        return taken


def wait(eng, sem, value):
    if not isinstance(value, int) or value > 0:
        eng.wait_ge(sem, value)


def each(eng, count, body):
    body(0)
    if count > 1:
        with eng.Fori(1, count) as i:
            body(i)


class Chain:

    def __init__(self, eng, sem, per_iteration=0):
        self.eng, self.sem, self.per, self.count, self.base = eng, sem, per_iteration, 0, 0

    def start(self, iteration):
        self.base, self.count = iteration * self.per, 0

    def step(self, ins):
        self.count += 1
        ins.then_inc(self.sem, 1)
        return self.count

    def link(self, ins):
        self.step(ins)
        self.eng.wait_ge(self.sem, self.base + self.count)

    def end(self):
        assert self.count == self.per, (self.count, self.per)


class Shared:

    def __init__(self, nc, ctx):
        mem = Names(nc, ctx, "all")
        self.ident = mem.sbuf("ident", [C, C])
        self.group_mean = mem.sbuf("group_mean", [C, C])
        self.stats = mem.sbuf("stats", [C, B, CHUNKS, 6])
        self.moments = mem.sbuf("moments", [C, B, 2])
        self.rstd = mem.sbuf("rstd", [C, B])
        self.shift = mem.sbuf("shift", [C, B])


def masks(nc, sh):
    with ExitStack() as ctx:
        mem = Names(nc, ctx, "masks")
        filled = mem.sem("filled")
        block = ctx.enter_context(nc.Block())

        @block.gpsimd
        def _(pool):
            pool.memset(sh.ident[:, :], 0.0).then_inc(filled, 1)
            pool.memset(sh.group_mean[:, :], 1.0 / GROUP).then_inc(filled, 1)
            pool.wait_ge(filled, 2)
            pool.affine_select(out=sh.ident[:, :], in_=sh.ident[:, :], compare_op=ALU.not_equal, fill=1.0,
                               base=0, pattern=[[-1, C]], channel_multiplier=1)
            pool.affine_select(out=sh.group_mean[:, :], in_=sh.group_mean[:, :], compare_op=ALU.is_ge, fill=0.0,
                               base=0, pattern=[[-GROUP, C // GROUP], [0, GROUP]], channel_multiplier=1).then_inc(filled, 1)
            pool.wait_ge(filled, 3)
            pool.affine_select(out=sh.group_mean[:, :], in_=sh.group_mean[:, :], compare_op=ALU.is_ge, fill=0.0,
                               base=GROUP - 1, pattern=[[GROUP, C // GROUP], [0, GROUP]], channel_multiplier=-1)


def input_stats(nc, sh, x_in):
    with ExitStack() as ctx:
        mem = Names(nc, ctx, "stat")
        xs = mem.sbuf("xs", [C, B, HW])
        loaded = [mem.sem(f"loaded{b}") for b in range(B)]
        block = ctx.enter_context(nc.Block())

        @block.sync
        def _(sp):
            for b in range(B):
                sp.dma_start(xs[:, b, :], x_in[b]).then_inc(loaded[b], 16)

        @block.vector
        def _(dve):
            for b in range(B):
                dve.wait_ge(loaded[b], 16)
                for j in range(CHUNKS):
                    dve.bn_stats(sh.stats[:, b, j, :], xs[:, b, j * CHUNK:(j + 1) * CHUNK])


def group_scales(nc, sh, layer):
    with ExitStack() as ctx:
        mem = Names(nc, ctx, f"gs{layer}")
        sq = mem.sbuf("sq", [C, B])
        gstat = mem.sbuf("gstat", [C, B, 2])
        stat_ps = mem.psum("stat_ps")
        chain_sem = mem.sem("chain")
        moments_ready = mem.sem("moments_ready")
        gstat_ready = mem.sem("gstat_ready")
        var_ready = mem.sem("var_ready")
        std_ready = mem.sem("std_ready")
        block = ctx.enter_context(nc.Block())

        @block.tensor
        def _(pe):
            pe.wait_ge(moments_ready, 1)
            pe.matmul(stat_ps[:, 0:2 * B], sh.group_mean[:, :], sh.moments[:, :, :].rearrange("c b t -> c (b t)"),
                      start=True, stop=True).then_inc(gstat_ready, 1)

        @block.scalar
        def _(act):
            act.wait_ge(var_ready, 1)
            act.activation(sh.rstd[:, :], sq[:, :], ACT.Sqrt).then_inc(std_ready, 1)

        @block.vector
        def _(dve):
            chain = Chain(dve, chain_sem)
            for b in range(B):
                last = dve.bn_aggr(sh.moments[:, b, :], sh.stats[:, b, :, :].rearrange("c j s -> c (j s)"))
            chain.link(last)
            chain.link(dve.tensor_tensor(sq[:, :], sh.moments[:, :, 0], sh.moments[:, :, 0], ALU.mult))
            dve.tensor_tensor(sh.moments[:, :, 1], sh.moments[:, :, 1], sq[:, :], ALU.add).then_inc(moments_ready, 1)
            dve.wait_ge(gstat_ready, 1)
            chain.link(dve.tensor_copy(gstat[:, :, :].rearrange("c b t -> c (b t)"), stat_ps[:, 0:2 * B]))
            chain.link(dve.tensor_tensor(sq[:, :], gstat[:, :, 0], gstat[:, :, 0], ALU.mult))
            chain.link(dve.tensor_tensor(sq[:, :], gstat[:, :, 1], sq[:, :], ALU.subtract))
            dve.tensor_scalar(sq[:, :], sq[:, :], GN_EPS, None, ALU.add).then_inc(var_ready, 1)
            dve.wait_ge(std_ready, 1)
            chain.link(dve.reciprocal(sh.rstd[:, :], sh.rstd[:, :]))
            dve.scalar_tensor_tensor(sh.shift[:, :], gstat[:, :, 0], -1.0, sh.rstd[:, :], op0=ALU.mult, op1=ALU.mult)

KH = KW = 16
KEYS = KH * KW
GROUPS, HEADS = 2, 4
GC, DH = C // GROUPS, C // HEADS
GROUP_HEADS = HEADS // GROUPS
SCALE = float(DH) ** -0.5
RPE = 2 * H - 1
TILE_ROWS, WINDOW = 2, 4
HALF = (H - 1) / 2.0
T_GRID, T_REF, T_ROW, T_NEGCOL, T_ONE, T_MEAN, T_END = np.cumsum([0, W, KH, WINDOW * KH, 1, 1, C]).tolist()


def first_tile(ky):
    return min(H // TILE_ROWS - WINDOW, int(ky * (H - 1) / KH) // TILE_ROWS)


def constant_table():
    t = np.zeros((C, T_END), np.float64)
    p = np.arange(C)
    query = (np.arange(H) + 0.5) / H * 2 - 1
    key = ((np.arange(KH) + 0.5) / KH * 2 - 1) * HALF
    t[:, T_GRID:T_REF] = query[None, :] * HALF + (RPE - 1) / 2.0 - p[:, None]
    t[:, T_REF:T_ROW] = key[None, :]
    rows = np.array([[TILE_ROWS * (first_tile(k) + s) for k in range(KH)] for s in range(WINDOW)]).reshape(-1)
    t[:, T_ROW:T_NEGCOL] = rows[None, :] + (p // W)[:, None] - HALF
    t[:, T_NEGCOL] = HALF - p % W
    t[:, T_ONE] = 1.0
    t[:, T_MEAN:T_END] = (p[:, None] // GC == p[None, :] // GC) / float(GC)
    return t.astype(np.float32)


def layer0(nc, sh, x_in, table_in, w, out):
    OCT = 8
    OCTS = W // OCT
    HAT_SLOTS = 4
    PAIR = C // W
    with ExitStack() as ctx:
        mem = Names(nc, ctx, "l0")
        table = mem.sbuf("table", [C, T_END])
        wqT = mem.sbuf("wqT", [C, C])
        wkT = mem.sbuf("wkT", [C, C])
        wvo = mem.sbuf("wvo", [C, HEADS, C])
        woff = mem.sbuf("woff", [C, 3, C])
        wdw = mem.sbuf("wdw", [C, 25])
        lnw = mem.sbuf("lnw", [C, 1])
        rpe = mem.sbuf("rpe", [C, HEADS, C])
        xraw = mem.sbuf("xraw", [C, HW])
        q = mem.sbuf("q", [C, HW])
        bias = mem.sbuf("bias", [C, KEYS, W])
        hats = mem.sbuf("hats", [C, 2, 2, KW * W])
        xn = hats[:, :, :, :].rearrange("c u a n -> c (u a n)")
        rows_T = mem.sbuf("rows_T", [C, 2, KW, C])
        xT = mem.sbuf("xT", [C, H // TILE_ROWS, C])
        probs = mem.sbuf("probs", [C, 2, OCT, KEYS])
        samplers = probs[:, 0, :, :].rearrange("c j n -> c (j n)").rearrange("c (t m) -> c t m", t=WINDOW)
        probsT = mem.sbuf("probsT", [C, 2, 2, GROUP_HEADS, OCT, H])
        hat_slots = [hats[:, 0, :, :], hats[:, 1, :, :],
                     probs[:, 1, :, :].rearrange("c j n -> c (j n)").rearrange("c (a n) -> c a n", a=2),
                     probsT[:, 0, :, :, :, :].rearrange("c t h j i -> c (t h j i)").rearrange("c (a n) -> c a n", a=2)]
        qd = mem.sbuf("qd", [C, 2, OCT, GROUP_HEADS, H])
        spare = probsT[:, 1, :, :, :, :].rearrange("c t h j i -> c (t h j i)").rearrange("c (k n) -> c k n", n=KEYS)
        off, cen, gel, xs = (spare[:, k, :] for k in range(4))
        gate = spare[:, 4:6, :].rearrange("c k n -> c (k n)")
        hat_x = spare[:, 6:8, :].rearrange("c a n -> c (a n)").rearrange("c (k g x) -> c k g x", g=GROUPS, x=KW)
        place = mem.sbuf("place", [C, GROUPS, 2, KEYS])
        keys = mem.sbuf("keys", [C, KEYS])
        vals = mem.sbuf("vals", [C, 2, HEADS * C])
        shift = mem.sbuf("shift", [C, 2, OCT])
        sums = mem.sbuf("sums", [C, 2, OCT])
        inv = mem.sbuf("inv", [C, 2, OCT])
        bank = [mem.psum(f"bank{k}") for k in range(8)]
        grid = table[:, T_GRID:T_REF]
        ref = table[:, T_REF:T_ROW]
        one = table[:, T_ONE:T_MEAN]

        with ExitStack() as sctx:
            smem = Names(nc, sctx, "l0s")
            raw = xraw[:, 0:4 * C].rearrange("c (k n) -> c k n", k=4)
            wvz = xraw[:, 4 * C:(4 + HEADS) * C].rearrange("c (k n) -> c k n", k=HEADS)
            woT = xraw[:, 2048:2048 + C]
            offc = smem.sbuf("offc", [C, 3])
            loaded = smem.sem("loaded")
            zeroed = smem.sem("zeroed")
            turned = smem.sem("turned")
            copied = smem.sem("copied")
            product = smem.sem("product")
            block = sctx.enter_context(nc.Block())
            col = lambda ap: ap.rearrange("(o a) -> o a", a=1)

            @block.sync
            def _(sp):
                n = 0
                for k, name in enumerate(("wq", "wk", "wv", "wo")):
                    sp.dma_start(raw[:, k, :], w[name]).then_inc(loaded, 16)
                sp.dma_start(table[:, :], table_in).then_inc(loaded, 16)
                for g in range(GROUPS):
                    rows = slice(GC * g, GC * (g + 1))
                    sp.dma_start(wdw[rows, :], w["w_dw"]).then_inc(loaded, 16)
                    sp.dma_start(lnw[rows, :], col(w["ln_w"])).then_inc(loaded, 16)
                    for k in range(3):
                        sp.dma_start(offc[rows, k:k + 1], col(w["w_off"][k])).then_inc(loaded, 16)
                sp.wait_ge(zeroed, 1)
                sp.dma_start(rpe[0:RPE, :, 0:RPE], w["rpe"].rearrange("h y x -> y h x")).then_inc(loaded, 16)
                sp.wait_ge(loaded, 16 * 16)

            @block.gpsimd
            def _(pool):
                pool.memset(rpe[:, :, :], 0.0).then_inc(zeroed, 1)
                pool.memset(qd[:, :, :, :, :], 0.0).then_inc(zeroed, 1)
                pool.memset(wvz, 0.0).then_inc(zeroed, 1)

            @block.tensor
            def _(pe):
                pe.wait_ge(loaded, 16 * 16)
                for k, m in enumerate((0, 1, 3)):
                    pe.transpose(bank[k][:, 0:C], raw[:, m, :], sh.ident[:, :]).then_inc(turned, 1)
                pe.wait_ge(copied, 1)
                for h in range(HEADS):
                    pe.matmul(bank[3][:, h * C:(h + 1) * C], wvz[:, h, :], woT, start=True, stop=True).then_inc(product, 1)

            @block.vector
            def _(dve):
                dve.wait_ge(zeroed, 3)
                dve.wait_ge(loaded, 16 * 16)
                for h in range(HEADS):
                    rows = slice(DH * h, DH * (h + 1))
                    dve.tensor_copy(wvz[rows, h, :], raw[rows, 2, :])
                dve.tensor_copy(woff[:, :, :], offc[:, :].rearrange("c (k o) -> c k o", o=1).to_broadcast([C, 3, C]))
                dve.tensor_scalar(rpe[:, :, :], rpe[:, :, :], -1.0, None, ALU.mult)
                dve.wait_ge(turned, 3)
                dve.tensor_copy(wqT[:, :], bank[0][:, 0:C])
                dve.tensor_scalar(wkT[:, :], bank[1][:, 0:C], -SCALE, None, ALU.mult)
                dve.tensor_copy(woT, bank[2][:, 0:C]).then_inc(copied, 1)
                dve.wait_ge(product, HEADS)
                dve.tensor_copy(wvo[:, :, :].rearrange("c h o -> c (h o)"), bank[3][:, :])

        waits_met = mem.sem("waits_met")
        xn_loaded = mem.sem("xn_loaded")
        xraw_loaded = mem.sem("xraw_loaded")
        stored = mem.sem("stored")
        normed = mem.sem("normed")
        q_in_psum = mem.sem("q_in_psum")
        q_by_dve = mem.sem("q_by_dve")
        q_by_act = mem.sem("q_by_act")
        xT_in_psum = mem.sem("xT_in_psum")
        xT_by_dve = mem.sem("xT_by_dve")
        xT_by_act = mem.sem("xT_by_act")
        conv_chain = mem.sem("conv_chain")
        mean_ready = mem.sem("mean_ready")
        sq_ready = mem.sem("sq_ready")
        var_ready = mem.sem("var_ready")
        std_ready = mem.sem("std_ready")
        scaled = mem.sem("scaled")
        gelu_ready = mem.sem("gelu_ready")
        offs_in_psum = mem.sem("offs_in_psum")
        tanh_done = mem.sem("tanh_done")
        place_ready = mem.sem("place_ready")
        dist_ready = mem.sem("dist_ready")
        abs_prelude = mem.sem("abs_prelude")
        hats_prelude = mem.sem("hats_prelude")
        samplers_ready = mem.sem("samplers_ready")
        var_chain = mem.sem("var_chain")
        xs_in_psum = mem.sem("xs_in_psum")
        xs_ready = mem.sem("xs_ready")
        kv_in_psum = mem.sem("kv_in_psum")
        k_ready = mem.sem("k_ready")
        v_ready = mem.sem("v_ready")
        conv_done = mem.sem("conv_done")
        sq_made = mem.sem("sq_made")
        subtracted = mem.sem("subtracted")
        abs_done = mem.sem("abs_done")
        hats_ready = mem.sem("hats_ready")
        s1_done = mem.sem("s1_done")
        t_copied = mem.sem("t_copied")
        s2_half = mem.sem("s2_half")
        b_copied = mem.sem("b_copied")
        qd_ready = mem.sem("qd_ready")
        qd_chain = mem.sem("qd_chain")
        l_in_psum = mem.sem("l_in_psum")
        added = mem.sem("added")
        min_ready = mem.sem("min_ready")
        exp_done = mem.sem("exp_done")
        inv_ready = mem.sem("inv_ready")
        scaled_by_pool = mem.sem("scaled_by_pool")
        scaled_by_act = mem.sem("scaled_by_act")
        pt_in_psum = mem.sem("pt_in_psum")
        pt_by_dve = mem.sem("pt_by_dve")
        pt_by_act = mem.sem("pt_by_act")
        av_done = mem.sem("av_done")
        acc_done = mem.sem("acc_done")
        stats_done = mem.sem("stats_done")
        CONV_STEPS = 26
        block = ctx.enter_context(nc.Block())

        def gated(eng, s, value):
            eng.wait_ge(s, value)
            eng.sem_inc(waits_met, 1)

        def batches(eng, body):
            with eng.Fori(0, B) as b:
                body(b)

        def pipelined(eng, count, slots, ahead, behind, late=lambda: None):
            ahead(0, 0)
            with eng.Fori(0, count // slots - 1) as kk:
                for u in range(slots):
                    ahead(kk * slots + (u + 1), (u + 1) % slots)
                    behind(kk * slots + u, u)
            for k in range(count - slots, count):
                if k + 1 < count:
                    ahead(k + 1, (k + 1) % slots)
                if k + 1 == count:
                    late()
                behind(k, k % slots)

        def octets(eng, step):
            step(0, 0, former=False)
            with eng.Fori(0, OCTS // 2 - 1) as oo:
                for u in range(2):
                    step(oo * 2 + (u + 1), 1 - u)
            step(OCTS - 1, 1, more=False)

        def bias_step(b, g, ky):
            return b * (2 * KH) + (ky + g * KH)

        def octet_step(b, g, o):
            return b * (2 * OCTS) + (o + g * OCTS)

        @block.sync
        def _(sp):
            def batch(ap, b):
                return ap[bass.ds(b, 1)].rearrange("b c n -> (b c) n")

            def load_xn(b):
                gated(sp, s2_half, b * (4 * KH) + 2 * HAT_SLOTS)
                sp.dma_start(xn, batch(x_in, b)).then_inc(xn_loaded, 16)

            def load_xraw(b):
                sp.dma_start(xraw[:, :], batch(x_in, b)).then_inc(xraw_loaded, 16)

            def store(b):
                gated(sp, stats_done, (b + 1) * CHUNKS)
                sp.dma_start(batch(out, b), xraw[:, :]).then_inc(stored, 16)
            load_xn(0)
            load_xraw(0)
            with sp.Fori(0, B - 1) as b:
                load_xn(b + 1)
                store(b)
                gated(sp, stored, (b + 1) * 16)
                load_xraw(b + 1)
            store(B - 1)
            sp.wait_ge(stored, 16 * B)

        @block.gpsimd
        def _(pool):
            def body(b):
                def subtract(g, ky, u):
                    a = bias_step(b, g, ky)
                    if u == 2:
                        pool.wait_ge(pt_in_psum, octet_step(b, g, 0) * 4 + 8)
                        pool.wait_ge(av_done, octet_step(b, g, 0) + 1)
                    gated(pool, s2_half, a * 2 + 2)
                    pool.tensor_tensor(hat_slots[u].rearrange("c a (n i) -> c a n i", i=W),
                                       grid.rearrange("c (a n i) -> c a n i", a=1, n=1).to_broadcast([C, 2, KW, W]),
                                       place[:, g, :, bass.ds(ky * KW, KW)].rearrange("c a (n o) -> c a n o", o=1).to_broadcast([C, 2, KW, W]),
                                       ALU.subtract).then_inc(subtracted, 1)

                def spread(g, o, u):
                    e = octet_step(b, g, o)
                    pool.wait_ge(l_in_psum, e * 4 + 4)
                    pool.wait_ge(subtracted, bias_step(b, g, KH))
                    pool.wait_ge(scaled_by_pool, e + 1)
                    for h in range(GROUP_HEADS):
                        rows = slice(GC * g + DH * h, GC * g + DH * (h + 1))
                        gated(pool, qd_chain, e * 2 + (h + 1))
                        pool.tensor_copy(qd[rows, u, :, h, :],
                                         q[rows, :].rearrange("c (i j) -> c j i", j=W)[:, bass.ds(o * OCT, OCT), :]).then_inc(qd_chain, 1)
                    pool.wait_ge(qd_chain, e * 2 + 3)
                    pool.sem_inc(qd_ready, 1)

                def scale(g, o, u):
                    e = octet_step(b, g, o)
                    pool.wait_ge(inv_ready, e * 2 + 1)
                    half = probs[:, u, 0:OCT // 2, :]
                    pool.tensor_tensor(half, half, inv[:, u, 0:OCT // 2].rearrange("c (j o) -> c j o", o=1).to_broadcast([C, OCT // 2, KEYS]),
                                       ALU.mult).then_inc(scaled_by_pool, 1)

                gated(pool, place_ready, (b + 1) * 5)
                for g in range(GROUPS):
                    with pool.Fori(0, KH // HAT_SLOTS) as kk:
                        for u in range(HAT_SLOTS):
                            subtract(g, kk * HAT_SLOTS + u, u)
                    pipelined(pool, OCTS, 2, lambda o, u: spread(g, o, u), lambda o, u: scale(g, o, u))
            pool.sem_inc(qd_chain, 1)
            pool.sem_inc(scaled_by_pool, 2)
            batches(pool, body)

        @block.tensor
        def _(pe):
            def body(b):
                pe.wait_ge(acc_done, b * (2 * OCTS) + 2)
                for k in range(CHUNKS):
                    pe.wait_ge(normed, b * CHUNKS + (k + 1))
                    pe.matmul(bank[k][:, :], wqT[:, :], xn[:, k * CHUNK:(k + 1) * CHUNK], start=True, stop=True).then_inc(q_in_psum, 1)
                for k in range(CHUNKS):
                    pe.wait_ge(q_by_act if k % 2 else q_by_dve, b * 4 + (k // 2 + 1))
                    for t in range(4):
                        last = pe.transpose(bank[k][:, t * C:(t + 1) * C], xn[:, (4 * k + t) * C:(4 * k + t + 1) * C], sh.ident[:, :])
                    last.then_inc(xT_in_psum, 1)
                mask = table[:, T_MEAN:T_END]
                pe.wait_ge(xT_by_dve, (b + 1) * 4)
                pe.wait_ge(xT_by_act, (b + 1) * 4)
                pe.wait_ge(conv_done, b + 1)
                pe.matmul(bank[0][:, 0:KEYS], mask, off, start=True, stop=True).then_inc(mean_ready, 1)
                pe.wait_ge(sq_made, b + 1)
                pe.matmul(bank[1][:, 0:KEYS], mask, gel, start=True, stop=True).then_inc(sq_ready, 1)
                pe.wait_ge(gelu_ready, b + 1)
                for g in range(GROUPS):
                    for k in range(3):
                        target = bank[2 + g][:, k * KEYS:(k + 1) * KEYS] if k < 2 else bank[4 + 2 * g][:, 0:KEYS]
                        last = pe.matmul(target, woff[GC * g:GC * (g + 1), k, :], gel[GC * g:GC * (g + 1), :], start=True, stop=True)
                last.then_inc(offs_in_psum, 1)
                def rows1(g, ky, u):
                    a = bias_step(b, g, ky)
                    pe.wait_ge(hats_ready, a + 1)
                    for r in range(4):
                        h, half = r // 2, r % 2
                        pe.wait_ge(t_copied, a * 4 + (r + 1))
                        pe.matmul(bank[r][:, :], rpe[:, GROUP_HEADS * g + h, :], hat_slots[u][:, 0, half * CHUNK:(half + 1) * CHUNK],
                                  start=True, stop=True).then_inc(s1_done, 1)

                def cols2(g, ky, u):
                    a = bias_step(b, g, ky)
                    pe.wait_ge(t_copied, a * 4 + 8)
                    for half in range(2):
                        pe.wait_ge(b_copied, a * 2 + (half + 1))
                        for n in range(8):
                            k = half * 8 + n
                            last = pe.matmul(bank[4 + half][:, n * W:(n + 1) * W], rows_T[:, u % 2, k, :], hat_slots[u][:, 1, k * W:(k + 1) * W],
                                             start=True, stop=True)
                        last.then_inc(s2_half, 1)

                def logits(g, o, u, half):
                    e = octet_step(b, g, o)
                    rows = slice(GC * g, GC * (g + 1))
                    if half == 0:
                        pe.wait_ge(qd_ready, e + 1)
                    for p in (2 * half, 2 * half + 1):
                        pe.wait_ge(added, e * 4 + (p + 1))
                        for j in (2 * p, 2 * p + 1):
                            last = pe.matmul(bank[p % 2][:, (j % 2) * KEYS:(j % 2 + 1) * KEYS], qd[rows, u, j, :, :].rearrange("c h i -> c (h i)"),
                                             keys[rows, :], start=True, stop=True)
                        last.then_inc(l_in_psum, 1)

                def turn(g, o, u, half):
                    e = octet_step(b, g, o)
                    pe.wait_ge(scaled_by_act if half else scaled_by_pool, e + 3)
                    for t in range(2):
                        pe.wait_ge(pt_by_act if t else pt_by_dve, e * 2 + (half + 1))
                        for jj in range(4):
                            j = half * 4 + jj
                            last = pe.transpose(bank[2 + t][:, jj * C:(jj + 1) * C], probs[:, u, j, t * C:(t + 1) * C], sh.ident[:, :])
                        last.then_inc(pt_in_psum, 1)

                def attend(g, o, u):
                    e = octet_step(b, g, o)
                    pe.wait_ge(pt_by_dve, e * 2 + 3)
                    pe.wait_ge(pt_by_act, e * 2 + 3)
                    pe.wait_ge(acc_done, e + 1)
                    for h in range(GROUP_HEADS):
                        for t in range(2):
                            last = pe.matmul(bank[4 + u][:, :], vals[:, t, (GROUP_HEADS * g + h) * C:(GROUP_HEADS * g + h + 1) * C],
                                             probsT[:, u, t, h, :, :].rearrange("c j i -> c (j i)"),
                                             start=(h == 0 and t == 0), stop=(h == GROUP_HEADS - 1 and t == 1))
                    last.then_inc(av_done, 1)

                def sample():
                    pe.wait_ge(samplers_ready, b + 1)
                    for ky in range(KH):
                        for t in range(WINDOW):
                            last = pe.matmul(bank[6][:, ky * 32:(ky + 1) * 32], xT[:, first_tile(ky) + t, :], samplers[:, t, ky * 32:(ky + 1) * 32],
                                             start=(t == 0), stop=(t == WINDOW - 1))
                    last.then_inc(xs_in_psum, 1)
                    pe.wait_ge(xs_ready, 2 * (b + 1))
                    pe.matmul(bank[7][:, 0:KEYS], wkT[:, :], xs, start=True, stop=True).then_inc(kv_in_psum, 1)
                    for t in range(2):
                        pe.matmul(bank[t][:, :], xs[:, t * C:(t + 1) * C], wvo[:, :, :].rearrange("c h o -> c (h o)"),
                                  start=True, stop=True).then_inc(kv_in_psum, 1)
                    pe.wait_ge(k_ready, b + 1)
                    pe.wait_ge(v_ready, 2 * (b + 1))

                for g in range(GROUPS):
                    pe.wait_ge(acc_done, b * (2 * OCTS) + (g * OCTS + 2))
                    pipelined(pe, KH, HAT_SLOTS, lambda ky, u: rows1(g, ky, u), lambda ky, u: cols2(g, ky, u))
                    if g == 0:
                        sample()
                    pe.wait_ge(b_copied, bias_step(b, g, KH - 1) * 2 + 4)
                    for half in range(2):
                        logits(g, 0, 0, half)

                    def step(o, u, more=True, former=True):
                        for half in range(2):
                            if more:
                                logits(g, o + 1, 1 - u, half)
                            if half == 0 and former:
                                attend(g, o - 1, 1 - u)
                            turn(g, o, u, half)
                    octets(pe, step)
                    attend(g, OCTS - 1, 1)
            pe.sem_inc(s2_half, 2 * HAT_SLOTS)
            pe.sem_inc(av_done, 1)
            pe.sem_inc(l_in_psum, 8)
            pe.sem_inc(pt_in_psum, 8)
            batches(pe, body)

        @block.scalar
        def _(act):
            def body(b):
                gated(act, xn_loaded, (b + 1) * 16)
                for k in range(CHUNKS):
                    part = slice(k * CHUNK, (k + 1) * CHUNK)
                    act.activation(xn[:, part], xn[:, part], ACT.Identity, scale=sh.rstd[:, bass.ds(b, 1)],
                                   bias=sh.shift[:, bass.ds(b, 1)]).then_inc(normed, 1)
                for k in range(1, CHUNKS, 2):
                    act.wait_ge(q_in_psum, b * CHUNKS + (k + 1))
                    act.activation(q[:, k * CHUNK:(k + 1) * CHUNK], bank[k][:, :], ACT.Copy).then_inc(q_by_act, 1)
                for k in range(1, CHUNKS, 2):
                    act.wait_ge(xT_in_psum, b * CHUNKS + (k + 1))
                    act.activation(xT[:, 4 * k:4 * k + 4, :].rearrange("c t n -> c (t n)"), bank[k][:, :], ACT.Copy).then_inc(xT_by_act, 1)
                act.wait_ge(var_ready, b + 1)
                act.activation(cen, gel, ACT.Sqrt).then_inc(std_ready, 1)
                act.wait_ge(scaled, b + 1)
                act.activation(gel, off, ACT.Gelu, scale=lnw[:, 0:1]).then_inc(gelu_ready, 1)
                act.wait_ge(offs_in_psum, b + 1)
                for g in range(GROUPS):
                    act.activation(place[:, g, :, :].rearrange("c a n -> c (a n)"), bank[2 + g][:, :], ACT.Tanh).then_inc(tanh_done, 1)
                for g in range(GROUPS):
                    act.activation(gate[:, g * KEYS:(g + 1) * KEYS], bank[4 + 2 * g][:, 0:KEYS], ACT.Tanh, scale=0.5).then_inc(tanh_done, 1)
                def copy_values():
                    for t in range(2):
                        act.wait_ge(kv_in_psum, b * 3 + (t + 2))
                        act.activation(vals[:, t, :], bank[t][:, :], ACT.Copy).then_inc(v_ready, 1)

                def distance(g, ky, u):
                    act.wait_ge(subtracted, bias_step(b, g, ky) + 1)
                    act.activation(hat_slots[u], hat_slots[u], ACT.Abs).then_inc(abs_done, 1)

                def hat(g, ky, u):
                    act.wait_ge(abs_done, bias_step(b, g, ky) + 1)
                    act.activation(hat_slots[u], hat_slots[u], ACT.Relu, scale=-1.0, bias=one).then_inc(hats_ready, 1)

                def exps(g, o, u, half):
                    e = octet_step(b, g, o)
                    act.wait_ge(min_ready, e * 2 + (half + 1))
                    for j in range(4 * half, 4 * half + 4):
                        act.activation(probs[:, u, j, :], probs[:, u, j, :], ACT.Exp, scale=-1.0, bias=shift[:, u, j:j + 1],
                                       accum_out=sums[:, u, j:j + 1]).then_inc(exp_done, 1)

                def scale(g, o, u):
                    e = octet_step(b, g, o)
                    act.wait_ge(inv_ready, e * 2 + 2)
                    for j in range(OCT // 2, OCT):
                        last = act.activation(probs[:, u, j, :], probs[:, u, j, :], ACT.Copy, scale=inv[:, u, j:j + 1])
                    last.then_inc(scaled_by_act, 1)

                def copy(g, o, u, half):
                    e = octet_step(b, g, o)
                    act.wait_ge(pt_in_psum, e * 4 + (2 * half + 10))
                    act.activation(probsT[:, u, 1, :, half * 4:half * 4 + 4, :], bank[3][:, :].rearrange("c (j h i) -> c h j i", j=4, h=GROUP_HEADS),
                                   ACT.Copy).then_inc(pt_by_act, 1)

                def sampling_hats():
                    by_key = lambda ap: ap.rearrange("c k g x -> c g k x")
                    act.wait_ge(place_ready, b * 5 + 5)
                    act.activation(by_key(hat_x), place[:, :, 1, :].rearrange("c g (k x) -> c g k x", x=KW), ACT.Abs,
                                   bias=table[:, T_NEGCOL:T_ONE]).then_inc(abs_prelude, 1)
                    act.wait_ge(dist_ready, b * WINDOW + WINDOW)
                    act.activation(samplers, samplers, ACT.Abs).then_inc(abs_prelude, 1)
                    act.wait_ge(abs_prelude, b * 2 + 2)
                    act.activation(hat_x, hat_x, ACT.Relu, scale=-1.0, bias=one).then_inc(hats_prelude, 1)
                    act.activation(samplers, samplers, ACT.Relu, scale=-1.0, bias=one).then_inc(hats_prelude, 1)

                for g in range(GROUPS):
                    def hats_of(k):
                        for u in range(HAT_SLOTS):
                            distance(g, k * HAT_SLOTS + u, u)
                            hat(g, k * HAT_SLOTS + u, u)
                    hats_of(0)
                    if g == 0:
                        sampling_hats()
                    with act.Fori(1, KH // HAT_SLOTS) as k:
                        hats_of(k)
                    if g == 0:
                        copy_values()
                    for half in range(2):
                        exps(g, 0, 0, half)

                    def step(o, u, more=True, former=True):
                        scale(g, o, u)
                        for half in range(2):
                            copy(g, o, u, half)
                            if more:
                                exps(g, o + 1, 1 - u, half)
                    octets(act, step)
            act.sem_inc(pt_by_act, 1)
            act.sem_inc(scaled_by_act, 2)
            batches(act, body)

        @block.vector
        def _(dve):
            def body(b):
                for k in range(0, CHUNKS, 2):
                    dve.wait_ge(q_in_psum, b * CHUNKS + (k + 1))
                    dve.tensor_copy(q[:, k * CHUNK:(k + 1) * CHUNK], bank[k][:, :]).then_inc(q_by_dve, 1)
                for k in range(0, CHUNKS, 2):
                    dve.wait_ge(xT_in_psum, b * CHUNKS + (k + 1))
                    dve.tensor_copy(xT[:, 4 * k:4 * k + 4, :].rearrange("c t n -> c (t n)"), bank[k][:, :]).then_inc(xT_by_dve, 1)
                dve.wait_ge(q_by_act, b * 4 + 4)
                dve.wait_ge(q_by_dve, b * 4 + 4)
                image = q[:, :].rearrange("c (y x) -> c y x", x=W)
                sums_of_taps = [ap.rearrange("c (y x) -> c y x", x=KW) for ap in (off, cen)]
                taps = [(2, 2), (2, 3)] + [(y, x) for y in range(5) for x in range(5) if (y, x) not in ((2, 2), (2, 3))]
                for n, (y, x) in enumerate(taps):
                    y0, x0 = int(y < 2), int(x < 2)
                    src = image[:, 4 * y0 + y - 2:H - 5 + y:4, 4 * x0 + x - 2:W - 5 + x:4]
                    tap = wdw[:, 5 * y + x:5 * y + x + 1]
                    if n < 2:
                        dve.tensor_scalar(sums_of_taps[n], src, tap, None, ALU.mult).then_inc(conv_chain, 1)
                    else:
                        dst = sums_of_taps[n % 2][:, y0:, x0:]
                        dve.wait_ge(conv_chain, b * CONV_STEPS + (n - 1))
                        dve.scalar_tensor_tensor(dst, src, tap, dst, op0=ALU.mult, op1=ALU.add).then_inc(conv_chain, 1)
                dve.wait_ge(conv_chain, b * CONV_STEPS + 25)
                dve.tensor_tensor(off, off, cen, ALU.add).then_inc(conv_chain, 1)
                dve.wait_ge(conv_chain, b * CONV_STEPS + 26)
                dve.sem_inc(conv_done, 1)
                dve.wait_ge(mean_ready, b + 1)
                dve.tensor_tensor(cen, off, bank[0][:, 0:KEYS], ALU.subtract).then_inc(var_chain, 1)
                dve.wait_ge(var_chain, b * 2 + 1)
                dve.tensor_tensor(gel, cen, cen, ALU.mult).then_inc(sq_made, 1)
                dve.wait_ge(sq_ready, b + 1)
                dve.tensor_scalar(gel, bank[1][:, 0:KEYS], GN_EPS, None, ALU.add).then_inc(var_ready, 1)
                dve.wait_ge(std_ready, b + 1)
                dve.reciprocal(cen, cen).then_inc(var_chain, 1)
                dve.wait_ge(var_chain, b * 2 + 2)
                dve.tensor_tensor(off, off, cen, ALU.mult).then_inc(scaled, 1)
                for g in range(GROUPS):
                    dve.wait_ge(tanh_done, b * 4 + (g + 1))
                    for axis in range(2):
                        p = place[:, g, axis, :].rearrange("c (k x) -> c k x", x=KW)
                        at = ref.rearrange("c (k o) -> c k o", o=1) if axis == 0 else ref.rearrange("c (o k) -> c o k", o=1)
                        dve.scalar_tensor_tensor(p, p, HALF / KH, at.to_broadcast([C, KH, KW]), op0=ALU.mult, op1=ALU.add).then_inc(place_ready, 1)
                dve.wait_ge(tanh_done, b * 4 + 4)
                dve.tensor_scalar(gate, gate, 0.5, 0.5, ALU.mult, ALU.add).then_inc(place_ready, 1)
                dve.wait_ge(place_ready, b * 5 + 5)
                for t in range(WINDOW):
                    dve.tensor_tensor(samplers[:, t, :].rearrange("c (k g x) -> c g k x", g=GROUPS, x=KW),
                                      place[:, :, 0, :].rearrange("c g (k x) -> c g k x", x=KW),
                                      table[:, T_ROW + t * KH:T_ROW + (t + 1) * KH].rearrange("c (g k x) -> c g k x", g=1, x=1).to_broadcast([C, GROUPS, KH, KW]),
                                      ALU.subtract).then_inc(dist_ready, 1)
                def sampling_weights():
                    dve.wait_ge(hats_prelude, b * 2 + 2)
                    dve.tensor_tensor(samplers, samplers, hat_x.rearrange("c k g x -> c (k g x)").rearrange("c (t m) -> c t m", t=1).to_broadcast([C, WINDOW, 2 * KEYS]),
                                      ALU.mult).then_inc(samplers_ready, 1)

                def copy_rows(g, ky, u):
                    a = bias_step(b, g, ky)
                    for r in range(4):
                        h, half = r // 2, r % 2
                        dve.wait_ge(s1_done, a * 4 + (r + 1))
                        dve.tensor_copy(rows_T[:, u, half * 8:half * 8 + 8, h * H:(h + 1) * H],
                                        bank[r][:, :].rearrange("c (n i) -> c n i", i=H)).then_inc(t_copied, 1)

                def copy_bias(g, ky, u):
                    a = bias_step(b, g, ky)
                    for half in range(2):
                        dve.wait_ge(s2_half, a * 2 + (half + 1 + 2 * HAT_SLOTS))
                        dve.tensor_copy(bias[:, bass.ds(ky * KW + half * 8, 8), :], bank[4 + half][:, :].rearrange("c (n j) -> c n j", j=W)).then_inc(b_copied, 1)

                def add_bias(g, o, u, half):
                    e = octet_step(b, g, o)
                    if half == 0:
                        dve.wait_ge(pt_in_psum, e * 4 + 4)
                    for p in (2 * half, 2 * half + 1):
                        dve.wait_ge(l_in_psum, e * 4 + (p + 1 + 8))
                        dve.tensor_tensor(probs[:, u, 2 * p:2 * p + 2, :], bank[p % 2][:, :].rearrange("c (j n) -> c j n", j=2),
                                          bias[:, :, :].rearrange("c n j -> c j n")[:, bass.ds(o * OCT + 2 * p, 2), :], ALU.add).then_inc(added, 1)

                def minimum(g, o, u, half):
                    e = octet_step(b, g, o)
                    dve.wait_ge(added, e * 4 + (2 * half + 4))
                    dve.tensor_reduce(shift[:, u, 4 * half:4 * half + 4], probs[:, u, 4 * half:4 * half + 4, :], axis=AX.X, op=ALU.min).then_inc(min_ready, 1)

                def copy(g, o, u, half):
                    e = octet_step(b, g, o)
                    dve.wait_ge(pt_in_psum, e * 4 + (2 * half + 9))
                    dve.tensor_copy(probsT[:, u, 0, :, half * 4:half * 4 + 4, :],
                                    bank[2][:, :].rearrange("c (j h i) -> c h j i", j=4, h=GROUP_HEADS)).then_inc(pt_by_dve, 1)

                def invert(g, o, u, half):
                    e = octet_step(b, g, o)
                    cols = slice(4 * half, 4 * half + 4)
                    dve.wait_ge(exp_done, e * 8 + (4 * half + 4))
                    dve.wait_ge(scaled_by_act if half else scaled_by_pool, e + 1)
                    dve.reciprocal(inv[:, u, cols], sums[:, u, cols]).then_inc(inv_ready, 1)

                def accumulate(g, o, u):
                    e = octet_step(b, g, o)
                    dve.wait_ge(av_done, e + 2)
                    at = xraw[:, :].rearrange("c (i j) -> c j i", j=W)[:, bass.ds(o * OCT, OCT), :]
                    dve.tensor_tensor(at, at, bank[4 + u][:, :].rearrange("c (j i) -> c j i", i=H), ALU.add).then_inc(acc_done, 1)

                def key_samples():
                    dve.wait_ge(xs_in_psum, b + 1)
                    for g in range(GROUPS):
                        rows = slice(GC * g, GC * (g + 1))
                        dve.tensor_tensor(xs[rows, :].rearrange("c (k x) -> c k x", x=KW),
                                          bank[6][rows, :].rearrange("c (k g x) -> c k g x", g=GROUPS, x=KW)[:, :, g, :],
                                          gate[rows, g * KEYS:(g + 1) * KEYS].rearrange("c (k x) -> c k x", x=KW), ALU.mult).then_inc(xs_ready, 1)
                    dve.wait_ge(kv_in_psum, b * 3 + 1)
                    dve.tensor_copy(keys[:, :], bank[7][:, 0:KEYS]).then_inc(k_ready, 1)

                def take_stats(o):
                    dve.wait_ge(acc_done, octet_step(b, GROUPS - 1, o) + 3)
                    dve.bn_stats(sh.stats[:, bass.ds(b, 1), bass.ds(o, 1), :].rearrange("c b k s -> c (b k s)"),
                                 xraw[:, :].rearrange("c (i j) -> c j i", j=W)[:, bass.ds(o * OCT, OCT), :]).then_inc(stats_done, 1)

                for g in range(GROUPS):
                    dve.wait_ge(added, b * (2 * OCTS * 4) + (g * OCTS * 4 + 2))
                    dve.wait_ge(acc_done, b * (2 * OCTS) + (g * OCTS + 2))
                    pipelined(dve, KH, 2, lambda ky, u: copy_rows(g, ky, u), lambda ky, u: copy_bias(g, ky, u),
                              sampling_weights if g == 0 else lambda: None)
                    if g == 0:
                        key_samples()
                        dve.wait_ge(xraw_loaded, (b + 1) * 16)
                    dve.wait_ge(b_copied, bias_step(b, g, KH - 1) * 2 + 4)
                    for half in range(2):
                        add_bias(g, 0, 0, half)
                        minimum(g, 0, 0, half)

                    def step(o, u, more=True, former=True):
                        invert(g, o, u, 0)
                        if more:
                            add_bias(g, o + 1, 1 - u, 0)
                            minimum(g, o + 1, 1 - u, 0)
                        invert(g, o, u, 1)
                        copy(g, o, u, 0)
                        if former:
                            accumulate(g, o - 1, 1 - u)
                        if more:
                            add_bias(g, o + 1, 1 - u, 1)
                        copy(g, o, u, 1)
                        if more:
                            minimum(g, o + 1, 1 - u, 1)
                        if former and g == GROUPS - 1:
                            take_stats(o - 1)
                    octets(dve, step)
                    accumulate(g, OCTS - 1, 1)
                take_stats(OCTS - 1)
            dve.sem_inc(t_copied, 4)
            dve.sem_inc(b_copied, 2)
            dve.sem_inc(added, 2)
            dve.sem_inc(pt_by_dve, 1)
            dve.sem_inc(acc_done, 2)
            batches(dve, body)

def layer1(nc, sh, x_in, w, out):
    PAIRS, K2, MIN_CONN, MAX_CONN, NORM_EPS, GN8 = B // 2, 9, 1, 8, 1e-12, 8
    STEPS = H // ROWS
    LX = mybir.AxisListType.X
    SLOTS = 4
    BY_DVE, BY_POOL = (0, 2, 3, 5, 6), (1, 4, 7)
    ROUND = float(3 << 22)
    with ExitStack() as ctx:
        mem = Names(nc, ctx, "l1")
        xblk = mem.sbuf("xblk", [C, 2, 2, CHUNK])
        xnorm = mem.sbuf("xnorm", [C, ROWS, 2, W])
        xt = mem.sbuf("xt", [C, 2, H + 2, C])
        xleft = mem.sbuf("xleft", [C, 2, ROWS + 1, C])
        xright = mem.sbuf("xright", [C, 2, ROWS + 1, C])
        prod = [mem.sbuf(f"prod{q}", [C, ROWS, C]) for q in range(5)]
        dots = mem.sbuf("dots", [C, K2, H])
        inv_avg = mem.sbuf("inv_avg", [C, 2, 3, H + 2])
        sim = mem.sbuf("sim", [C, K2, H])
        rank = mem.sbuf("rank", [C, K2, H])
        wins = mem.sbuf("wins", [C, K2, H])
        beats = mem.sbuf("beats", [C, K2 - 1, H])
        total = mem.sbuf("total", [C, H])
        lap = mem.sbuf("lap", [C, H])
        kval = mem.sbuf("kval", [C, H])
        extreme = mem.sbuf("extreme", [C, 2])
        ext_row = mem.sbuf("ext_row", [2, 2])
        ext_wide = mem.sbuf("ext_wide", [2, 2, W])
        ext = mem.sbuf("ext", [C, 3])
        wsrc = mem.sbuf("wsrc", [C, K2, H])
        edge = mem.sbuf("edge", [C, 4])
        diag = mem.sbuf("diag", [C, K2, C])
        wdiag = mem.sbuf("wdiag", [C, SLOTS, K2, C])
        stage = mem.sbuf("stage", [C, 2, ROWS + 2, C])
        xres = mem.sbuf("xres", [C, 2, 2, CHUNK])
        affine = mem.sbuf("affine", [C, 2, CHUNK])
        enh = mem.sbuf("enh", [C, 2, 2, CHUNK])
        hid = mem.sbuf("hid", [C, 2, 2, CHUNK])
        res = mem.sbuf("res", [C, 2, 2, CHUNK])
        w1T = mem.sbuf("w1T", [C, 2, C])
        w2T = mem.sbuf("w2T", [C, 2, C])
        b1 = mem.sbuf("b1", [C, 2])
        b2 = mem.sbuf("b2", [C, 1])
        gscale = mem.sbuf("gscale", [C, B])
        gshift = mem.sbuf("gshift", [C, B])

        chain_sem = mem.sem("setup_chain")
        waits_met = mem.sem("waits_met")
        weight_chain = mem.sem("weight_chain")

        with ExitStack() as sctx:
            smem = Names(nc, sctx, "l1s")
            w1, w2 = xblk[:, 0, :, 0:C], xblk[:, 1, :, 0:C]
            gnw = smem.sbuf("gnw", [C, 2])
            mean8 = res[:, 0, 0, 0:C]
            mn = smem.sbuf("mn", [C, 2, B])
            g8 = smem.sbuf("g8", [C, 2, B])
            tmp = smem.sbuf("tmp", [C, B])
            ps = smem.psum("ps")
            ps2 = smem.psum("ps2")
            loaded = smem.sem("loaded")
            masks_ready = smem.sem("masks_ready")
            pool_chain = smem.sem("pool_chain")
            wt_in_psum = smem.sem("wt_in_psum")
            moments_ready = smem.sem("moments_ready")
            g8_ready = smem.sem("g8_ready")
            var_ready = smem.sem("var_ready")
            std_ready = smem.sem("std_ready")
            block = sctx.enter_context(nc.Block())

            @block.sync
            def _(sp):
                sp.dma_start(w1, w["w1"].rearrange("(h o) c -> o h c", h=2)).then_inc(loaded, 16)
                sp.dma_start(w2, w["w2"].rearrange("o (h c) -> o h c", h=2)).then_inc(loaded, 16)
                for h in range(2):
                    sp.dma_start(b1[:, h:h + 1], w["b1"][h * C:(h + 1) * C].rearrange("(o a) -> o a", a=1)).then_inc(loaded, 16)
                sp.dma_start(b2[:, :], w["b2"].rearrange("(o a) -> o a", a=1)).then_inc(loaded, 16)
                sp.dma_start(gnw[:, 0:1], w["gn_weight"].rearrange("(o a) -> o a", a=1)).then_inc(loaded, 16)
                sp.dma_start(gnw[:, 1:2], w["gn_bias"].rearrange("(o a) -> o a", a=1)).then_inc(loaded, 16)
                sp.wait_ge(loaded, 112)

            @block.gpsimd
            def _(pool):
                chain = Chain(pool, pool_chain)
                pool.memset(mean8, 1.0 / GN8)
                pool.memset(edge[:, :], 0.0)
                pool.memset(inv_avg[:, :, :, :], 0.0)
                pool.memset(wsrc[:, :, :], 0.0)
                chain.link(pool.memset(diag[:, :, :], 0.0))
                chain.link(pool.affine_select(out=mean8, in_=mean8, compare_op=ALU.is_ge, fill=0.0, base=0,
                                              pattern=[[-GN8, C // GN8], [0, GN8]], channel_multiplier=1))
                chain.link(pool.affine_select(out=mean8, in_=mean8, compare_op=ALU.is_ge, fill=0.0, base=GN8 - 1,
                                              pattern=[[GN8, C // GN8], [0, GN8]], channel_multiplier=-1))
                for b in range(2):
                    for k in range(K2):
                        part = diag[64 * b:64 * b + 64, k, 64 * b:64 * b + 64]
                        chain.link(pool.affine_select(out=part, in_=part, compare_op=ALU.not_equal, fill=1.0, base=-(k % 3 - 1),
                                                      pattern=[[-1, W]], channel_multiplier=1))
                    for col, at in ((0, 0), (2, W - 1)):
                        part = edge[64 * b:64 * b + 64, col:col + 1]
                        chain.link(pool.affine_select(out=part, in_=part, compare_op=ALU.not_equal, fill=1.0, base=-at,
                                                      pattern=[[0, 1]], channel_multiplier=1))
                pool.sem_inc(masks_ready, 1)

            @block.tensor
            def _(pe):
                pe.wait_ge(loaded, 112)
                for h in range(2):
                    pe.transpose(ps[:, h * C:(h + 1) * C], w1[:, h, :], sh.ident[:, :])
                for h in range(2):
                    last = pe.transpose(ps[:, (2 + h) * C:(3 + h) * C], w2[:, h, :], sh.ident[:, :])
                last.then_inc(wt_in_psum, 1)
                pe.wait_ge(moments_ready, 1)
                pe.wait_ge(masks_ready, 1)
                pe.matmul(ps2[:, 0:2 * B], mean8, mn[:, :, :].rearrange("c t b -> c (t b)"),
                          start=True, stop=True).then_inc(g8_ready, 1)

            @block.scalar
            def _(act):
                act.wait_ge(var_ready, 1)
                act.activation(tmp[:, :], tmp[:, :], ACT.Sqrt).then_inc(std_ready, 1)

            @block.vector
            def _(dve):
                chain = Chain(dve, chain_sem)
                link = chain.link
                mean, second = sh.moments[:, :, 0], sh.moments[:, :, 1]
                link(dve.tensor_tensor(mn[:, 0, :], mean, sh.rstd[:, :], ALU.mult))
                link(dve.tensor_tensor(tmp[:, :], mn[:, 0, :], sh.shift[:, :], ALU.mult))
                link(dve.tensor_tensor(mn[:, 0, :], mn[:, 0, :], sh.shift[:, :], ALU.add))
                link(dve.tensor_tensor(mn[:, 1, :], second, sh.rstd[:, :], ALU.mult))
                link(dve.tensor_tensor(mn[:, 1, :], mn[:, 1, :], sh.rstd[:, :], ALU.mult))
                link(dve.scalar_tensor_tensor(mn[:, 1, :], tmp[:, :], 2.0, mn[:, 1, :], op0=ALU.mult, op1=ALU.add))
                link(dve.tensor_tensor(tmp[:, :], sh.shift[:, :], sh.shift[:, :], ALU.mult))
                dve.tensor_tensor(mn[:, 1, :], mn[:, 1, :], tmp[:, :], ALU.add).then_inc(moments_ready, 1)
                dve.wait_ge(wt_in_psum, 1)
                dve.tensor_copy(w1T[:, :, :].rearrange("c h o -> c (h o)"), ps[:, 0:2 * C])
                dve.tensor_copy(w2T[:, :, :].rearrange("c h o -> c (h o)"), ps[:, 2 * C:4 * C])
                dve.wait_ge(g8_ready, 1)
                link(dve.tensor_copy(g8[:, :, :].rearrange("c t b -> c (t b)"), ps2[:, 0:2 * B]))
                link(dve.tensor_tensor(tmp[:, :], g8[:, 0, :], g8[:, 0, :], ALU.mult))
                link(dve.tensor_tensor(tmp[:, :], g8[:, 1, :], tmp[:, :], ALU.subtract))
                dve.tensor_scalar(tmp[:, :], tmp[:, :], GN_EPS, None, ALU.add).then_inc(var_ready, 1)
                dve.wait_ge(std_ready, 1)
                link(dve.reciprocal(tmp[:, :], tmp[:, :]))
                dve.wait_ge(loaded, 112)
                link(dve.tensor_scalar(tmp[:, :], tmp[:, :], gnw[:, 0:1], None, ALU.mult))
                link(dve.tensor_tensor(gscale[:, :], tmp[:, :], sh.rstd[:, :], ALU.mult))
                link(dve.tensor_tensor(g8[:, 1, :], sh.shift[:, :], g8[:, 0, :], ALU.subtract))
                link(dve.tensor_tensor(g8[:, 1, :], g8[:, 1, :], tmp[:, :], ALU.mult))
                dve.tensor_scalar(gshift[:, :], g8[:, 1, :], gnw[:, 1:2], None, ALU.add)
                dve.wait_ge(masks_ready, 1)
                dve.tensor_scalar(edge[:, 1:2], edge[:, 0:1], -1.0, 1.0, ALU.mult, ALU.add)
                dve.tensor_scalar(edge[:, 3:4], edge[:, 2:3], -1.0, 1.0, ALU.mult, ALU.add)

        turn_ps = [mem.psum("turn_ps")]
        gather_ps = [[mem.psum(f"gather_ps{u}{half}") for half in range(2)] for u in range(2)]
        hid_ps = [mem.psum(f"hid_ps{h}") for h in range(2)]
        ffn_ps = mem.psum("ffn_ps")

        blk_loaded = [mem.sem(f"blk_loaded{u}") for u in range(2)]
        normed = mem.sem("normed")
        turned = mem.sem("turned")
        turn_copied = mem.sem("turn_copied")
        shifted = [mem.sem(f"shifted{u}") for u in range(2)]
        squared = mem.sem("squared")
        pool_prods = mem.sem("pool_prods")
        dve_prods = mem.sem("dve_prods")
        summed = mem.sem("summed")
        norm_sums = mem.sem("norm_sums")
        roots = mem.sem("roots")
        cols_ready = mem.sem("cols_ready")
        cols_shifted = mem.sem("cols_shifted")
        ext_ready = mem.sem("ext_ready")
        ext_turned = mem.sem("ext_turned")
        sims_ready = mem.sem("sims_ready")
        exps_ready = mem.sem("exps_ready")
        weights_ready = mem.sem("weights_ready")
        weights_shifted = mem.sem("weights_shifted")
        res_loaded = [mem.sem(f"res_loaded{u}") for u in range(2)]
        staged = mem.sem("staged")
        diag_dve = mem.sem("diag_dve")
        diag_pool = mem.sem("diag_pool")
        row_done = mem.sem("row_done")
        affine_ready = mem.sem("affine_ready")
        enh_ready = mem.sem("enh_ready")
        hid_in_psum = mem.sem("hid_in_psum")
        hid_ready = mem.sem("hid_ready")
        ffn_in_psum = mem.sem("ffn_in_psum")
        ffn_copied = mem.sem("ffn_copied")
        res_half = mem.sem("res_half")
        res_ready = mem.sem("res_ready")
        stats_done = mem.sem("stats_done")
        stored = [mem.sem(f"stored{u}") for u in range(2)]
        SHIFTS = 8 * 16
        NCOLS = 24 * 16
        WS = 4 * 16

        block = ctx.enter_context(nc.Block())

        def rows_of(t, r, n):
            return xt[:, t % 2, bass.ds(r, n), :]

        def apart(eng, at):
            if not isinstance(at, int):
                eng.sem_inc(waits_met, 1)

        def second_before(t, c):
            return t > 1 or (t == 1 and not (isinstance(c, int) and c < 2))

        def block_before(t, c, lag):
            return (t - 1, c - lag + STEPS) if isinstance(c, int) and c < lag else (t, c - lag)

        def steps(eng, t, step):
            def body(j):
                for u in range(2):
                    step(j * 2 + u, u)
            peeled = 2 if t == 1 else 1
            for j in range(peeled):
                body(j)
            with eng.Fori(peeled, STEPS // 2) as j:
                body(j)

        def image(ap, t, c):
            return ap[2 * t:2 * t + 2].rearrange("b c n -> c b n")[:, :, bass.ds(c * CHUNK, CHUNK)]

        @block.sync
        def _(sp):
            def load_block(t, c, u):
                wait(sp, normed, c + (t * STEPS - 1))
                apart(sp, c)
                sp.dma_start(xblk[:, u, :, :], image(x_in, t, c)).then_inc(blk_loaded[u], 16)

            def shift(t, c, u):
                n = t * STEPS + c
                sp.wait_ge(turn_copied, (n + 1) * 2)
                wait(sp, summed, n - 1)
                apart(sp, c)
                src = rows_of(t, c * ROWS, ROWS + 1)
                for b in range(2):
                    p = 64 * b
                    sp.dma_start(xleft[p + 1:p + 64, u, :, :], src[p:p + 63]).then_inc(shifted[u], 16)
                    sp.dma_start(xleft[p:p + 1, u, :, :], src[p + 1:p + 2]).then_inc(shifted[u], 16)
                    sp.dma_start(xright[p:p + 63, u, :, :], src[p + 1:p + 64]).then_inc(shifted[u], 16)
                    sp.dma_start(xright[p + 63:p + 64, u, :, :], src[p + 62:p + 63]).then_inc(shifted[u], 16)

            def load_res(t, c, u):
                g = (t - 1) * STEPS + c
                wait(sp, res_ready, (g - 1) * 2)
                apart(sp, c)
                sp.dma_start(xres[:, u, :, :], image(x_in, t - 1, c)).then_inc(res_loaded[u], 16)

            def store(t, c, u):
                sp.wait_ge(res_ready, (c + ((t - 1) * STEPS + 1)) * 2)
                apart(sp, c)
                sp.dma_start(image(out, t - 1, c), res[:, u, :, :]).then_inc(stored[u], 16)

            for t in range(PAIRS + 1):
                def step(c, u):
                    if t < PAIRS:
                        load_block(t, c, u)
                    if t >= 1:
                        load_res(t, c, u)
                    if t < PAIRS:
                        shift(t, c, u)
                    if second_before(t, c):
                        store(*block_before(t, c, 2), u)
                steps(sp, t, step)
                if t < PAIRS:
                    sp.wait_ge(cols_ready, t + 1)
                    for b in range(2):
                        p = 64 * b
                        lo, hi = slice(p, p + 63), slice(p + 1, p + 64)
                        first, second, but1, last = (slice(p + q, p + q + 1) for q in (0, 1, 62, 63))
                        moves = [
                            (inv_avg[hi, 0, 0, 1:H + 1], inv_avg[lo, 0, 1, 1:H + 1]),
                            (inv_avg[hi, 1, 0, 1:H + 1], inv_avg[lo, 1, 1, 1:H + 1]),
                            (inv_avg[lo, 0, 2, 1:H + 1], inv_avg[hi, 0, 1, 1:H + 1]),
                            (inv_avg[lo, 1, 2, 1:H + 1], inv_avg[hi, 1, 1, 1:H + 1]),
                            (inv_avg[first, 0, 0, 1:H + 1], inv_avg[second, 0, 1, 1:H + 1]),
                            (inv_avg[last, 0, 2, 1:H + 1], inv_avg[but1, 0, 1, 1:H + 1]),
                            (dots[hi, 3, :], dots[lo, 5, :]),
                            (dots[first, 3, :], dots[first, 5, :]),
                        ]
                        more = [
                            (dots[lo, 8, 0:H - 1], dots[hi, 0, 1:H]),
                            (dots[last, 8, 0:H - 1], dots[but1, 2, 1:H]),
                            (dots[hi, 6, 0:H - 1], dots[lo, 2, 1:H]),
                            (dots[first, 6, 0:H - 1], dots[second, 0, 1:H]),
                        ]
                        for to, of in moves + more:
                            sp.dma_start(to, of).then_inc(cols_shifted, 16)
                    sp.wait_ge(weights_ready, t + 1)
                    by_dx = lambda ap, dx: ap.rearrange("p (e d) y -> p e d y", d=3)[:, :, dx, :]
                    for b in range(2):
                        p = 64 * b
                        lo, hi = slice(p, p + 63), slice(p + 1, p + 64)
                        sp.dma_start(by_dx(wsrc[hi, :, :], 2), by_dx(sim[lo, :, :], 2)).then_inc(weights_shifted, 16)
                        sp.dma_start(by_dx(wsrc[lo, :, :], 0), by_dx(sim[hi, :, :], 0)).then_inc(weights_shifted, 16)
            for c in (STEPS - 2, STEPS - 1):
                store(PAIRS, c, c % 2)
            for u in range(2):
                sp.wait_ge(stored[u], 16 * PAIRS * STEPS // 2)

        @block.gpsimd
        def _(pool):
            def build(t, c, *rows):
                g = (t - 1) * STEPS + c
                pool.wait_ge(weights_shifted, WS * t)
                for y in rows:
                    wait(pool, row_done, g * ROWS + (y + 1 - SLOTS))
                    apart(pool, c)
                    pool.tensor_tensor(wdiag[:, y % SLOTS, :, :], diag[:, :, :],
                                      wsrc[:, :, bass.ds(c * ROWS + y, 1)].to_broadcast([C, K2, C]), ALU.mult).then_inc(diag_pool, 1)

            def prod_up(t, c):
                n = t * STEPS + c
                pool.wait_ge(turn_copied, (n + 1) * 2)
                wait(pool, summed, n)
                apart(pool, c)
                x, up = rows_of(t, c * ROWS + 1, ROWS), rows_of(t, c * ROWS, ROWS)
                pool.tensor_tensor(prod[2][:, :, :], x, up, ALU.mult).then_inc(pool_prods, 1)

            def prod_right(t, c, u):
                x = rows_of(t, c * ROWS + 1, ROWS)
                pool.wait_ge(shifted[u], (c + (t * STEPS + 2 - u)) * (SHIFTS // 2))
                apart(pool, c)
                pool.tensor_tensor(prod[1][:, :, :], x, xright[:, u, 1:ROWS + 1, :], ALU.mult).then_inc(pool_prods, 1)

            def result(g, u, *images):
                for b in images:
                    pool.wait_ge(ffn_copied, g * 2 + (b + 1))
                    pool.tensor_tensor(res[:, u, b, :], res[:, u, b, :], enh[:, u, b, :], ALU.add).then_inc(res_half, 1)
                    pool.wait_ge(res_half, g * 2 + (b + 1))
                    pool.tensor_tensor(res[:, u, b, :], res[:, u, b, :], xres[:, u, b, :], ALU.add).then_inc(res_ready, 1)

            for t in range(PAIRS + 1):
                def step(c, u):
                    if t >= 1:
                        build(t, c, 1)
                    if second_before(t, c):
                        result(c + ((t - 1) * STEPS - 2), u, 0)
                    if t >= 1:
                        build(t, c, 4)
                    if second_before(t, c):
                        result(c + ((t - 1) * STEPS - 2), u, 1)
                    if t < PAIRS and not (isinstance(c, int) and c == 0):
                        prod_up(t, c - 1)
                    if t >= 1:
                        build(t, c, 7)
                    if t < PAIRS and not (isinstance(c, int) and c == 0):
                        prod_right(t, c - 1, 1 - u)
                steps(pool, t, step)
                if t < PAIRS:
                    prod_up(t, STEPS - 1)
                    prod_right(t, STEPS - 1, 1)
            for g in (PAIRS * STEPS - 2, PAIRS * STEPS - 1):
                result(g, g % 2, 0, 1)

        @block.tensor
        def _(pe):
            def turn(t, c, u):
                n = t * STEPS + c
                pe.wait_ge(normed, n + 1)
                if isinstance(c, int) and c == 0:
                    wait(pe, weights_ready, t)
                for half in range(2):
                    wait(pe, turn_copied, n * 2 + half)
                    for r in range(4):
                        y = 4 * half + r
                        last = pe.transpose(turn_ps[0][:, r * C:(r + 1) * C], xnorm[:, y, :, :].rearrange("c b w -> c (b w)"), sh.ident[:, :])
                    last.then_inc(turned, 1)

            def gather(t, c, u, rows):
                g = (t - 1) * STEPS + c
                for y in rows:
                    if y == 0:
                        pe.wait_ge(staged, g + 1)
                        wait(pe, enh_ready, (g - 1) * 2)
                    for ready, own in ((diag_dve, BY_DVE), (diag_pool, BY_POOL)):
                        if y in own:
                            pe.wait_ge(ready, g * len(own) + (own.index(y) + 1))
                    for k in range(K2):
                        last = pe.matmul(gather_ps[u][y // 4][:, y % 4 * C:(y % 4 + 1) * C], stage[:, u, y + k // 3, :],
                                         wdiag[:, y % SLOTS, k, :], start=(k == 0), stop=(k == K2 - 1))
                    last.then_inc(row_done, 1)

            def hidden(g, u, b):
                pe.wait_ge(enh_ready, g * 2 + 2)
                for h in range(2):
                    wait(pe, hid_ready, (g * 2 + b - 1) * 2 + h + 1)
                    pe.matmul(hid_ps[h][:, :], w1T[:, h, :], enh[:, u, b, :], start=True, stop=True).then_inc(hid_in_psum, 1)

            def down(g, b):
                wait(pe, ffn_copied, g * 2 + b)
                for h in range(2):
                    pe.wait_ge(hid_ready, (g * 2 + b) * 2 + (h + 1))
                    last = pe.matmul(ffn_ps[:, :], w2T[:, h, :], hid[:, b, h, :], start=(h == 0), stop=(h == 1))
                last.then_inc(ffn_in_psum, 1)

            for t in range(PAIRS + 1):
                def step(c, u):
                    before = t >= 1 and not (isinstance(c, int) and t == 1 and c == 0)
                    g = (t - 1) * STEPS - 1 + c
                    if t >= 1:
                        gather(t, c, u, (0, 1))
                    if before:
                        hidden(g, 1 - u, 0)
                    if t < PAIRS:
                        turn(t, c, u)
                    if t >= 1:
                        gather(t, c, u, (2, 3))
                    if before:
                        down(g, 0)
                        hidden(g, 1 - u, 1)
                    if t >= 1:
                        gather(t, c, u, (4, 5))
                    if before:
                        down(g, 1)
                    if t >= 1:
                        gather(t, c, u, (6, 7))
                steps(pe, t, step)
                if t < PAIRS:
                    pe.wait_ge(ext_ready, 2 * t + 1)
                    pe.transpose(turn_ps[0][0:2, 0:C], extreme[:, :], sh.ident[:, :]).then_inc(ext_turned, 1)
                    pe.wait_ge(ext_ready, 2 * t + 2)
                    pe.transpose(turn_ps[0][:, C:C + 2], ext_wide[:, :, :].rearrange("q b w -> q (b w)"),
                                 sh.ident[0:2, 0:2]).then_inc(ext_turned, 1)
            g = PAIRS * STEPS - 1
            for b in range(2):
                hidden(g, 1, b)
                down(g, b)

        @block.scalar
        def _(act):
            def norm(t, c, u):
                n = t * STEPS + c
                act.wait_ge(blk_loaded[u], (n + (2 - u)) * 8)
                wait(act, turned, n * 2)
                for b in range(2):
                    last = act.activation(xnorm[:, :, b, :], xblk[:, u, b, :].rearrange("c (r w) -> c r w", w=W), ACT.Identity,
                                          scale=sh.rstd[:, 2 * t + b:2 * t + b + 1], bias=sh.shift[:, 2 * t + b:2 * t + b + 1])
                last.then_inc(normed, 1)

            def copy_turned(t, c, u):
                n = t * STEPS + c
                for half in range(2):
                    act.wait_ge(turned, n * 2 + (half + 1))
                    apart(act, c)
                    if isinstance(c, int) and c == 0 and half == 0:
                        act.activation(xt[:, t % 2, 0, :], turn_ps[0][:, C:2 * C], ACT.Copy)
                    act.activation(rows_of(t, c * ROWS + (1 + 4 * half), 4), turn_ps[0][:, :].rearrange("p (r c) -> p r c", c=C),
                                   ACT.Copy).then_inc(turn_copied, 1)

            def relu(g, b):
                for h in range(2):
                    act.wait_ge(hid_in_psum, (g * 2 + b) * 2 + (h + 1))
                    wait(act, ffn_in_psum, (g - 1) * 2 + b + 1)
                    act.activation(hid[:, b, h, :], hid_ps[h][:, :], ACT.Relu, bias=b1[:, h:h + 1]).then_inc(hid_ready, 1)

            def copy_ffn(g, u, b):
                act.wait_ge(ffn_in_psum, g * 2 + (b + 1))
                if b == 0:
                    wait(act, stored[u], (g - u) * 8)
                    wait(act, stats_done, (g - 1) * 2)
                act.activation(res[:, u, b, :], ffn_ps[:, :], ACT.Identity, bias=b2[:, :]).then_inc(ffn_copied, 1)

            def square(t, c):
                n = t * STEPS + c
                act.wait_ge(turn_copied, (n + 1) * 2)
                wait(act, summed, n)
                apart(act, c)
                act.activation(prod[0][:, :, :], rows_of(t, c * ROWS + 1, ROWS), ACT.Square).then_inc(squared, 1)

            def gn_affine(t, c, u):
                g = (t - 1) * STEPS + c
                act.wait_ge(res_loaded[u], (g + (2 - u)) * 8)
                wait(act, enh_ready, g * 2)
                for b in range(2):
                    n = 2 * (t - 1) + b
                    act.activation(affine[:, b, :], xres[:, u, b, :], ACT.Identity, scale=gscale[:, n:n + 1],
                                   bias=gshift[:, n:n + 1]).then_inc(affine_ready, 1)

            for t in range(PAIRS + 1):
                if 2 <= t < PAIRS:
                    act.wait_ge(staged, (t - 1) * STEPS)

                def step(c, u):
                    before = t >= 1 and not (isinstance(c, int) and t == 1 and c == 0)
                    g = (t - 1) * STEPS - 1 + c
                    if t < PAIRS:
                        norm(t, c, u)
                    if before:
                        relu(g, 0)
                    if t < PAIRS:
                        copy_turned(t, c, u)
                    if before:
                        copy_ffn(g, 1 - u, 0)
                        relu(g, 1)
                    if t < PAIRS and not (isinstance(c, int) and c == 0):
                        square(t, c - 1)
                    if before:
                        copy_ffn(g, 1 - u, 1)
                    if t >= 1:
                        gn_affine(t, c, u)
                steps(act, t, step)
                if t < PAIRS:
                    square(t, STEPS - 1)
                    act.wait_ge(turn_copied, (t + 1) * STEPS * 2)
                    act.activation(xt[:, t % 2, H + 1, :], xt[:, t % 2, H - 1, :], ACT.Copy)
                    act.wait_ge(norm_sums, t + 1)
                    act.activation(total[:, :], dots[:, 4, :], ACT.Sqrt).then_inc(roots, 1)
                    act.wait_ge(sims_ready, t + 1)
                    act.activation(wins[:, :, :], sim[:, :, :], ACT.Exp).then_inc(exps_ready, 1)
            g = PAIRS * STEPS - 1
            for b in range(2):
                relu(g, b)
                copy_ffn(g, 1, b)

        @block.vector
        def _(dve):
            chain = Chain(dve, weight_chain)
            link = chain.link

            def build(t, c, *rows):
                g = (t - 1) * STEPS + c
                for y in rows:
                    wait(dve, row_done, g * ROWS + (y + 1 - SLOTS))
                    dve.tensor_tensor(wdiag[:, y % SLOTS, :, :], diag[:, :, :],
                                      wsrc[:, :, bass.ds(c * ROWS + y, 1)].to_broadcast([C, K2, C]), ALU.mult).then_inc(diag_dve, 1)

            def put_stage(t, c, u):
                g = (t - 1) * STEPS + c
                wait(dve, row_done, (g - 1) * ROWS)
                dve.tensor_copy(stage[:, u, :, :], rows_of(t - 1, c * ROWS, ROWS + 2)).then_inc(staged, 1)

            def enhance(g, u):
                for half in range(2):
                    dve.wait_ge(row_done, g * ROWS + 4 * (half + 1))
                    if half == 0:
                        dve.wait_ge(affine_ready, g * 2 + 2)
                        wait(dve, res_half, (g - 1) * 2)
                    part = lambda ap: ap.rearrange("c b (y x) -> c y b x", x=W)[:, 4 * half:4 * half + 4, :, :]
                    dve.tensor_tensor(part(enh[:, u, :, :]), gather_ps[u][half][:, :].rearrange("c (y b x) -> c y b x", b=2, x=W),
                                      part(affine[:, :, :]), ALU.add).then_inc(enh_ready, 1)

            def stats(t, c, u):
                g = c + (t - 1) * STEPS
                for b in range(2):
                    dve.wait_ge(res_ready, g * 2 + (b + 1))
                    dve.bn_stats(sh.stats[:, 2 * (t - 1) + b, bass.ds(c, 1), :].rearrange("c k s -> c (k s)"),
                                 res[:, u, b, :]).then_inc(stats_done, 1)

            def sums(t, c, u):
                side_prods(t, c, u)
                side_sums(t, c)
                pool_sums(t, c)

            def side_prods(t, c, u):
                n = t * STEPS + c
                x = rows_of(t, c * ROWS + 1, ROWS)
                dve.wait_ge(turn_copied, (n + 1) * 2)
                dve.wait_ge(shifted[u], (c + (t * STEPS + 2 - u)) * (SHIFTS // 2))
                wait(dve, summed, n)
                dve.tensor_tensor(prod[3][:, :, :], x, xleft[:, u, 0:ROWS, :], ALU.mult).then_inc(dve_prods, 1)
                dve.tensor_tensor(prod[4][:, :, :], x, xright[:, u, 0:ROWS, :], ALU.mult).then_inc(dve_prods, 1)

            def sum_up(t, c, *those):
                n, col = t * STEPS + c, bass.ds(c * ROWS, ROWS)
                for q, k, ready, value in those:
                    dve.wait_ge(ready, n * value[0] + value[1])
                    last = dve.reduce_sum(dots[:, k, col], prod[q][:, :, :], axis=LX)
                return last

            def side_sums(t, c):
                dve.reduce_sum(inv_avg[:, 1, 1, bass.ds(c * ROWS + 1, ROWS)], rows_of(t, c * ROWS + 1, ROWS), axis=LX)
                sum_up(t, c, (3, 0, dve_prods, (2, 1)), (4, 2, dve_prods, (2, 2)))

            def pool_sums(t, c):
                sum_up(t, c, (0, 4, squared, (1, 1)), (2, 1, pool_prods, (2, 1)), (1, 5, pool_prods, (2, 2))).then_inc(summed, 1)

            def weights(t):
                dve.wait_ge(summed, (t + 1) * STEPS)
                dve.tensor_copy(dots[:, 7, 0:H - 1], dots[:, 1, 1:H]).then_inc(norm_sums, 1)
                dve.tensor_copy(dots[:, 7, H - 1:H], dots[:, 1, H - 1:H])
                dve.wait_ge(roots, t + 1)
                link(dve.tensor_scalar(total[:, :], total[:, :], NORM_EPS, None, ALU.max))
                dve.tensor_scalar(inv_avg[:, 1, 1, 1:H + 1], inv_avg[:, 1, 1, 1:H + 1], 1.0 / C, None, ALU.mult)
                link(dve.reciprocal(inv_avg[:, 0, 1, 1:H + 1], total[:, :]))
                dve.tensor_copy(inv_avg[:, 0, 1, 0:1], inv_avg[:, 0, 1, 2:3]).then_inc(cols_ready, 1)
                dve.tensor_copy(inv_avg[:, 0, 1, H + 1:H + 2], inv_avg[:, 0, 1, H - 1:H])
                dve.wait_ge(cols_shifted, NCOLS * (t + 1))
                for d in (0, 2):
                    dve.tensor_copy(inv_avg[:, 0, d, 0:1], inv_avg[:, 0, d, 2:3])
                    dve.tensor_copy(inv_avg[:, 0, d, H + 1:H + 2], inv_avg[:, 0, d, H - 1:H])
                dve.tensor_copy(dots[:, 8, H - 1:H], dots[:, 2, H - 1:H])
                link(dve.tensor_copy(dots[:, 6, H - 1:H], dots[:, 0, H - 1:H]))
                a = inv_avg[:, 1, :, :]
                link(dve.tensor_tensor(lap[:, :], a[:, 1, 0:H], a[:, 1, 2:H + 2], ALU.add))
                link(dve.tensor_tensor(lap[:, :], lap[:, :], a[:, 0, 1:H + 1], ALU.add))
                link(dve.tensor_tensor(lap[:, :], lap[:, :], a[:, 2, 1:H + 1], ALU.add))
                link(dve.scalar_tensor_tensor(lap[:, :], a[:, 1, 1:H + 1], 4.0, lap[:, :], op0=ALU.mult, op1=ALU.subtract))
                link(dve.scalar_tensor_tensor(lap[:, :], lap[:, :], -1.0, lap[:, :], op0=ALU.mult, op1=ALU.max))
                dve.tensor_reduce(extreme[:, 0:1], lap[:, :], axis=LX, op=ALU.min)
                dve.tensor_reduce(extreme[:, 1:2], lap[:, :], axis=LX, op=ALU.max, negate=True).then_inc(ext_ready, 1)
                for e in range(3):
                    last = dve.tensor_tensor(sim[:, 3 * e:3 * e + 3, :], dots[:, 3 * e:3 * e + 3, :],
                                             inv_avg[:, 0, :, e:e + H], ALU.mult)
                link(last)
                centre = inv_avg[:, 0, 1:2, 1:H + 1].to_broadcast([C, K2, H])
                dve.tensor_tensor(sim[:, :, :], sim[:, :, :], centre, ALU.mult).then_inc(sims_ready, 1)
                dve.wait_ge(ext_turned, 2 * t + 1)
                link(dve.tensor_reduce(ext_row[:, :], turn_ps[0][0:2, 0:C].rearrange("q (b w) -> q b w", b=2), axis=LX, op=ALU.min))
                dve.tensor_copy(ext_wide[:, :, :], ext_row[:, :].rearrange("q (b o) -> q b o", o=1).to_broadcast([2, 2, W])).then_inc(ext_ready, 1)
                dve.wait_ge(ext_turned, 2 * t + 2)
                link(dve.tensor_copy(ext[:, 0:2], turn_ps[0][:, C:C + 2]))
                link(dve.tensor_tensor(ext[:, 2:3], ext[:, 0:1], ext[:, 1:2], ALU.add))
                link(dve.tensor_scalar(ext[:, 2:3], ext[:, 2:3], -1.0, 1e-8, ALU.mult, ALU.add))
                link(dve.reciprocal(ext[:, 2:3], ext[:, 2:3]))
                link(dve.tensor_scalar(kval[:, :], lap[:, :], ext[:, 0:1], ext[:, 2:3], ALU.subtract, ALU.mult))
                link(dve.tensor_scalar(kval[:, :], kval[:, :], float(MAX_CONN - MIN_CONN), ROUND, ALU.mult, ALU.add))
                link(dve.tensor_scalar(kval[:, :], kval[:, :], ROUND, float(MIN_CONN), ALU.subtract, ALU.add))
                dve.wait_ge(sims_ready, t + 1)
                dve.wait_ge(exps_ready, t + 1)
                for k in range(K2):
                    last = dve.memset(rank[:, k, :], float(K2 - 1 - k))
                link(last)
                for j in range(K2 - 1):
                    m = K2 - 1 - j
                    link(dve.tensor_tensor(beats[:, 0:m, :], sim[:, j:j + 1, :].to_broadcast([C, m, H]), sim[:, j + 1:K2, :], ALU.is_ge))
                    dve.tensor_tensor(rank[:, j + 1:K2, :], rank[:, j + 1:K2, :], beats[:, 0:m, :], ALU.add)
                    link(dve.reduce_sum(total[:, :], beats[:, 0:m, :].rearrange("p k y -> p y k"), axis=LX))
                    link(dve.tensor_tensor(rank[:, j, :], rank[:, j, :], total[:, :], ALU.subtract))
                link(dve.tensor_tensor(rank[:, :, :], rank[:, :, :], kval[:, :].rearrange("p (o y) -> p o y", o=1).to_broadcast([C, K2, H]), ALU.is_lt))
                link(dve.tensor_tensor(wins[:, :, :], wins[:, :, :], rank[:, :, :], ALU.mult))
                link(dve.reduce_sum(total[:, :], wins[:, :, :].rearrange("p k y -> p y k"), axis=LX))
                link(dve.reciprocal(total[:, :], total[:, :]))
                link(dve.tensor_tensor(sim[:, :, :], wins[:, :, :], total[:, :].rearrange("p (o y) -> p o y", o=1).to_broadcast([C, K2, H]), ALU.mult))
                by_dx = lambda ap, d: ap.rearrange("p (e d) y -> p e d y", d=3)[:, :, d, :]
                left, right = by_dx(sim[:, :, :], 0), by_dx(sim[:, :, :], 2)
                link(dve.scalar_tensor_tensor(right, left, edge[:, 0:1], right, op0=ALU.mult, op1=ALU.add))
                link(dve.tensor_scalar(left, left, edge[:, 1:2], None, ALU.mult))
                link(dve.scalar_tensor_tensor(left, right, edge[:, 2:3], left, op0=ALU.mult, op1=ALU.add))
                link(dve.tensor_scalar(right, right, edge[:, 3:4], None, ALU.mult))
                if t:
                    dve.wait_ge(diag_pool, t * STEPS * len(BY_POOL))
                    dve.wait_ge(diag_dve, t * STEPS * len(BY_DVE))
                dve.tensor_copy(by_dx(wsrc[:, :, :], 1), by_dx(sim[:, :, :], 1)).then_inc(weights_ready, 1)

            for t in range(PAIRS + 1):
                if t >= 1:
                    dve.wait_ge(weights_shifted, WS * t)

                def step(c, u):
                    before = t >= 1 and not (isinstance(c, int) and t == 1 and c == 0)
                    g = (t - 1) * STEPS - 1 + c
                    if t >= 1:
                        put_stage(t, c, u)
                        build(t, c, 0, 2)
                    if before:
                        enhance(g, 1 - u)
                    lagging = t < PAIRS and not (isinstance(c, int) and c == 0)
                    if lagging:
                        side_prods(t, c - 1, 1 - u)
                    if t >= 1:
                        build(t, c, 3)
                    if lagging:
                        side_sums(t, c - 1)
                    if t >= 1:
                        build(t, c, 5)
                    if lagging:
                        pool_sums(t, c - 1)
                    if t >= 1:
                        build(t, c, 6)
                    if second_before(t, c):
                        stats(*block_before(t, c, 2), u)
                steps(dve, t, step)
                if t < PAIRS:
                    sums(t, STEPS - 1, 1)
                    weights(t)
            g = PAIRS * STEPS - 1
            enhance(g, 1)
            for c in (STEPS - 2, STEPS - 1):
                stats(PAIRS, c, c % 2)

def layer2(nc, sh, x_in, w, out):
    ROUNDS = B // 2
    P5, P11 = 2, 5
    BLOCKS, BROWS = 4, H // 4
    XW = W + 2 * P11
    with ExitStack() as ctx:
        mem = Names(nc, ctx, "l2")
        xin = mem.sbuf("xin", [C, 2, HW])
        xpad = mem.sbuf("xpad", [C, 2, H + 2, XW])
        sum33 = mem.sbuf("sum33", [C, H, W])
        mid5 = mem.sbuf("mid5", [C, H + 2 * P5, W])
        mid11 = mem.sbuf("mid11", [C, H + 2 * P11, W])
        res = mem.sbuf("res", [C, 2, HW])
        w33 = mem.sbuf("w33", [C, 9])
        w15 = mem.sbuf("w15", [C, 5])
        w51 = mem.sbuf("w51", [C, 5])
        w111 = mem.sbuf("w111", [C, 11])
        w1111 = mem.sbuf("w1111", [C, 11])
        biases = mem.sbuf("biases", [C, 6])
        w3 = mem.sbuf("w3", [C, C])
        w3T = mem.sbuf("w3T", [C, C])
        fold5 = mem.sbuf("fold5", [C, 5, C])
        fold11 = mem.sbuf("fold11", [C, 11, C])
        bsum = mem.sbuf("bsum", [C, 1])
        mix_bias = mem.sbuf("mix_bias", [C, 1])
        NPS = 4
        mix = [mem.psum(f"mix{k}") for k in range(NPS)]
        setup_ps = mem.psum("setup_ps")

        weights_loaded = mem.sem("weights_loaded")
        pads_zero = mem.sem("pads_zero")
        setup_chain = mem.sem("setup_chain")
        w3T_in_psum = mem.sem("w3T_in_psum")
        w3T_ready = mem.sem("w3T_ready")
        bias_in_psum = mem.sem("bias_in_psum")
        mix_bias_ready = mem.sem("mix_bias_ready")
        folds_ready = mem.sem("folds_ready")
        x_loaded = [mem.sem(f"x_loaded{s}") for s in range(2)]
        normed = [mem.sem(f"normed{s}") for s in range(2)]
        first_taps = mem.sem("first_taps")
        tap_chain = mem.sem("tap_chain")
        taps_done = mem.sem("taps_done")
        mixed = mem.sem("mixed")
        evacuated = mem.sem("evacuated")
        gated = mem.sem("gated")
        res_ready = mem.sem("res_ready")
        stats_done = mem.sem("stats_done")
        stored = [mem.sem(f"stored{s}") for s in range(2)]
        smalls = [(w33, w["w0"]), (w15, w["w0_1"]), (w51, w["w0_2"]), (w111, w["w1_1"]), (w1111, w["w1_2"]), (w3, w["w3"])]
        vectors = ["b0", "b0_1", "b0_2", "b1_1", "b1_2", "b3"]
        LOADS = 16 * (len(smalls) + len(vectors))
        block = ctx.enter_context(nc.Block())

        def interior(s, r0=0, nr=H):
            return xpad[:, s, 1 + r0:1 + r0 + nr, P11:P11 + W]

        def tap_sums(s, r):
            return [(sum33[:, r:r + BROWS, :], None, [(w33[:, 3 * dy + dx:3 * dy + dx + 1],
                     xpad[:, s, r + dy:r + dy + BROWS, P11 - 1 + dx:P11 - 1 + dx + W]) for dy in range(3) for dx in range(3)]),
                    (mid5[:, P5 + r:P5 + r + BROWS, :], biases[:, 1:2], [(w15[:, k:k + 1],
                     xpad[:, s, 1 + r:1 + r + BROWS, P11 - P5 + k:P11 - P5 + k + W]) for k in range(5)]),
                    (mid11[:, P11 + r:P11 + r + BROWS, :], biases[:, 3:4], [(w111[:, k:k + 1],
                     xpad[:, s, 1 + r:1 + r + BROWS, k:k + W]) for k in range(11)])]

        def chunks_read(blk):
            return min(CHUNKS, (blk * BROWS + BROWS - 1 + P11) // ROWS + 1)

        @block.sync
        def _(sp):
            for t, src in smalls:
                sp.dma_start(t[:, :], src).then_inc(weights_loaded, 16)
            for k, name in enumerate(vectors):
                sp.dma_start(biases[:, k:k + 1], w[name]).then_inc(weights_loaded, 16)

            def load(i, s):
                wait(sp, res_ready, (i * 2 + (s - 1)) * CHUNKS)
                sp.dma_start(xin[:, s, :], x_in[bass.ds(i * 2 + s, 1)].rearrange("b c n -> (b c) n")).then_inc(x_loaded[s], 16)

            def store(i, s):
                n = i * 2 + s
                sp.wait_ge(res_ready, (n + 1) * CHUNKS)
                sp.dma_start(out[bass.ds(n, 1)].rearrange("b c n -> (b c) n"), res[:, s, :]).then_inc(stored[s], 16)

            load(0, 0)
            load(0, 1)
            with sp.Fori(0, ROUNDS - 1) as i:
                for s in range(2):
                    store(i, s)
                    load(i + 1, s)
            for s in range(2):
                store(ROUNDS - 1, s)
            for s in range(2):
                sp.wait_ge(stored[s], 16 * ROUNDS)

        @block.gpsimd
        def _(pool):
            pool.memset(xpad[:, :, :, :], 0.0).then_inc(pads_zero, 1)
            for t, p in ((mid5, P5), (mid11, P11)):
                pool.memset(t[:, 0:p, :], 0.0).then_inc(pads_zero, 1)
                pool.memset(t[:, H + p:H + 2 * p, :], 0.0).then_inc(pads_zero, 1)

            def body(i):
                for s in range(2):
                    n = i * 2 + s
                    for k in range(CHUNKS):
                        part = res[:, s, k * CHUNK:(k + 1) * CHUNK]
                        image = part.rearrange("c (h w) -> c h w", w=W)
                        pool.wait_ge(evacuated, n * CHUNKS + (k + 1))
                        pool.tensor_tensor(image, image, interior(s, k * ROWS, ROWS), ALU.mult).then_inc(gated, 1)
                        pool.wait_ge(gated, n * CHUNKS + (k + 1))
                        pool.tensor_tensor(part, part, xin[:, s, k * CHUNK:(k + 1) * CHUNK], ALU.add).then_inc(res_ready, 1)
            each(pool, ROUNDS, body)

        @block.tensor
        def _(pe):
            pe.wait_ge(weights_loaded, LOADS)
            pe.transpose(setup_ps[:, 0:C], w3[:, :], sh.ident[:, :]).then_inc(w3T_in_psum, 1)
            pe.wait_ge(w3T_ready, 2)
            pe.matmul(setup_ps[:, C:C + 1], w3T[:, :], bsum[:, :], start=True, stop=True).then_inc(bias_in_psum, 1)
            pe.wait_ge(folds_ready, 1)
            pe.wait_ge(pads_zero, 5)

            def body(i):
                for s in range(2):
                    n = i * 2 + s
                    for k in range(CHUNKS):
                        need = min(BLOCKS - 1, (k * ROWS + ROWS - 1 + P11) // BROWS)
                        pe.wait_ge(taps_done, n * BLOCKS + (need + 1))
                        if not isinstance(n, int) or n * CHUNKS + k >= NPS:
                            pe.wait_ge(evacuated, n * CHUNKS + (k + 1 - NPS))
                        bank = mix[k % NPS]
                        r = k * ROWS
                        flat = lambda ap: ap.rearrange("c h w -> c (h w)")
                        for j in range(11):
                            pe.matmul(bank[:, :], fold11[:, j, :], flat(mid11[:, r + j:r + j + ROWS, :]), start=(j == 0), stop=False)
                        for j in range(5):
                            pe.matmul(bank[:, :], fold5[:, j, :], flat(mid5[:, r + j:r + j + ROWS, :]), start=False, stop=False)
                        pe.matmul(bank[:, :], w3T[:, :], flat(sum33[:, r:r + ROWS, :]), start=False, stop=True).then_inc(mixed, 1)
            each(pe, ROUNDS, body)

        @block.scalar
        def _(act):
            act.wait_ge(pads_zero, 5)

            def norm(i, s):
                act.wait_ge(x_loaded[s], (i + 1) * 16)
                n = i * 2 + s
                wait(act, taps_done, (n - 1) * BLOCKS)
                wait(act, gated, (n - 1) * CHUNKS)
                act.activation(interior(s), xin[:, s, :].rearrange("c (h w) -> c h w", w=W), ACT.Identity,
                               scale=sh.rstd[:, bass.ds(n, 1)], bias=sh.shift[:, bass.ds(n, 1)]).then_inc(normed[s], 1)

            def first(i, s, blk):
                n = i * 2 + s
                wait(act, mixed, (n - 1) * CHUNKS + chunks_read(blk))
                for acc, bias, terms in tap_sums(s, blk * BROWS):
                    tap, src = terms[0]
                    more = {} if bias is None else {"bias": bias}
                    act.activation(acc, src, ACT.Identity, scale=tap, **more).then_inc(first_taps, 1)

            def evacuate(i, s, ahead=True):
                n = i * 2 + s
                if ahead:
                    act.wait_ge(normed[1 - s], i + (s + 1))
                wait(act, stored[s], i * 16)
                wait(act, stats_done, (n - 1) * CHUNKS)
                for k in range(CHUNKS):
                    act.wait_ge(mixed, n * CHUNKS + (k + 1))
                    bank = mix[k % NPS]
                    act.activation(res[:, s, k * CHUNK:(k + 1) * CHUNK], bank[:, :], ACT.Identity,
                                   bias=mix_bias[:, :]).then_inc(evacuated, 1)
                    for blk in range(BLOCKS):
                        if ahead and k + 1 == chunks_read(blk):
                            first(i + s, 1 - s, blk)

            act.wait_ge(weights_loaded, LOADS)
            norm(0, 0)
            act.wait_ge(normed[0], 1)
            for blk in range(BLOCKS):
                first(0, 0, blk)
            norm(0, 1)
            act.wait_ge(mix_bias_ready, 1)
            evacuate(0, 0)
            with act.Fori(1, ROUNDS) as i:
                norm(i, 0)
                evacuate(i - 1, 1)
                norm(i, 1)
                evacuate(i, 0)
            evacuate(ROUNDS - 1, 1, ahead=False)

        @block.vector
        def _(dve):
            dve.wait_ge(weights_loaded, LOADS)
            setup = Chain(dve, setup_chain)
            setup.link(dve.tensor_tensor(bsum[:, :], biases[:, 0:1], biases[:, 2:3], ALU.add))
            dve.tensor_tensor(bsum[:, :], bsum[:, :], biases[:, 4:5], ALU.add).then_inc(w3T_ready, 1)
            dve.wait_ge(w3T_in_psum, 1)
            dve.tensor_copy(w3T[:, :], setup_ps[:, 0:C]).then_inc(w3T_ready, 1)
            dve.wait_ge(w3T_ready, 2)
            for t, taps, n in ((fold5, w51, 5), (fold11, w1111, 11)):
                for k in range(n):
                    last = dve.tensor_scalar(t[:, k, :], w3T[:, :], taps[:, k:k + 1], None, ALU.mult)
            last.then_inc(folds_ready, 1)
            dve.wait_ge(bias_in_psum, 1)
            dve.tensor_tensor(mix_bias[:, :], setup_ps[:, C:C + 1], biases[:, 5:6], ALU.add).then_inc(mix_bias_ready, 1)

            chain = Chain(dve, tap_chain, 2 * BLOCKS * 21)

            def taps(n, s):
                for blk in range(BLOCKS):
                    r = blk * BROWS
                    ended = [0, 0, 0]
                    sums = tap_sums(s, r)
                    for j in range(1, 11):
                        for q, (acc, bias, terms) in enumerate(sums):
                            if j >= len(terms):
                                continue
                            tap, src = terms[j]
                            if j == 1:
                                dve.wait_ge(first_taps, n * (3 * BLOCKS) + (3 * blk + q + 1))
                            else:
                                dve.wait_ge(tap_chain, chain.base + ended[q])
                            last = dve.scalar_tensor_tensor(acc, src, tap, acc, op0=ALU.mult, op1=ALU.add)
                            done = j == 10
                            if done:
                                last.then_inc(taps_done, 1)
                            else:
                                ended[q] = chain.step(last)

            def stats(n, s):
                for k in range(CHUNKS):
                    dve.wait_ge(res_ready, n * CHUNKS + (k + 1))
                    dve.bn_stats(sh.stats[:, bass.ds(n, 1), k, :].rearrange("c b s -> c (b s)"),
                                 res[:, s, k * CHUNK:(k + 1) * CHUNK]).then_inc(stats_done, 1)

            def batch(i, s):
                n = i * 2 + s
                dve.wait_ge(normed[s], i + 1)
                taps(n, s)

            chain.start(0)
            batch(0, 0)
            batch(0, 1)
            stats(0, 0)
            chain.end()
            with dve.Fori(1, ROUNDS) as i:
                chain.start(i)
                batch(i, 0)
                stats(i * 2 - 1, 1)
                batch(i, 1)
                stats(i * 2, 0)
                chain.end()
            stats(B - 1, 1)

def layer3(nc, sh, x_in, w_dirs, out):
    K, PAD = 9, 4
    EDGE = 2
    HALVES, HB = 2, B // 2
    SWEEPS = [("rows", +1), ("rows", -1), ("cols", +1), ("cols", -1)]
    STEPS = [H - 1, H - 2, W - 1, W - 2]
    with ExitStack() as ctx:
        mem = Names(nc, ctx, "l3")
        state = mem.sbuf("state", [C, B, H, W])
        wraw = mem.sbuf("wraw", [C, C, K])
        taps_hi = mem.sbuf("taps_hi", [C, 4, K, C], FP32R)
        taps_lo = mem.sbuf("taps_lo", [C, 4, K, C], FP32R)
        carry_hi = mem.sbuf("carry_hi", [C, HALVES, HB, EDGE + W + EDGE], FP32R)
        carry_lo = mem.sbuf("carry_lo", [C, HALVES, HB, EDGE + W + EDGE], FP32R)
        xres = mem.sbuf("xres", [C, 2, HW // 2])
        conv = [mem.psum(f"conv{h}", [C, CHUNK]) for h in range(HALVES)]
        wt_ps = [mem.psum(f"wt{h}", [C, CHUNK]) for h in range(2)]

        x_loaded = [mem.sem(f"x_loaded{b}") for b in range(B)]
        w_loaded = mem.sem("w_loaded")
        wt_ready = mem.sem("wt_ready")
        wt_copied = mem.sem("wt_copied")
        conv_done = [mem.sem(f"conv_done{h}") for h in range(HALVES)]
        line_ready = [mem.sem(f"line_ready{h}") for h in range(HALVES)]
        hi_ready = [mem.sem(f"hi_ready{h}") for h in range(HALVES)]
        lo_ready = [mem.sem(f"lo_ready{h}") for h in range(HALVES)]
        taps_hi_ready = mem.sem("taps_hi_ready")
        edges_zero = mem.sem("edges_zero")
        waits_met = mem.sem("waits_met")
        res_loaded = [mem.sem(f"res_loaded{h}") for h in range(2)]
        out_ready = mem.sem("out_ready")
        stored = [mem.sem(f"stored{h}") for h in range(2)]

        def line(b0, nb, sweep, at, lo, n):
            if SWEEPS[sweep][0] == "rows":
                return state[:, b0:b0 + nb, bass.ds(at, 1), lo:lo + n].rearrange("c b o w -> c b (o w)")
            return state[:, b0:b0 + nb, lo:lo + n, bass.ds(at, 1)].rearrange("c b h o -> c b (h o)")

        block = ctx.enter_context(nc.Block())

        @block.sync
        def _(sp):
            for b in range(B):
                sp.dma_start(state[:, b, :, :].rearrange("c h w -> c (h w)"), x_in[b]).then_inc(x_loaded[b], 16)
                if b % 2 == 1:
                    s = b // 2
                    if s:
                        sp.wait_ge(wt_ready, 3 * s)
                    sp.dma_start(wraw[:, :, :], w_dirs[s]).then_inc(w_loaded, 16)
            for t in range(2 * B):
                b, half = t // 2, t % 2
                src = x_in[b][:, half * (HW // 2):(half + 1) * (HW // 2)]
                if t >= 2:
                    sp.wait_ge(stored[t % 2], 16 * (t // 2))
                sp.dma_start(xres[:, t % 2, :], src).then_inc(res_loaded[t % 2], 16)
                if t >= 1:
                    u = t - 1
                    sp.wait_ge(out_ready, u + 1)
                    sp.dma_start(out[u // 2][:, (u % 2) * (HW // 2):(u % 2 + 1) * (HW // 2)],
                                 xres[:, u % 2, :]).then_inc(stored[u % 2], 16)
            u = 2 * B - 1
            sp.wait_ge(out_ready, u + 1)
            sp.dma_start(out[u // 2][:, (u % 2) * (HW // 2):(u % 2 + 1) * (HW // 2)],
                         xres[:, u % 2, :]).then_inc(stored[u % 2], 16)
            sp.wait_ge(stored[0], 16 * B)
            sp.wait_ge(stored[1], 16 * B)

        @block.tensor
        def _(pe):
            n = 0
            for s in range(4):
                pe.wait_ge(w_loaded, 16 * (s + 1))
                for k0 in range(0, K, 4):
                    ks = range(k0, min(k0 + 4, K))
                    if n >= 2:
                        pe.wait_ge(wt_copied, n - 1)
                    for k in ks:
                        last = pe.transpose(wt_ps[n % 2][:, (k - k0) * C:(k - k0 + 1) * C], wraw[:, :, k], sh.ident[:, :])
                    last.then_inc(wt_ready, 1)
                    n += 1
            pe.wait_ge(wt_copied, n)
            order = [PAD] + [k for k in range(K) if k != PAD]
            done = 0
            for s, (axis, way) in enumerate(SWEEPS):
                done += axis == "cols" and way > 0
                with pe.Fori(0, STEPS[s]) as i:
                    for h in range(HALVES):
                        passes = [(taps_hi, carry_hi), (taps_lo, carry_hi), (taps_hi, carry_lo)]
                        pe.wait_ge(hi_ready[h], i + (done + 1))
                        for p, (w, carry) in enumerate(passes):
                            if p == 2:
                                pe.wait_ge(lo_ready[h], i + (done + 1))
                            for j, k in enumerate(order):
                                off = k - PAD
                                odd = off % 2
                                lo, ncol = max(0, -off - odd), W - abs(off) + odd
                                at = EDGE + lo + off
                                last = pe.matmul(conv[h][:, 0:HB * W].rearrange("c (b w) -> c b w", b=HB)[:, :, lo:lo + ncol],
                                                 w[:, s, k, :], carry[:, h, :, at:at + ncol],
                                                 start=(p == 0 and j == 0), stop=(p == 2 and j == K - 1))
                        last.then_inc(conv_done[h], 1)
                done += STEPS[s]

        @block.scalar
        def _(act):
            n = 0
            for s in range(4):
                for k0 in range(0, K, 4):
                    nk = min(4, K - k0)
                    act.wait_ge(wt_ready, n + 1)
                    act.activation(taps_hi[:, s, k0:k0 + nk, :].rearrange("c k o -> c (k o)"), wt_ps[n % 2][:, 0:nk * C],
                                   ACT.Copy).then_inc(taps_hi_ready, 1)
                    n += 1

        @block.vector
        def _(dve):
            ident_row = sh.ident[:, 0:1].to_broadcast([C, HALVES * HB * (EDGE + W + EDGE)])
            for carry in (carry_hi, carry_lo):
                dve.tensor_scalar(carry[:, :, :, :].rearrange("c h b x -> c (h b x)"), ident_row, 0.0, None, ALU.mult).then_inc(edges_zero, 1)
            dve.wait_ge(edges_zero, 2)

            def part(h, s, at, count):
                row = line(h * HB, HB, s, at, 0, W)
                dve.wait_ge(line_ready[h], count)
                dve.sem_inc(waits_met, 1)
                dve.tensor_copy(carry_hi[:, h, :, EDGE:EDGE + W], row).then_inc(hi_ready[h], 1)
                dve.wait_ge(hi_ready[h], count)
                dve.tensor_tensor(carry_lo[:, h, :, EDGE:EDGE + W], row, carry_hi[:, h, :, EDGE:EDGE + W], ALU.subtract).then_inc(lo_ready[h], 1)

            n = 0
            for s in range(4):
                for k0 in range(0, K, 4):
                    nk = min(4, K - k0)
                    dve.wait_ge(taps_hi_ready, n + 1)
                    flat = lambda ap: ap[:, s, k0:k0 + nk, :].rearrange("c k o -> c (k o)")
                    dve.tensor_tensor(flat(taps_lo), wt_ps[n % 2][:, 0:nk * C], flat(taps_hi), ALU.subtract).then_inc(wt_copied, 1)
                    n += 1
                for b in (2 * s, 2 * s + 1):
                    flat_b = state[:, b, :, :].rearrange("c h w -> c (h w)")
                    dve.wait_ge(x_loaded[b], 16)
                    last = dve.tensor_scalar(flat_b, flat_b, sh.rstd[:, b:b + 1], sh.shift[:, b:b + 1], ALU.mult, ALU.add)
                    if b % HB == HB - 1:
                        last.then_inc(line_ready[b // HB], 1)
                        part(b // HB, 0, 0, 1)
            done = 0
            for s, (axis, way) in enumerate(SWEEPS):
                if axis == "cols" and way > 0:
                    for h in range(HALVES):
                        dve.wait_ge(lo_ready[h], done + 1)
                        dve.sem_inc(line_ready[h], 1)
                        part(h, s, 0, done + 2)
                    done += 1
                with dve.Fori(0, STEPS[s]) as i:
                    at = i + 1 if way > 0 else i * -1 + (H - 2)
                    for h in range(HALVES):
                        dve.wait_ge(conv_done[h], i + (done + (1 if s < 2 else 0)))
                        row = line(h * HB, HB, s, at, 0, W)
                        dve.scalar_tensor_tensor(row, conv[h][:, 0:HB * W].rearrange("c (b w) -> c b w", b=HB), 0.0,
                                                 row, op0=ALU.max, op1=ALU.add).then_inc(line_ready[h], 1)
                        part(h, s, at, i + (done + 2))
                done += STEPS[s]
            dve.wait_ge(line_ready[0], done + 1)
            dve.wait_ge(line_ready[1], done + 1)
            for t in range(2 * B):
                b, half = t // 2, t % 2
                flat = state[:, b, :, :].rearrange("c h w -> c (h w)")[:, half * (HW // 2):(half + 1) * (HW // 2)]
                dve.wait_ge(res_loaded[t % 2], 16 * (t // 2 + 1))
                dve.tensor_tensor(xres[:, t % 2, :], xres[:, t % 2, :], flat, ALU.add).then_inc(out_ready, 1)

def program(nc, x, table, w, out):
    SEMAPHORES_OF_PART.clear()
    mids = [nc.dram_tensor(f"after_layer{k}", (B, C, HW), FP32, kind="Internal").ap() for k in range(3)]
    of_layer = lambda k: {name[len("L0_conv_"):]: ap for name, ap in w.items() if name.startswith(f"L{k}_")}
    with ExitStack() as ctx:
        sh = Shared(nc, ctx)
        masks(nc, sh)
        input_stats(nc, sh, x)
        next_part(nc)
        group_scales(nc, sh, 0)
        next_part(nc)
        layer0(nc, sh, x, table, of_layer(0), mids[0])
        next_part(nc)
        group_scales(nc, sh, 1)
        next_part(nc)
        layer1(nc, sh, mids[0], of_layer(1), mids[1])
        next_part(nc)
        group_scales(nc, sh, 2)
        next_part(nc)
        layer2(nc, sh, mids[1], of_layer(2), mids[2])
        next_part(nc)
        group_scales(nc, sh, 3)
        nc.all_engine_barrier()
        w3 = of_layer(3)
        layer3(nc, sh, mids[2], [w3["w_d"], w3["w_u"], w3["w_r"], w3["w_l"]], out)


_SHAPES = {
    "L0_conv_w_dw": (GC, 25), "L0_conv_ln_w": (GC,), "L0_conv_w_off": (3, GC),
    "L0_conv_wq": (C, C), "L0_conv_wk": (C, C), "L0_conv_wv": (C, C), "L0_conv_wo": (C, C), "L0_conv_rpe": (HEADS, RPE, RPE),
    "L1_conv_gn_weight": (C,), "L1_conv_gn_bias": (C,), "L1_conv_w1": (2 * C, C), "L1_conv_b1": (2 * C,),
    "L1_conv_w2": (C, 2 * C), "L1_conv_b2": (C,),
    "L2_conv_w0": (C, 9), "L2_conv_b0": (C, 1), "L2_conv_w0_1": (C, 5), "L2_conv_b0_1": (C, 1), "L2_conv_w0_2": (C, 5),
    "L2_conv_b0_2": (C, 1), "L2_conv_w1_1": (C, 11), "L2_conv_b1_1": (C, 1), "L2_conv_w1_2": (C, 11), "L2_conv_b1_2": (C, 1),
    "L2_conv_w3": (C, C), "L2_conv_b3": (C, 1),
    "L3_conv_w_d": (C, C, 9), "L3_conv_w_u": (C, C, 9), "L3_conv_w_r": (C, C, 9), "L3_conv_w_l": (C, C, 9),
}


def kernel(**inputs):
    import concourse.bacc as _bacc
    from concourse.bass_utils import run_bass_kernel_spmd as _run

    nc = _bacc.Bacc("TRN2", target_bir_lowering=False, num_devices=1)
    arrays = {"x": np.ascontiguousarray(inputs["x"]).reshape(B, C, HW), "coordinates": constant_table()}
    for name, shape in _SHAPES.items():
        arrays[name] = np.ascontiguousarray(inputs[name]).reshape(shape)
    aps = {name: nc.dram_tensor(f"in_{name}", a.shape, mybir.dt.from_np(a.dtype), kind="ExternalInput").ap()
           for name, a in arrays.items()}
    out = nc.dram_tensor("out", (B, C, HW), FP32, kind="ExternalOutput").ap()
    program(nc, aps["x"], aps["coordinates"], {name: aps[name] for name in _SHAPES}, out)
    r = _run(nc, [{f"in_{name}": a for name, a in arrays.items()}], core_ids=[0])
    return r.results[0]["out"].reshape(B, C, H, W)
```
